# Optimizing a Trainium2 kernel written in Bass

```python
import numpy as np
import jax
import jax.numpy as jnp

def _softmax(x, axis=-1):
    return jax.nn.softmax(x, axis=axis)

def _gelu(x):
    return jax.nn.gelu(x, approximate=True)

def _silu(x):
    return jax.nn.silu(x)

def _sigmoid(x):
    return jax.nn.sigmoid(x)

def _layernorm(x, axis=-1, eps=1e-05):
    m = jnp.mean(x, axis=axis, keepdims=True)
    v = jnp.var(x, axis=axis, keepdims=True)
    return (x - m) / jnp.sqrt(v + eps)

def _scatter_add(tgt, idx, src, axis=0):
    return tgt.at[idx].add(src)

def _segment_sum(src, seg, n):
    return jax.ops.segment_sum(src, seg, n)
kernel_name = 'mk_gps_d1_gnn_r8_ba2a71'

def setup_inputs(seed: int=0):
    np.random.seed(seed)
    _w = jnp.asarray

    def _rec_inputs():
        import jax
        import jax.numpy as jnp
        _gk = jax.random.key(seed)
        x = -0.0002117 + 1 * jax.random.normal(jax.random.fold_in(_gk, 1), (6250, 256), jnp.float32)
        _s = jax.random.randint(jax.random.fold_in(_gk, 2), (100000,), 0, 6250, jnp.int32)
        _d = jax.random.randint(jax.random.fold_in(_gk, 3), (100000,), 0, 6250, jnp.int32)
        _loop = jnp.arange(6250, dtype=jnp.int32)
        src = jnp.concatenate([_s, _d, _loop])
        dst = jnp.concatenate([_d, _s, _loop])
        _o = jnp.argsort(dst, stable=True)
        src = src[_o]
        dst = dst[_o]
        edge_weight = jax.random.uniform(jax.random.fold_in(_gk, 12), (206250,), jnp.float32, 0.0, 1)
        return (x, src, dst, edge_weight)
    x, src, dst, edge_weight = _rec_inputs()

    def _L0_gnn_setup():
        import jax, jax.numpy as jnp
        import numpy as np
        N = 12500
        E = 400000
        F_IN = 256
        F_OUT = 256

        def _spmm(edge_index, edge_weight, x, n):
            dst, src = (edge_index[0], edge_index[1])
            msg = edge_weight[:, None] * x[src]
            return jax.ops.segment_sum(msg, dst, num_segments=n)
        key = jax.random.key(seed)
        k1, k2, k3, k4, k5 = jax.random.split(key, 5)
        feature = jax.random.normal(k1, (N, F_IN), dtype=jnp.float32)
        edge_index = jax.random.randint(k2, (2, E), 0, N)
        edge_weight = jax.random.uniform(k3, (E,), dtype=jnp.float32)
        stdv = 1.0 / np.sqrt(F_OUT)
        weight = jax.random.uniform(k4, (F_IN, F_OUT), dtype=jnp.float32, minval=-stdv, maxval=stdv)
        bias = jax.random.uniform(k5, (F_OUT,), dtype=jnp.float32, minval=-stdv, maxval=stdv)
        return {'feature': feature, 'edge_weight': edge_weight, 'weight': weight, 'bias': bias, 'edge_index': edge_index, 'mode': 2}
    _L0_gnn_all = _L0_gnn_setup()
    _L0_gnn_in = {k: v for k, v in _L0_gnn_all.items() if k in ('weight', 'bias')}
    del _L0_gnn_all

    def _L0_mix_setup():
        import jax, jax.numpy as jnp
        import numpy as np
        NHEAD = 8
        ATT_EPS = 1e-06
        LN_EPS = 1e-05

        def _layernorm(x, g, b):
            mu = jnp.mean(x, axis=-1, keepdims=True)
            var = jnp.mean(jnp.square(x - mu), axis=-1, keepdims=True)
            return (x - mu) * jax.lax.rsqrt(var + LN_EPS) * g + b
        key = jax.random.key(seed)
        ks = jax.random.split(key, 7)
        N, L, C = (4, 2048, 256)
        s = 1.0 / np.sqrt(C)
        return {'x': jax.random.normal(ks[0], (N, L, C), jnp.float32), 'Wq': jax.random.normal(ks[1], (C, C), jnp.float32) * s, 'Wk': jax.random.normal(ks[2], (C, C), jnp.float32) * s, 'Wv': jax.random.normal(ks[3], (C, C), jnp.float32) * s, 'Wm': jax.random.normal(ks[4], (C, C), jnp.float32) * s, 'W1': jax.random.normal(ks[5], (2 * C, 2 * C), jnp.float32) * (1.0 / np.sqrt(2 * C)), 'W2': jax.random.normal(ks[6], (2 * C, C), jnp.float32) * (1.0 / np.sqrt(2 * C)), 'g1': jnp.ones((C,), jnp.float32), 'b1': jnp.zeros((C,), jnp.float32), 'g2': jnp.ones((C,), jnp.float32), 'b2': jnp.zeros((C,), jnp.float32)}
    _L0_mix_all = _L0_mix_setup()
    _L0_mix_in = {k: v for k, v in _L0_mix_all.items() if k in ('Wq', 'Wk', 'Wv', 'Wm', 'W1', 'W2', 'g1', 'b1', 'g2', 'b2')}
    del _L0_mix_all

    def _L0_ffn_setup():
        import jax, jax.numpy as jnp
        import numpy as np
        TOP_K = 2
        LN_EPS = 1e-05
        key = jax.random.key(seed)
        ks = jax.random.split(key, 8)
        B, S, D, E, H = (16, 1024, 256, 8, 1024)
        x = jax.random.normal(ks[0], (B, S, D), dtype=jnp.float32)
        Wr = jax.random.normal(ks[1], (D, E), dtype=jnp.float32) * 0.1
        br = jnp.zeros((E,), dtype=jnp.float32)
        ln_g = jnp.ones((E, D), dtype=jnp.float32)
        ln_b = jnp.zeros((E, D), dtype=jnp.float32)
        W1 = jax.random.normal(ks[2], (E, D, H), dtype=jnp.float32) * (1.0 / np.sqrt(D))
        b1 = jnp.zeros((E, H), dtype=jnp.float32)
        W2 = jax.random.normal(ks[3], (E, H, D), dtype=jnp.float32) * (1.0 / np.sqrt(H))
        b2 = jnp.zeros((E, D), dtype=jnp.float32)
        return {'x': x, 'Wr': Wr, 'br': br, 'ln_g': ln_g, 'ln_b': ln_b, 'W1': W1, 'b1': b1, 'W2': W2, 'b2': b2}
    _L0_ffn_all = _L0_ffn_setup()
    _L0_ffn_in = {k: v for k, v in _L0_ffn_all.items() if k in ('Wr', 'br', 'ln_g', 'ln_b', 'W1', 'b1', 'W2', 'b2')}
    del _L0_ffn_all
    return {'x': x, 'src': src, 'dst': dst, 'edge_weight': edge_weight, 'L0_gnn_weight': _L0_gnn_in['weight'], 'L0_gnn_bias': _L0_gnn_in['bias'], 'L0_mix_Wq': _L0_mix_in['Wq'], 'L0_mix_Wk': _L0_mix_in['Wk'], 'L0_mix_Wv': _L0_mix_in['Wv'], 'L0_mix_Wm': _L0_mix_in['Wm'], 'L0_mix_W1': _L0_mix_in['W1'], 'L0_mix_W2': _L0_mix_in['W2'], 'L0_mix_g1': _L0_mix_in['g1'], 'L0_mix_b1': _L0_mix_in['b1'], 'L0_mix_g2': _L0_mix_in['g2'], 'L0_mix_b2': _L0_mix_in['b2'], 'L0_ffn_Wr': _L0_ffn_in['Wr'], 'L0_ffn_br': _L0_ffn_in['br'], 'L0_ffn_ln_g': _L0_ffn_in['ln_g'], 'L0_ffn_ln_b': _L0_ffn_in['ln_b'], 'L0_ffn_W1': _L0_ffn_in['W1'], 'L0_ffn_b1': _L0_ffn_in['b1'], 'L0_ffn_W2': _L0_ffn_in['W2'], 'L0_ffn_b2': _L0_ffn_in['b2']}

def reference(x, src, dst, edge_weight, L0_gnn_weight, L0_gnn_bias, L0_mix_Wq, L0_mix_Wk, L0_mix_Wv, L0_mix_Wm, L0_mix_W1, L0_mix_W2, L0_mix_g1, L0_mix_b1, L0_mix_g2, L0_mix_b2, L0_ffn_Wr, L0_ffn_br, L0_ffn_ln_g, L0_ffn_ln_b, L0_ffn_W1, L0_ffn_b1, L0_ffn_W2, L0_ffn_b2):
    import jax
    import jax.numpy as jnp

    def _L0_gnn_ref(feature, edge_weight, weight, bias, edge_index, mode):
        import jax, jax.numpy as jnp
        import numpy as np
        N = 12500
        E = 400000
        F_IN = 256
        F_OUT = 256

        def _spmm(edge_index, edge_weight, x, n):
            dst, src = (edge_index[0], edge_index[1])
            msg = edge_weight[:, None] * x[src]
            return jax.ops.segment_sum(msg, dst, num_segments=n)
        if mode in (1, 2):
            feature = feature - jnp.mean(feature, axis=0, keepdims=True)
        if mode == 2:
            std = jnp.std(feature, axis=0, ddof=1) + 0.0001
            feature = feature / std
        support = _spmm(edge_index, edge_weight, feature, feature.shape[0])
        output = support @ weight
        return output + bias

    def _L0_mix_ref(x, Wq, Wk, Wv, Wm, W1, W2, g1, b1, g2, b2):
        import jax, jax.numpy as jnp
        import numpy as np
        NHEAD = 8
        ATT_EPS = 1e-06
        LN_EPS = 1e-05

        def _layernorm(x, g, b):
            mu = jnp.mean(x, axis=-1, keepdims=True)
            var = jnp.mean(jnp.square(x - mu), axis=-1, keepdims=True)
            return (x - mu) * jax.lax.rsqrt(var + LN_EPS) * g + b
        N, L, C = x.shape
        H = NHEAD
        D = C // H
        q = (x @ Wq).reshape(N, L, H, D)
        k = (x @ Wk).reshape(N, L, H, D)
        v = (x @ Wv).reshape(N, L, H, D)
        Q = jax.nn.elu(q) + 1.0
        K = jax.nn.elu(k) + 1.0
        v = v / L
        KV = jnp.einsum('nshd,nshv->nhdv', K, v)
        Z = 1.0 / (jnp.einsum('nlhd,nhd->nlh', Q, K.sum(axis=1)) + ATT_EPS)
        msg = jnp.einsum('nlhd,nhdv,nlh->nlhv', Q, KV, Z) * L
        msg = msg.reshape(N, L, C) @ Wm
        msg = _layernorm(msg, g1, b1)
        h = jnp.concatenate([x, msg], axis=-1) @ W1
        h = jax.nn.relu(h) @ W2
        msg = _layernorm(h, g2, b2)
        return x + msg

    def _L0_ffn_ref(x, Wr, br, ln_g, ln_b, W1, b1, W2, b2):
        import jax, jax.numpy as jnp
        import numpy as np
        TOP_K = 2
        LN_EPS = 1e-05
        B, S, D = x.shape
        N = B * S
        xt = x.reshape(N, D)
        logits = xt @ Wr + br
        probs = jax.nn.softmax(logits, axis=-1)
        top_p, top_idx = jax.lax.top_k(probs, TOP_K)
        weights = top_p / top_p.sum(axis=-1, keepdims=True)
        mu = xt.mean(axis=-1, keepdims=True)
        var = ((xt - mu) ** 2).mean(axis=-1, keepdims=True)
        xn = (xt - mu) * jax.lax.rsqrt(var + LN_EPS)
        xe = xn[None, :, :] * ln_g[:, None, :] + ln_b[:, None, :]
        h = jax.nn.gelu(jnp.einsum('end,edh->enh', xe, W1) + b1[:, None, :], approximate=False)
        y = jnp.einsum('enh,ehd->end', h, W2) + b2[:, None, :]
        y_tok = jnp.transpose(y, (1, 0, 2))
        sel = jnp.take_along_axis(y_tok, top_idx[:, :, None], axis=1)
        out = (weights[:, :, None] * sel).sum(axis=1)
        return out.reshape(B, S, D)
    edge_index = jnp.stack([src, dst])
    xn = _layernorm(x, axis=-1)
    x = x + _L0_gnn_ref(xn, edge_weight, L0_gnn_weight, L0_gnn_bias, edge_index, 2) + _L0_mix_ref(xn[None], L0_mix_Wq, L0_mix_Wk, L0_mix_Wv, L0_mix_Wm, L0_mix_W1, L0_mix_W2, L0_mix_g1, L0_mix_b1, L0_mix_g2, L0_mix_b2)[0]
    x = x + _L0_ffn_ref(_layernorm(x, axis=-1)[None], L0_ffn_Wr, L0_ffn_br, L0_ffn_ln_g, L0_ffn_ln_b, L0_ffn_W1, L0_ffn_b1, L0_ffn_W2, L0_ffn_b2)[0]
    return x

_drawn_inputs = setup_inputs


def setup_inputs(seed=0):
    import zlib

    import numpy as np

    out = dict(_drawn_inputs(seed))
    spreads = {'L0_mix_g1': (1.0, 0.2),
     'L0_mix_b1': (0.0, 0.277),
     'L0_mix_g2': (1.0, 0.2),
     'L0_mix_b2': (0.0, 0.1),
     'L0_ffn_br': (0.0, 0.1),
     'L0_ffn_ln_g': (1.0, 0.2),
     'L0_ffn_ln_b': (0.0, 0.451),
     'L0_ffn_b1': (0.0, 0.44),
     'L0_ffn_b2': (0.0, 0.306)}
    factors = {'L0_gnn_bias': 3.712}
    for name, (base, spread) in spreads.items():
        noise = np.random.default_rng([zlib.crc32(name.encode()), seed]).standard_normal(out[name].shape)
        drawn = base * np.exp(spread * noise) if base else spread * noise
        out[name] = jnp.asarray(drawn.astype(out[name].dtype))
    for name, factor in factors.items():
        out[name] = (out[name] * factor).astype(out[name].dtype)
    return out
```

```python
from contextlib import ExitStack

import concourse.bass as bass
from concourse import mybir

ALU = mybir.AluOpType
ACT = mybir.ActivationFunctionType
F32 = mybir.dt.float32
BF16 = mybir.dt.bfloat16
I32 = mybir.dt.int32
U32 = mybir.dt.uint32
AX_X = mybir.AxisListType.X
EPS = 1e-5
ATT_EPS = 1e-6
STD_EPS = 1e-4


class Steps:

    LEAD = 2

    def __init__(self, sem, names):
        self.sem, self.names, self.k = sem, names.split(), 0

    def first(self, engine):
        engine.sem_inc(self.sem, self.LEAD * len(self.names))

    def __call__(self, name):
        assert self.names[self.k % len(self.names)] == name, (self.names[self.k % len(self.names)], name)
        self.k += 1
        return self.sem, 1

    def done(self, turn, name):
        n = len(self.names)
        return self.sem, (turn + self.LEAD) * n + self.names.index(name) + 1


def gps_layer(nc, x, src, dst, edge_weight, gnn_W, gnn_b, Wq, Wk, Wv, Wm, W1, W2, g1, b1, g2, b2,
              Wr, br, ln_g, ln_b, eW1, eb1, eW2, eb2, out):
    N, F = x.shape
    E = src.shape[0]
    P = 128
    T = -(-N // P)
    TAIL = N - (T - 1) * P
    FC = F // P
    HID = W1.shape[1]
    HC = HID // P
    HEADS = 8
    HD = F // HEADS
    HPC = P // HD
    NE, _, EH = eW1.shape
    EHC = EH // P
    BLK = 256
    BM = BLK // P
    MAXBLK = 2 * N // BLK + NE
    REG = (-(-N // BLK) + 1) * BLK
    CH = -(-E // P)
    CB = -(-CH // P)
    U = 7
    NG = 5
    NACC = 4
    AROWS = -(-(N + P) // (2 * P)) * 2 * P
    EPAD = CH * P + U * P
    BIG = 2048
    PADDST = T * P - 1
    assert CH < BIG and FC == 2 and TAIL < P

    sums = [nc.dram_tensor(f"sums{k}", [AROWS, F], F32).ap() for k in range(NACC)]
    src_d = nc.dram_tensor("src_padded", [EPAD], I32).ap()
    dst_d = nc.dram_tensor("dst_padded", [EPAD], I32).ap()
    w_d = nc.dram_tensor("w_padded", [EPAD], F32).ap()
    erows = nc.dram_tensor("expert_rows", [NE * REG, F], F32).ap()
    eouts = nc.dram_tensor("expert_outs", [(MAXBLK + 1) * BLK, F], F32).ap()

    with ExitStack() as ctx:
        def sb(name, shape, dt=F32):
            return ctx.enter_context(nc.sbuf_tensor("sb_" + name, shape, dt))

        def ps(name, shape, dt=F32):
            return ctx.enter_context(nc.psum_tensor("ps_" + name, shape, dt))

        def sem(name):
            return ctx.enter_context(nc.semaphore(name))

        x1 = sb("x1", [P, T, F])
        ident = sb("ident", [P, P])
        ones = sb("ones", [P, P])
        tri = sb("tri", [P, P])
        bdmask = sb("bdmask", [P, HPC, HD])
        hmask = sb("hmask", [P, HPC])
        valid = sb("valid", [P, T])
        idrow = sb("idrow", [P, P])
        down8 = sb("down8", [P, NE])
        carry = sb("carry", [P, NE])
        ebase = sb("ebase", [P, NE])
        cidx = sb("cidx", [P, CB])
        cinv = sb("cinv", [P, CB])
        dummy = sb("dummy", [P, U])
        trilow = sb("trilow", [P, P])
        tlo = sb("tlo", [P, T])
        thi = sb("thi", [P, T])
        bidx = sb("bidx", [1, MAXBLK])
        PADP = 2
        assert (EPAD - E) % PADP == 0
        padi = sb("padi", [PADP, (EPAD - E) // PADP], I32)
        padz = sb("padz", [PADP, (EPAD - E) // PADP], I32)
        zrows = sb("zrows", [P, BM * F])
        wq = sb("wq", [P, FC, F])
        wkv = sb("wkv", [P, FC, 2 * F])
        wm = sb("wm", [P, FC, F])
        w1 = sb("w1", [P, 2 * FC, HID])
        w2 = sb("w2", [P, HC, F])
        wg = sb("wg", [P, FC, F])
        wgs = sb("wgs", [P, FC, F])
        wr = sb("wr", [P, FC, NE])
        PR = NE * EHC + 4 * FC + 2 * NE * FC - 2 * FC
        rows_p = sb("rows_p", [PR, P])
        colp = sb("colp", [P, PR])
        R_B1, R_G, R_B, R_G1, R_BB1 = 0, NE * EHC, NE * EHC + NE * FC, NE * EHC + 2 * NE * FC, NE * EHC + 2 * NE * FC + FC
        g2_bc = sb("g2_bc", [P, F])
        bias_bc = sb("bias_bc", [P, F])
        gb_bc = sb("gb_bc", [P, F])
        br_bc = sb("br_bc", [P, NE])
        xn = sb("xn", [P, T, F])
        bst = sb("bst", [P, T, 6])
        rmean = sb("rmean", [P, T])
        rvar = sb("rvar", [P, T])
        rtmp = sb("rtmp", [P, T])
        rrstd = sb("rrstd", [P, T])
        xs = sb("xs", [P, 2, F])
        xnT = sb("xnT", [P, 2, FC, P])
        kmin = sb("kmin", [P, 2, F])
        kexp = sb("kexp", [P, 2, F])
        kelu = sb("kelu", [P, 2, F])
        vaug = sb("vaug", [P, 2, FC, P + 1])
        cst = sb("cst", [P, FC, T, 6])
        cmv = sb("cmv", [P, FC, 2])
        cstd = sb("cstd", [P, FC])
        dmean = sb("dmean", [P, FC, P])
        mean_bc = sb("mean_bc", [P, F])
        kvbd = sb("kvbd", [P, FC, P + HPC])
        ring = sb("ring", [P, U * (F + P)])
        assert CB * P <= U * (F + P) and T * CB <= U * P
        dstc = ring[:, 0:CB * P].bitcast(I32).rearrange("p (b e) -> p b e", b=CB)
        msgs = ring[:, 0:U * F].rearrange("p (k f) -> p k f", k=U)
        coef = ring[:, U * F:U * (F + P)].rearrange("p (k q) -> p k q", k=U)
        cmax = sb("cmax", [P, CB])
        cmin = sb("cmin", [P, CB])
        vmax = sb("vmax", [P, 2 * T])
        vred = sb("vred", [2 * T, 1])
        brow = sb("brow", [1, 2 * T])
        bnd = sb("bnd", [1, 2, T], I32)
        bndf = sb("bndf", [1, 2, T])
        src_e = sb("src_e", [P, U], I32)
        dst_e = sb("dst_e", [P, U], I32)
        w_e = sb("w_e", [P, U])
        src_row = sb("src_row", [P, P * U], I32)
        srcf = sb("srcf", [P, U])
        dstf = sb("dstf", [P, U])
        reads = sb("reads", [P, U, P])
        same = sb("same", [P, U, P])
        indA, indB = (b[:].rearrange("p k e -> p (k e)")[:, 0:T * CB].rearrange("p (t b) -> p t b", t=T)
                      for b in (reads, same))
        before = sb("before", [P, U])
        junk = sb("junk", [P, U, P], BF16)
        away = sb("away", [P, U])
        idxf = sb("idxf", [P, U])
        idx = sb("idx", [P, U], I32)
        qmin = sb("qmin", [P, FC, P])
        qexp = sb("qexp", [P, FC, P])
        qelu = sb("qelu", [P, FC, P])
        rden = sb("rden", [P, FC, HPC])
        msg = sb("msg", [P, F])
        msgT = sb("msgT", [P, FC, P])
        lnst = sb("lnst", [P, 6])
        lnmv = sb("lnmv", [P, 2])
        lnve = sb("lnve", [P, 1])
        lnln = sb("lnln", [P, 1])
        lny = sb("lny", [P, 1])
        lna = sb("lna", [P, 1])
        lnr = sb("lnr", [P, 1])
        mrow = sb("mrow", [P, F])
        mT = sb("mT", [P, FC, P])
        hT = sb("hT", [P, HC, P])
        assert 2 * NACC * F <= U * (F + P)
        parts = ring[:, 0:2 * NACC * F].rearrange("p (s k f) -> p s k f", s=2, k=NACC)
        aggT = sb("aggT", [P, 2, FC, P])
        xn2 = sb("xn2", [P, 2, F])
        TE = T * NE
        logits = sb("logits", [P, T, NE])
        hot = sb("hot", [P, 2, T, NE])
        hots = sb("hots", [P, T, NE])
        work = sb("work", [P, 2, T, NE])
        best = sb("best", [P, 2, T])
        which = sb("which", [P, T])
        wts = sb("wts", [P, T, 2])
        slotf = sb("slotf", [P, T, 2])
        slotc = sb("slotc", [P, T, 2])
        slot_now = sb("slot_now", [P, 2, 2], I32)
        lastcnt = sb("lastcnt", [P, NE])
        cnt = sb("cnt", [P, NE])
        cnti = sb("cnti", [P, NE], I32)
        nblk = sb("nblk", [P, NE])
        cum = sb("cum", [P, NE])
        delta = sb("delta", [P, NE])
        one8 = sb("one8", [P, NE])
        le, lenb = (b[0:1].rearrange("p s f -> p (s f)")[:, 0:MAXBLK * NE].rearrange("p (m e) -> p m e", e=NE)
                    for b in (kmin, kexp))
        be = sb("be", [1, MAXBLK])
        bprev = sb("bprev", [1, MAXBLK])
        bstart = sb("bstart", [1, MAXBLK])
        btab = sb("btab", [1, 2, MAXBLK], I32)
        ztab = sb("ztab", [1, NE + 1], I32)
        pA = ps("A", [P, 512])
        pT = ps("T", [P, 512])
        pQ = ps("Q", [P, 512])
        pM = ps("M", [P, 512])
        pH = ps("H", [P, 512])
        pY = ps("Y", [P, 512])
        pG = ps("G", [P, 512])
        pR = ps("R", [P, 512])

        pC, pX = (pA, pY), (pG, pR)
        consts_made = sem("consts_made")
        spacer = sem("spacer")
        pads_made = sem("pads_made")
        x_zeroed = sem("x_zeroed")
        x_loaded = sem("x_loaded")
        kv_weights = sem("kv_weights")
        weights = sem("weights")
        edges_padded = sem("edges_padded")
        chunks_zeroed = sem("chunks_zeroed")
        chunks_loaded = sem("chunks_loaded")
        prefix_kept = sem("prefix_kept")
        zero_made = sem("zero_made")
        sums_zeroed = sem("sums_zeroed")
        dve1 = Steps(sem("dve_norm"), "stats")
        dve2 = Steps(sem("dve_rstd"), "msum mean dif m2 dif2 dif4 var ve a nr y rstd")
        act2 = Steps(sem("act_rstd"), "ln exp")
        PK = Steps(sem("pe_kv"), "trans kv")
        PKA = Steps(sem("pe_kvacc"), "kvacc")
        DK = Steps(sem("dve_kv"), "norm cstat0 cstat1 kmin kelu")
        GK = Steps(sem("pool_kv"), "keep res")
        AK = Steps(sem("act_kv"), "xnT kexp vcopy")
        dve3 = Steps(sem("dve_cols"), "aggr0 aggr1 std inv wgs0 wgs1 dm0 dm1 meanbc "
                                      "kv0 kv1 ks0 ks1 gb")
        cen_made = sem("rows_centred")
        act3 = Steps(sem("act_cols"), "sqrt")
        pe3 = Steps(sem("pe_cols"), "params mean")
        ccopy = sem("params_copied")
        dveb = Steps(sem("dve_span"), "cmax cmin indA indB ind vhi vmaxhi vlo vmaxlo vred row "
                                      "hi1 lo1 hi2 lo2 n1 n2 mul elo ielo in shr min")
        peb = Steps(sem("pe_span"), "t1 t2")
        edges_loaded = sem("edges_loaded")
        floats_made = sem("floats_made")
        onehots_made = sem("onehots_made")
        counted = sem("counted")
        idx_float = sem("idx_float")
        idx_ready = sem("idx_ready")
        coef_done = sem("coef_done")
        coef_copied = sem("coef_copied")
        NPAIR = (U + 1) // 2
        msg_done = sem("msg_done")
        msg_copied = sem("msg_copied")
        scattered = [sem(f"scattered{k}") for k in range(U)]
        LN = "st ag ve a nr r ap"
        ln = lambda p: " ".join(p + s for s in LN.split())
        PM = Steps(sem("pe_mixer"), "xT q num msgT mm mT hid h2")
        DM = Steps(sem("dve_mixer"), "idrow xs qmin qelu eps rden msg " + ln("m") + " " + ln("h") + " g2 b2 res")
        AM = Steps(sem("act_mixer"), "xT qexp msgT mln mexp mT0 mT1 relu hln hexp")
        parts_loaded = [sem("parts_loaded0"), sem("parts_loaded1")]
        GG = Steps(sem("pool_gnn"), "add1 add2 add3")
        PG = Steps(sem("pe_gnn"), "aggT gnn")
        AG = Steps(sem("act_gnn"), "aggT")
        DG = Steps(sem("dve_gnn"), "res stats")
        RS = "msum mean dif m2 dif2 dif4 var ve a nr y rstd"
        dveo, acto = Steps(sem("dve_rstd_o"), RS), Steps(sem("act_rstd_o"), "ln exp")
        dvei, acti = Steps(sem("dve_rstd_i"), RS), Steps(sem("act_rstd_i"), "ln exp")
        DR = Steps(sem("dve_router"), "xt stats")
        GR = Steps(sem("pool_router"), "keep")
        PR_ = Steps(sem("pe_router"), "xT log")
        AR = Steps(sem("act_router"), "xT log")
        dver = Steps(sem("dve_top2"), "br b0 e0 r0 w0 h0 p0 l1 b1 e1 r1 w1 h1 dif den wa wb v0 v1 sum tot "
                     "s1 s2 s4 s8 s16 s32 sub rank base p0x s0x p1x s1x last")
        actr = Steps(sem("act_top2"), "exp")
        per = Steps(sem("pe_rank"), "rank tot")
        DD = Steps(sem("dve_dispatch"), "xn2 slot")
        dispatched = [sem("dispatched0"), sem("dispatched1")]
        dve5 = Steps(sem("dve_blocks"), "cnt c255 ci sh nb cum le lenb be bprev st1 st2 itab ibe izt inb")
        dve6 = Steps(sem("dve_slots"), "excl rows delta hot0 hot1 shift slot")
        all_scattered = sem("all_scattered")
        zero_rows = sem("zero_rows")
        zero_outs = sem("zero_outs")
        outs_zeroed = sem("outs_zeroed")
        ew1_loaded = sem("ew1_loaded")
        ew2_loaded = sem("ew2_loaded")
        eb2_loaded = sem("eb2_loaded")
        xb_loaded = sem("xb_loaded")
        PE_ = Steps(sem("pe_experts"), "t0 t1 " + " ".join(f"h{j}" for j in range(EHC)) + " y0 y1")
        DE = Steps(sem("dve_experts"), "x0 x1 y0 y1")
        AE = Steps(sem("act_experts"), " ".join(f"g{j}" for j in range(EHC)))
        out_rows = sem("out_rows")
        DC = Steps(sem("dve_combine"), "idx a b")
        got = [[sem(f"got{s}{j}") for j in range(2)] for s in range(2)]
        stored = [sem("stored0"), sem("stored1")]

        xn_flat, used = xn[:].rearrange("p t f -> p (t f)"), [0]

        def over_xn(n):
            used[0] += n
            assert used[0] <= T * F
            return xn_flat[:, used[0] - n:used[0]]

        ew1 = over_xn(FC * EH).rearrange("p (c h) -> p c h", c=FC)
        ew2 = over_xn(EHC * F).rearrange("p (j f) -> p j f", j=EHC)
        ehT = over_xn(EHC * BLK).rearrange("p (j q) -> p j q", j=EHC)
        xeT = over_xn(FC * BLK).rearrange("p (c q) -> p c q", c=FC)
        xb = over_xn(BM * F).rearrange("p (m f) -> p m f", m=BM)
        yb = over_xn(BM * F).rearrange("p (m f) -> p m f", m=BM)
        eb2_bc = over_xn(F)
        yg = parts
        idx_c = sb("idx_c", [P, 2, 2], I32)
        ob = over_xn(2 * F).rearrange("p (s f) -> p s f", s=2)

        def apart(engine):
            engine.sem_inc(spacer, 1)

        def tile(buf, t):
            return buf[:, t, :] if isinstance(t, int) else buf[:, bass.ds(t, 1), :]

        def col(buf, t):
            return buf[:, t:t + 1] if isinstance(t, int) else buf[:, bass.ds(t, 1)]

        block = ctx.enter_context(nc.Block())
        XCH = 12
        nxc = (T - 1) // XCH
        assert nxc * XCH == T - 1

        @block.sync
        def _(sp):
            xr = x[0:(T - 1) * P, :].rearrange("(t p) f -> p t f", p=P)
            for k in range(nxc):
                sp.dma_start(x1[:, k * XCH:(k + 1) * XCH, :], xr[:, k * XCH:(k + 1) * XCH, :]).then_inc(x_loaded, 16)
            sp.wait_ge(x_zeroed, 1)
            sp.dma_start(x1[0:TAIL, T - 1, :], x[(T - 1) * P:N, :]).then_inc(x_loaded, 16)
            sp.dma_start(wkv[:, :, 0:F], Wk.rearrange("(c p) n -> p c n", p=P)).then_inc(kv_weights, 16)
            sp.dma_start(wkv[:, :, F:2 * F], Wv.rearrange("(c p) n -> p c n", p=P)).then_inc(kv_weights, 16)
            g = 15
            for d, s in ((src_d, src), (dst_d, dst), (w_d, edge_weight)):
                sp.dma_start(d[0:E].rearrange("(g e) -> g e", g=g), s.rearrange("(g e) -> g e", g=g)).then_inc(edges_padded, 16)
            sp.wait_ge(pads_made, 2)
            for d, b in ((src_d, padz[:]), (dst_d, padi[:]), (w_d, padz[:].bitcast(F32))):
                sp.dma_start(d[E:EPAD].rearrange("(p e) -> p e", p=PADP), b).then_inc(edges_padded, 16)
            for b, w in ((wq, Wq), (wm, Wm), (w1, W1), (w2, W2), (wg, gnn_W), (wr, Wr)):
                sp.dma_start(b[:], w.rearrange("(c p) n -> p c n", p=P)).then_inc(weights, 16)
            sp.dma_start(rows_p[R_B1:R_G, :], eb1.rearrange("e (j p) -> (e j) p", p=P)).then_inc(weights, 16)
            sp.dma_start(rows_p[R_G:R_B, :], ln_g.rearrange("e (j p) -> (e j) p", p=P)).then_inc(weights, 16)
            sp.dma_start(rows_p[R_B:R_G1, :], ln_b.rearrange("e (j p) -> (e j) p", p=P)).then_inc(weights, 16)
            sp.dma_start(rows_p[R_G1:R_BB1, :], g1.rearrange("(j p) -> j p", p=P)).then_inc(weights, 16)
            sp.dma_start(rows_p[R_BB1:PR, :], b1.rearrange("(j p) -> j p", p=P)).then_inc(weights, 16)
            for b, v in ((g2_bc, g2), (bias_bc, b2), (gb_bc, gnn_b), (br_bc, br)):
                sp.dma_start(b[:], v.partition_broadcast(P)).then_inc(weights, 16)
            sp.wait_ge(edges_padded, 6 * 16)
            sp.wait_ge(chunks_zeroed, 1)
            full = CH // P
            sp.dma_start(dstc[:, 0:full, :], dst_d[0:full * P * P].rearrange("(b p e) -> p b e", p=P, e=P)).then_inc(chunks_loaded, 16)
            sp.dma_start(dstc[0:CH - full * P, full, :],
                         dst_d[full * P * P:CH * P].rearrange("(p e) -> p e", e=P)).then_inc(chunks_loaded, 16)
            sp.wait_ge(zero_made, 1)
            for a in sums:
                n2 = AROWS // (2 * P)
                sp.dma_start(a.rearrange("(p j m) f -> p j (m f)", p=P, m=2),
                             zrows[:].unsqueeze(1).to_broadcast([P, n2, 2 * F])).then_inc(sums_zeroed, 16)
            sp.wait_ge(*dveb.done(0, "min"))
            groups = sp.alloc_register("sp_groups")
            first_edge = sp.alloc_register("sp_first_edge")
            sp.reg_mov(groups, 0)
            with sp.Fori(0, T) as t:
                e0 = sp.value_load(bnd[0:1, 0, bass.ds(t, 1)], min_val=0, max_val=CH * P)
                n = sp.value_load(bnd[0:1, 1, bass.ds(t, 1)], min_val=NG, max_val=-(-CH // U))
                sp.reg_mov(first_edge, e0)
                g0 = sp.snap(groups)
                with sp.Fori(0, n) as i:
                    eg = sp.snap(first_edge, min_val=0, max_val=EPAD - U * P)
                    sp.wait_ge(counted, (g0 + i) * (U + 1) + 1)
                    apart(sp)
                    sp.wait_ge(onehots_made, (g0 + i) * (2 * U) + 1)
                    apart(sp)
                    at = bass.ds(eg, U * P)
                    for b, d in ((src_e, src_d), (dst_e, dst_d), (w_e, w_d)):
                        sp.dma_start(b[:], d[at].rearrange("(p k) -> p k", k=U)).then_inc(edges_loaded, 16)
                    sp.dma_start(src_row[:], src_d[at].partition_broadcast(P)).then_inc(edges_loaded, 16)
                    sp.reg_add(first_edge, first_edge, U * P)
                sp.reg_add(groups, groups, n)
            sp.wait_ge(all_scattered, 1)
            with sp.Fori(0, T // 2) as i:
                for s in range(2):
                    sp.wait_ge(*PG.done(2 * i + s - 2, "aggT"))
                    for k in range(NACC):
                        sp.dma_start(parts[:, s, k, :], sums[k][bass.ds((2 * i + s) * P, P), :]).then_inc(parts_loaded[s], 16)
            sp.wait_ge(*PG.done(T - 3, "aggT"))
            for k in range(NACC):
                sp.dma_start(parts[:, 0, k, :], sums[k][(T - 1) * P:T * P, :]).then_inc(parts_loaded[0], 16)
            sp.wait_ge(*dve5.done(0, "inb"))
            sp.wait_ge(dispatched[0], 2 * 16 * (T // 2 + 1))
            sp.wait_ge(dispatched[1], 2 * 16 * (T // 2))
            for e in range(NE):
                z0 = sp.value_load(ztab[0:1, e:e + 1], min_val=0, max_val=NE * REG - BLK)
                sp.dma_start(erows[bass.ds(z0, BLK), :].rearrange("(p m) f -> p (m f)", m=BM), zrows[:]).then_inc(zero_rows, 16)
            sp.wait_ge(zero_rows, NE * 16)
            nb = sp.value_load(ztab[0:1, NE:NE + 1], min_val=1, max_val=MAXBLK)
            with sp.Fori(0, nb) as b:
                r0 = sp.value_load(btab[0:1, 0, bass.ds(b, 1)], min_val=0, max_val=NE * REG - BLK)
                e = sp.value_load(btab[0:1, 1, bass.ds(b, 1)], min_val=0, max_val=NE - 1)
                sp.wait_ge(*PE_.done(b - 1, "t1"))
                sp.dma_start(xb[:], erows[bass.ds(r0, BLK), :].rearrange("(m p) f -> p m f", p=P)).then_inc(xb_loaded, 16)
                sp.wait_ge(*PE_.done(b - 1, f"h{EHC - 1}"))
                sp.dma_start(ew1[:], eW1[bass.ds(e, 1)].rearrange("e (c p) h -> p (e c) h", p=P)).then_inc(ew1_loaded, 16)
                sp.wait_ge(*DE.done(b - 1, "y1"))
                sp.dma_start(ew2[:], eW2[bass.ds(e, 1)].rearrange("e (j p) f -> p (e j) f", p=P)).then_inc(ew2_loaded, 16)
                sp.dma_start(eb2_bc[:], eb2[bass.ds(e, 1), :].rearrange("e f -> (e f)").partition_broadcast(P)).then_inc(eb2_loaded, 16)
            zeroed = sp.alloc_register("sp_zeroed")
            sp.reg_mov(zeroed, 0)
            with sp.Fori(nb, MAXBLK + 1) as b:
                sp.reg_add(zeroed, zeroed, 16)
                sp.dma_start(eouts[bass.ds(b * BLK, BLK), :].rearrange("(p m) f -> p (m f)", m=BM), zrows[:]).then_inc(zero_outs, 16)
            sp.wait_ge(zero_outs, sp.snap(zeroed, min_val=16, max_val=16 * (MAXBLK + 1)))
            sp.sem_inc(outs_zeroed, 1)
            with sp.Fori(0, T // 2) as i:
                for s in range(2):
                    sp.wait_ge(*DC.done(2 * i + s, "b"))
                    sp.dma_start(out[bass.ds((2 * i + s) * P, P), :], ob[:, s]).then_inc(stored[s], 16)
            sp.wait_ge(*DC.done(T - 1, "b"))
            sp.dma_start(out[(T - 1) * P:N, :], ob[0:TAIL, 0]).then_inc(stored[0], 16)
            sp.wait_ge(stored[0], 16 * (T // 2 + 1))
            sp.wait_ge(stored[1], 16 * (T // 2))

        @block.gpsimd
        def _(pool):
            g = nc.gpsimd
            chain = sem("pool_chain")
            made = [0]

            def link(ins):
                made[0] += 1
                ins.then_inc(chain, 1)
                pool.wait_ge(chain, made[0])

            g.memset(x1[:, T - 1, :], 0.0).then_inc(x_zeroed, 1)
            g.memset(padz[:], 0).then_inc(pads_made, 1)
            g.memset(padi[:], PADDST).then_inc(pads_made, 1)
            g.memset(dstc[:, CB - 1, :], PADDST).then_inc(chunks_zeroed, 1)
            link(g.memset(ident[:], 0.0))
            link(g.affine_select(out=ident[:], in_=ident[:], compare_op=ALU.not_equal, fill=1.0, base=0,
                                 pattern=[[-1, P]], channel_multiplier=1))
            link(g.memset(tri[:], 0.0))
            link(g.affine_select(out=tri[:], in_=tri[:], compare_op=ALU.is_ge, fill=1.0, base=0,
                                 pattern=[[-1, P]], channel_multiplier=1))
            link(g.memset(hmask[:], 1.0))
            link(g.affine_select(out=hmask[:], in_=hmask[:], compare_op=ALU.is_ge, fill=0.0, base=0,
                                 pattern=[[-HD, HPC]], channel_multiplier=1))
            link(g.affine_select(out=hmask[:], in_=hmask[:], compare_op=ALU.is_ge, fill=0.0, base=HD - 1,
                                 pattern=[[HD, HPC]], channel_multiplier=-1))
            link(g.memset(bdmask[:], 1.0))
            link(g.affine_select(out=bdmask[:], in_=bdmask[:], compare_op=ALU.is_ge, fill=0.0, base=0,
                                 pattern=[[-HD, HPC], [0, HD]], channel_multiplier=1))
            link(g.affine_select(out=bdmask[:], in_=bdmask[:], compare_op=ALU.is_ge, fill=0.0, base=HD - 1,
                                 pattern=[[HD, HPC], [0, HD]], channel_multiplier=-1))
            link(g.memset(valid[:], 1.0))
            link(g.affine_select(out=valid[:], in_=valid[:], compare_op=ALU.is_ge, fill=0.0, base=N - 1,
                                 pattern=[[-P, T]], channel_multiplier=-1))
            g.memset(ones[:], 1.0)
            g.memset(zrows[:], 0.0).then_inc(zero_made, 1)
            link(g.memset(trilow[:], 0.0))
            link(g.affine_select(out=trilow[:], in_=trilow[:], compare_op=ALU.is_ge, fill=1.0, base=0,
                                 pattern=[[1, P]], channel_multiplier=-1))
            g.memset(one8[:], 1.0)
            io = dict(allow_small_or_imprecise_dtypes=True)
            g.iota(idrow[:], [[1, P]], base=-P, channel_multiplier=0, **io)
            g.iota(down8[:], [[-1, NE]], base=NE, channel_multiplier=0, **io)
            g.iota(ebase[:], [[REG, NE]], base=0, channel_multiplier=0, **io)
            g.iota(dummy[:], [[0, U]], base=N, channel_multiplier=1, **io)
            g.iota(cidx[:], [[P, CB]], base=1, channel_multiplier=1, **io)
            g.iota(cinv[:], [[-P, CB]], base=BIG, channel_multiplier=-1, **io)
            g.iota(tlo[:], [[P, T]], base=0, channel_multiplier=0, **io)
            g.iota(thi[:], [[P, T]], base=P - 1, channel_multiplier=0, **io)
            g.iota(bidx[:], [[1, MAXBLK]], base=0, channel_multiplier=0, **io).then_inc(consts_made, 1)

            GK.first(pool)

            def kv_tile(t, s):
                flat = (lambda z: z) if isinstance(t, int) else (lambda z: z.rearrange("p a f -> p (a f)"))
                pool.wait_ge(*DK.done(t, "norm"))
                g.tensor_copy(flat(tile(xn, t)), xs[:, s, :]).then_inc(*GK("keep"))
                g.tensor_tensor(flat(tile(x1, t)), flat(tile(x1, t)), xs[:, s, :], ALU.add).then_inc(*GK("res"))

            with pool.Fori(0, T // 2) as i:
                for s in range(2):
                    kv_tile(2 * i + s, s)
            kv_tile(T - 1, 0)

            pool.wait_ge(sums_zeroed, 16 * NACC)
            pool.wait_ge(*dveb.done(0, "min"))
            total = pool.alloc_register("pool_total")
            pool.reg_mov(total, 0)
            with pool.Fori(0, T) as t:
                pool.reg_add(total, total, pool.value_load(bnd[0:1, 1, bass.ds(t, 1)], min_val=NG, max_val=-(-CH // U)))
            with pool.Fori(0, pool.snap(total, min_val=NG * T, max_val=T * -(-CH // U))) as i:
                for k in range(U):
                    pool.wait_ge(idx_ready, i * U + k + 1)
                    apart(pool)
                    pool.wait_ge(msg_copied, (i + 1) * NPAIR + k // 2 + 1)
                    apart(pool)
                    if k >= NACC:
                        pool.wait_ge(scattered[k - NACC], i * 16 + 16)
                    else:
                        pool.wait_ge(scattered[k + NACC if k + NACC < U else k], i * 16)
                    apart(pool)
                    g.indirect_dma_start(sums[k % NACC], bass.IndirectOffsetOnAxis(ap=idx[:, k:k + 1], axis=0),
                                         msgs[:, k, :], None, compute_op=ALU.add).then_inc(scattered[k], 16)
            for k in range(U):
                pool.wait_ge(scattered[k], pool.snap(total, min_val=NG * T, max_val=T * -(-CH // U)) * 16)
                apart(pool)
            pool.sem_inc(all_scattered, 1)
            GG.first(pool)

            def add_parts(t, s, turn):
                pool.wait_ge(parts_loaded[s], 16 * NACC * (turn + 1))
                pool.wait_ge(*PG.done(t - 2, "aggT"))
                assert NACC == 4
                for k in range(1, NACC):
                    g.tensor_tensor(parts[:, s, 0, :], parts[:, s, 0, :], parts[:, s, k, :], ALU.add).then_inc(*GG(f"add{k}"))
                    pool.wait_ge(*GG.done(t, f"add{k}"))
                pool.wait_ge(consts_made, 1)

            with pool.Fori(0, T // 2) as i:
                for s in range(2):
                    add_parts(2 * i + s, s, i)
            add_parts(T - 1, 0, T // 2)
            GR.first(pool)

            def keep(t, s):
                pool.wait_ge(*DR.done(t, "xt"))
                g.tensor_copy(tile(xn, t) if isinstance(t, int) else tile(xn, t).rearrange("p a f -> p (a f)"),
                              xs[:, s, :]).then_inc(*GR("keep"))

            with pool.Fori(0, T // 2) as i:
                for s in range(2):
                    keep(2 * i + s, s)
            keep(T - 1, 0)

            def dispatch(t, s, rows):
                pool.wait_ge(*DD.done(t, "slot"))
                apart(pool)
                for j in range(2):
                    g.indirect_dma_start(
                        erows, bass.IndirectOffsetOnAxis(ap=slot_now[0:rows, s, j:j + 1], axis=0),
                        xn2[0:rows, s, :], None).then_inc(dispatched[s], 16)

            with pool.Fori(0, T // 2) as i:
                for s in range(2):
                    dispatch(2 * i + s, s, P)
            dispatch(T - 1, 0, TAIL)

            pool.wait_ge(*dve5.done(0, "inb"))
            nb = pool.value_load(ztab[0:1, NE:NE + 1], min_val=1, max_val=MAXBLK)
            pool.wait_ge(outs_zeroed, 1)
            pool.wait_ge(out_rows, nb * 16)
            apart(pool)

            def fetch(t, s, rows):
                pool.wait_ge(*DC.done(t, "idx"))
                apart(pool)
                pool.wait_ge(*DC.done(t - 2, "b"))
                apart(pool)
                for j in range(2):
                    g.indirect_dma_start(
                        yg[0:rows, s, j, :], None, eouts,
                        bass.IndirectOffsetOnAxis(ap=idx_c[0:rows, s, j:j + 1], axis=0)).then_inc(got[s][j], 16)

            with pool.Fori(0, T // 2) as i:
                for s in range(2):
                    fetch(2 * i + s, s, P)
            fetch(T - 1, 0, TAIL)

        @block.tensor
        def _(pe):
            for st in (PK, PKA, pe3, PM, PE_, peb, PG, PR_, per):
                st.first(pe)
            mm = nc.tensor.matmul
            pe.wait_ge(consts_made, 1)
            pe.wait_ge(kv_weights, 32)

            def project(t, s):
                tp = pT[:, 256 * s:256 * s + 256]
                pk = (pQ, pM)[s]
                pe.wait_ge(*DK.done(t, "norm"))
                pe.wait_ge(*AK.done(t - 2, "xnT"))
                pe.wait_ge(*DK.done(t - 2, "cstat1"))
                for c in range(FC):
                    last_ = nc.tensor.transpose(tp[:, c * P:(c + 1) * P], xs[:, s, c * P:(c + 1) * P], ident[:])
                last_.then_inc(*PK("trans"))
                pe.wait_ge(*AK.done(t, "xnT"))
                pe.wait_ge(*AK.done(t - 2, "vcopy"))
                pe.wait_ge(*DK.done(t - 2, "kelu"))
                for c in range(FC):
                    last_ = mm(pk[:], xnT[:, s, c, :], wkv[:, c, :], start=(c == 0), stop=(c == FC - 1))
                last_.then_inc(*PK("kv"))

            def accumulate(t, s, first=False, last=False):
                pe.wait_ge(*DK.done(t, "kelu"))
                pe.wait_ge(*AK.done(t, "vcopy"))
                for c in range(FC):
                    acc = (pG, pH)[c]
                    last_ = mm(acc[:, 0:P + 1], kelu[:, s, c * P:(c + 1) * P], vaug[:, s, c, :],
                               start=first, stop=last)
                last_.then_inc(*PKA("kvacc"))

            project(0, 0)
            project(1, 1)
            accumulate(0, 0, first=True)
            with pe.Fori(0, T // 2 - 1) as i:
                project(2 * i + 2, 0)
                accumulate(2 * i + 1, 1)
                project(2 * i + 3, 1)
                accumulate(2 * i + 2, 0)
            project(T - 1, 0)
            accumulate(T - 2, 1)
            accumulate(T - 1, 0, last=True)

            pe.wait_ge(weights, 16 * 15)
            nc.tensor.transpose(pR[:, 0:PR], rows_p[:], ident[0:PR, 0:PR]).then_inc(*pe3("params"))
            pe.wait_ge(*dve3.done(0, "dm1"))
            for c in range(FC):
                last_ = mm(pY[:, c * P:(c + 1) * P], ones[:], dmean[:, c, :], start=True, stop=True)
            last_.then_inc(*pe3("mean"))
            pe.wait_ge(*dveb.done(0, "vmaxlo"))
            nc.tensor.transpose(pA[0:2 * T, 0:P], vmax[:], ident[:]).then_inc(*peb("t1"))
            pe.wait_ge(*dveb.done(0, "vred"))
            nc.tensor.transpose(pA[0:1, 256:256 + 2 * T], vred[:], ident[0:2 * T, 0:2 * T]).then_inc(*peb("t2"))

            pe.wait_ge(*dveb.done(0, "min"))
            pe.wait_ge(*dve3.done(0, "gb"))
            pe.wait_ge(ccopy, 1)
            groups = pe.alloc_register("pe_groups")
            pe.reg_mov(groups, 0)
            W_ = P + HPC

            def turn(src_, step):
                for c in range(FC):
                    last_ = nc.tensor.transpose(pT[:, c * P:(c + 1) * P], src_[:, c * P:(c + 1) * P], ident[:])
                last_.then_inc(*PM(step))

            def step_xT(t):
                pe.wait_ge(*DM.done(t, "xs"))
                pe.wait_ge(*AM.done(t - 1, "mT1"))
                turn(xs[:, 0, :], "xT")

            def step_q(t):
                pe.wait_ge(*AM.done(t, "xT"))
                pe.wait_ge(*DM.done(t - 1, "hap"))
                for o in range(FC):
                    for c in range(FC):
                        last_ = mm(pQ[:, o * P:(o + 1) * P], wq[:, c, o * P:(o + 1) * P], xnT[:, 0, c, :],
                                   start=(c == 0), stop=(c == FC - 1))
                last_.then_inc(*PM("q"))

            def step_num(t):
                pe.wait_ge(*DM.done(t, "qelu"))
                for c in range(FC):
                    last_ = mm(pM[:, c * W_:(c + 1) * W_], qelu[:, c, :], kvbd[:, c, :], start=True, stop=True)
                last_.then_inc(*PM("num"))

            def step_msgT(t):
                pe.wait_ge(*DM.done(t, "msg"))
                turn(msg[:], "msgT")

            def step_mm(t):
                pe.wait_ge(*AM.done(t, "msgT"))
                for c in range(FC):
                    last_ = mm(pQ[:, 0:F], msgT[:, c, :], wm[:, c, :], start=(c == 0), stop=(c == FC - 1))
                last_.then_inc(*PM("mm"))

            def step_mT(t):
                pe.wait_ge(*DM.done(t, "map"))
                turn(mrow[:], "mT")

            def step_hid(t):
                pe.wait_ge(*AM.done(t, "mT1"))
                for o in range(HC):
                    for c in range(2 * FC):
                        r = xnT[:, 0, c, :] if c < FC else mT[:, c - FC, :]
                        last_ = mm(pH[:, o * P:(o + 1) * P], w1[:, c, o * P:(o + 1) * P], r,
                                   start=(c == 0), stop=(c == 2 * FC - 1))
                last_.then_inc(*PM("hid"))

            def step_h2(t):
                pe.wait_ge(*AM.done(t, "relu"))
                for c in range(HC):
                    last_ = mm(pQ[:, 0:F], hT[:, c, :], w2[:, c, :], start=(c == 0), stop=(c == HC - 1))
                last_.then_inc(*PM("h2"))

            def coefs(g):
                pe.wait_ge(onehots_made, g * (2 * U) + 2 * U + 1)
                for k in range(U):
                    if k % 4 == 0:
                        pe.wait_ge(coef_copied, g * 2 + k // 4 + 1)
                    last_ = mm(pC[k // 4][:, (k % 4) * P:(k % 4 + 1) * P], reads[:, k, :], same[:, k, :], start=True, stop=True)
                    if k % 4 == 3 or k == U - 1:
                        last_.then_inc(coef_done, 1)

            def messages(g, t):
                for k in range(U):
                    if k % 4 == 0:
                        pe.wait_ge(coef_copied, g * 2 + 2 + k // 4 + 1)
                    if k % 2 == 0:
                        pe.wait_ge(msg_copied, g * NPAIR + NPAIR + k // 2 - 1)
                    last_ = mm(pX[k // 2 % 2][:, (k % 2) * F:(k % 2 + 1) * F], coef[:, k, :],
                               tile(xn, t).rearrange("p a f -> p (a f)"), start=True, stop=True)
                    if k % 2 == 1 or k == U - 1:
                        last_.then_inc(msg_done, 1)

            before_coefs = [step_xT, step_num, step_msgT, step_mT, step_h2]
            before_msgs = [step_q, None, step_mm, step_hid, None]
            with pe.Fori(0, T) as t:
                n = pe.value_load(bnd[0:1, 1, bass.ds(t, 1)], min_val=NG, max_val=-(-CH // U))
                g0 = pe.snap(groups)
                for i in range(NG):
                    before_coefs[i](t)
                    coefs(g0 + i)
                    if before_msgs[i]:
                        before_msgs[i](t)
                    messages(g0 + i, t)
                with pe.If(n > NG):
                    with pe.Fori(NG, n) as i:
                        coefs(g0 + i)
                        messages(g0 + i, t)
                pe.reg_add(groups, groups, n)

            pe.wait_ge(*DM.done(T - 1, "res"))

            def gnn_T(t, s):
                pe.wait_ge(*GG.done(t, "add3"))
                pe.wait_ge(*AG.done(t - 2, "aggT"))
                for c in range(FC):
                    last_ = nc.tensor.transpose((pT, pQ)[s][:, c * P:(c + 1) * P], parts[:, s, 0, c * P:(c + 1) * P], ident[:])
                last_.then_inc(*PG("aggT"))

            def gnn_W_(t, s):
                pe.wait_ge(*AG.done(t, "aggT"))
                pe.wait_ge(*DG.done(t - 2, "res"))
                for c in range(FC):
                    last_ = mm((pM, pH)[s][:, 0:F], aggT[:, s, c, :], wgs[:, c, :], start=(c == 0), stop=(c == FC - 1))
                last_.then_inc(*PG("gnn"))

            with pe.Fori(0, T // 2) as i:
                for s in range(2):
                    gnn_T(2 * i + s, s)
                    gnn_W_(2 * i + s, s)
            gnn_T(T - 1, 0)
            gnn_W_(T - 1, 0)

            def route(t, s):
                pe.wait_ge(*DR.done(t, "xt"))
                pe.wait_ge(*AR.done(t - 2, "xT"))
                for c in range(FC):
                    last_ = nc.tensor.transpose((pT, pQ)[s][:, c * P:(c + 1) * P], xs[:, s, c * P:(c + 1) * P], ident[:])
                last_.then_inc(*PR_("xT"))
                pe.wait_ge(*AR.done(t, "xT"))
                pe.wait_ge(*AR.done(t - 2, "log"))
                for c in range(FC):
                    last_ = mm((pM, pH)[s][:, 0:NE], aggT[:, s, c, :], wr[:, c, :], start=(c == 0), stop=(c == FC - 1))
                last_.then_inc(*PR_("log"))

            with pe.Fori(0, T // 2) as i:
                for s in range(2):
                    route(2 * i + s, s)
            route(T - 1, 0)
            pe.wait_ge(*dver.done(0, "sum"))
            mm(pA[:, 0:TE], tri[:], hots[:].rearrange("p t e -> p (t e)"), start=True, stop=True).then_inc(*per("rank"))
            mm(pY[:, 0:TE], ones[:], hots[:].rearrange("p t e -> p (t e)"), start=True, stop=True).then_inc(*per("tot"))

            pe.wait_ge(*dve5.done(0, "inb"))
            nb = pe.value_load(ztab[0:1, NE:NE + 1], min_val=1, max_val=MAXBLK)
            with pe.Fori(0, nb) as b:
                pe.wait_ge(xb_loaded, 16 * b + 16)
                for c in range(FC):
                    pe.wait_ge(*DE.done(b - 1, f"x{c}"))
                    for m in range(BM):
                        last_ = nc.tensor.transpose((pT, pR)[c][:, m * P:(m + 1) * P], xb[:, m, c * P:(c + 1) * P], ident[:])
                    last_.then_inc(*PE_(f"t{c}"))
                pe.wait_ge(ew1_loaded, 16 * b + 16)
                pe.wait_ge(*DE.done(b, "x1"))
                for j in range(EHC):
                    if j >= 4:
                        pe.wait_ge(*AE.done(b, f"g{j - 4}"))
                    else:
                        pe.wait_ge(*AE.done(b - 1, f"g{j + 4}"))
                    for c in range(FC):
                        last_ = mm((pA, pQ, pM, pH)[j % 4][:, 0:BLK], ew1[:, c, j * P:(j + 1) * P], xeT[:, c, :],
                                   start=(c == 0), stop=(c == FC - 1))
                    last_.then_inc(*PE_(f"h{j}"))
                pe.wait_ge(ew2_loaded, 16 * b + 16)
                for m in range(BM):
                    pe.wait_ge(*DE.done(b - 1, f"y{m}"))
                    for j in range(EHC):
                        if m == 0:
                            pe.wait_ge(*AE.done(b, f"g{j}"))
                        last_ = mm((pY, pG)[m][:, 0:F], ehT[:, j, m * P:(m + 1) * P], ew2[:, j, :],
                                   start=(j == 0), stop=(j == EHC - 1))
                    last_.then_inc(*PE_(f"y{m}"))

        @block.scalar
        def _(act):
            a = nc.scalar.activation
            for st in (act2, AK, act3, AM, AE, AG, AR, acto, acti, actr):
                st.first(act)
            act.sem_inc(coef_copied, 2)
            act.sem_inc(msg_copied, NPAIR)

            def all_rstd(DV, AC):
                act.wait_ge(*DV.done(0, "ve"))
                a(rrstd[:], rvar[:], ACT.Ln).then_inc(*AC("ln"))
                act.wait_ge(*AC.done(0, "ln"))
                a(rtmp[:], rrstd[:], ACT.Exp, scale=-0.5).then_inc(*AC("exp"))

            all_rstd(dve2, act2)

            def kv_tile(t, s):
                tp = pT[:, 256 * s:256 * s + 256].rearrange("p (c q) -> p c q", c=FC)
                pk = (pQ, pM)[s]
                act.wait_ge(*PK.done(t, "trans"))
                act.wait_ge(*PK.done(t - 2, "kv"))
                a(xnT[:, s], tp, ACT.Copy).then_inc(*AK("xnT"))
                act.wait_ge(*DK.done(t, "kmin"))
                act.wait_ge(*DK.done(t - 2, "kelu"))
                a(kexp[:, s, :], kmin[:, s, :], ACT.Exp).then_inc(*AK("kexp"))
                act.wait_ge(*PKA.done(t - 2, "kvacc"))
                a(vaug[:, s, :, 0:P], pk[:, F:2 * F].rearrange("p (c q) -> p c q", c=FC), ACT.Copy).then_inc(*AK("vcopy"))

            with act.Fori(0, T // 2) as i:
                for s in range(2):
                    kv_tile(2 * i + s, s)
            kv_tile(T - 1, 0)

            act.wait_ge(*dve3.done(0, "aggr1"))
            a(cstd[:], cmv[:, :, 1], ACT.Sqrt, scale=float(N) / (N - 1)).then_inc(*act3("sqrt"))
            act.wait_ge(*pe3.done(0, "params"))
            a(colp[:], pR[:, 0:PR], ACT.Copy).then_inc(ccopy, 1)

            def rstd_ln(t, p):
                act.wait_ge(*DM.done(t, p + "ve"))
                a(lnln[:], lnve[:], ACT.Ln).then_inc(*AM(p + "ln"))
                act.wait_ge(*AM.done(t, p + "ln"))
                a(lny[:], lnln[:], ACT.Exp, scale=-0.5).then_inc(*AM(p + "exp"))

            act.wait_ge(*dveb.done(0, "min"))
            groups = act.alloc_register("act_groups")
            act.reg_mov(groups, 0)

            def copyT(t, out_, name):
                act.wait_ge(*PM.done(t, name))
                a(out_, pT[:, 0:F].rearrange("p (c q) -> p c q", c=FC), ACT.Copy).then_inc(*AM(name))

            def step_xT(t):
                act.wait_ge(*PM.done(t - 1, "hid"))
                copyT(t, xnT[:, 0], "xT")

            def step_qexp(t):
                act.wait_ge(*DM.done(t, "qmin"))
                a(qexp[:], qmin[:], ACT.Exp).then_inc(*AM("qexp"))

            def step_mT(t):
                act.wait_ge(*PM.done(t, "mT"))
                for c in range(FC):
                    a(mT[:, c, :], pT[:, c * P:(c + 1) * P], ACT.Identity, scale=colp[:, R_G1 + c:R_G1 + c + 1],
                      bias=colp[:, R_BB1 + c:R_BB1 + c + 1]).then_inc(*AM(f"mT{c}"))

            def step_relu(t):
                act.wait_ge(*PM.done(t, "hid"))
                a(hT[:], pH[:].rearrange("p (c q) -> p c q", c=HC), ACT.Relu).then_inc(*AM("relu"))

            def coefs(g):
                for b in range(2):
                    ks = range(4 * b, min(4 * b + 4, U))
                    act.wait_ge(coef_done, g * 2 + b + 1)
                    act.wait_ge(msg_done, g * NPAIR)
                    a(coef[:, ks[0]:ks[-1] + 1, :], pC[b][:, 0:len(ks) * P].rearrange("p (k q) -> p k q", q=P),
                      ACT.Copy).then_inc(coef_copied, 1)

            def messages(g):
                act.wait_ge(idx_float, g * 2 + 2)
                for k in range(U):
                    act.wait_ge(scattered[k], g * 16)
                    a(idx[:, k:k + 1], idxf[:, k:k + 1], ACT.Copy).then_inc(idx_ready, 1)
                    if k % 2 == 1 or k == U - 1:
                        j = k // 2
                        k0 = 2 * j
                        act.wait_ge(msg_done, g * NPAIR + j + 1)
                        a(msgs[:, k0:k + 1, :], pX[j % 2][:, 0:(k + 1 - k0) * F].rearrange("p (k f) -> p k f", f=F),
                          ACT.Copy).then_inc(msg_copied, 1)

            after_a = [step_xT, None, lambda t: copyT(t, msgT[:], "msgT"), step_mT, None]
            after_b = [step_qexp, None, lambda t: rstd_ln(t, "m"), step_relu, lambda t: rstd_ln(t, "h")]
            with act.Fori(0, T) as t:
                n = act.value_load(bnd[0:1, 1, bass.ds(t, 1)], min_val=NG, max_val=-(-CH // U))
                g0 = act.snap(groups)
                for i in range(NG):
                    if after_a[i]:
                        after_a[i](t)
                    coefs(g0 + i)
                    if after_b[i]:
                        after_b[i](t)
                    messages(g0 + i)
                with act.If(n > NG):
                    with act.Fori(NG, n) as i:
                        coefs(g0 + i)
                        messages(g0 + i)
                act.reg_add(groups, groups, n)

            def gnn(t, s):
                act.wait_ge(*PG.done(t, "aggT"))
                act.wait_ge(*PG.done(t - 2, "gnn"))
                a(aggT[:, s], (pT, pQ)[s][:, 0:F].rearrange("p (c q) -> p c q", c=FC), ACT.Copy).then_inc(*AG("aggT"))

            with act.Fori(0, T // 2) as i:
                for s in range(2):
                    gnn(2 * i + s, s)
            gnn(T - 1, 0)
            all_rstd(dveo, acto)

            def route(t, s):
                act.wait_ge(*PR_.done(t, "xT"))
                act.wait_ge(*PR_.done(t - 2, "log"))
                a(aggT[:, s], (pT, pQ)[s][:, 0:F].rearrange("p (c q) -> p c q", c=FC), ACT.Copy).then_inc(*AR("xT"))
                act.wait_ge(*PR_.done(t, "log"))
                lo_ = tile(logits, t)
                a(lo_ if isinstance(t, int) else lo_.rearrange("p a e -> p (a e)"), (pM, pH)[s][:, 0:NE],
                  ACT.Copy).then_inc(*AR("log"))

            with act.Fori(0, T // 2) as i:
                for s in range(2):
                    route(2 * i + s, s)
            route(T - 1, 0)
            all_rstd(dvei, acti)
            act.wait_ge(*dver.done(0, "dif"))
            a(best[:, 0, :], best[:, 1, :], ACT.Exp).then_inc(*actr("exp"))

            act.wait_ge(*dve5.done(0, "inb"))
            nb = act.value_load(ztab[0:1, NE:NE + 1], min_val=1, max_val=MAXBLK)
            with act.Fori(0, nb) as b:
                e = act.value_load(btab[0:1, 1, bass.ds(b, 1)], min_val=0, max_val=NE - 1)
                for j in range(EHC):
                    act.wait_ge(*PE_.done(b, f"h{j}"))
                    act.wait_ge(*PE_.done(b - 1, "y1"))
                    a(ehT[:, j, :], (pA, pQ, pM, pH)[j % 4][:, 0:BLK], ACT.Gelu,
                      bias=colp[:, bass.ds(e * EHC + R_B1 + j, 1)]).then_inc(*AE(f"g{j}"))
                act.wait_ge(*DE.done(b, "y1"))
                act.dma_start(eouts[bass.ds(b * BLK, BLK), :].rearrange("(m p) f -> p m f", p=P), yb[:]).then_inc(out_rows, 16)

        @block.vector
        def _(dve):
            v = nc.vector
            kept = [0]
            for st in (dve1, dve2, DK, dve3, DM, dve5, DE, DC, dveb, dve6, DG, DR, dveo, dvei, dver, DD):
                st.first(dve)
            for st in (counted, onehots_made):
                dve.sem_inc(st, 1)
            dve.wait_ge(consts_made, 1)
            dve.wait_ge(x_loaded, 16 * (nxc + 1))
            with dve.Fori(0, T) as t:
                v.bn_stats(tile(bst, t), tile(x1, t)).then_inc(*dve1("stats"))
            dve.wait_ge(*dve1.done(T - 1, "stats"))
            own = lambda st, name: dve.wait_ge(*st.done(0, name))

            def all_rstd(D, AC):
                me, mo, ve, vo = bst[:, :, 1], bst[:, :, 4], bst[:, :, 2], bst[:, :, 5]
                v.tensor_tensor(rmean[:], me, mo, ALU.add).then_inc(*D("msum"))
                own(D, "msum")
                v.tensor_scalar(rmean[:], rmean[:], 0.5, None, ALU.mult).then_inc(*D("mean"))
                v.tensor_tensor(rtmp[:], me, mo, ALU.subtract).then_inc(*D("dif"))
                v.tensor_tensor(rvar[:], ve, vo, ALU.add).then_inc(*D("m2"))
                own(D, "m2")
                v.tensor_tensor(rtmp[:], rtmp[:], rtmp[:], ALU.mult).then_inc(*D("dif2"))
                v.tensor_scalar(rvar[:], rvar[:], 1.0 / F, None, ALU.mult).then_inc(*D("dif4"))
                own(D, "dif4")
                v.scalar_tensor_tensor(rvar[:], rtmp[:], 0.25, rvar[:], ALU.mult, ALU.add).then_inc(*D("var"))
                own(D, "var")
                v.tensor_scalar(rvar[:], rvar[:], EPS, None, ALU.add).then_inc(*D("ve"))
                dve.wait_ge(*AC.done(0, "exp"))
                v.tensor_tensor(rrstd[:], rtmp[:], rtmp[:], ALU.mult).then_inc(*D("a"))
                own(D, "a")
                v.tensor_tensor(rvar[:], rrstd[:], rvar[:], ALU.mult).then_inc(*D("nr"))
                own(D, "nr")
                v.tensor_scalar(rvar[:], rvar[:], -0.5, 1.5, ALU.mult, ALU.add).then_inc(*D("y"))
                own(D, "y")
                v.tensor_tensor(rrstd[:], rtmp[:], rvar[:], ALU.mult).then_inc(*D("rstd"))
                own(D, "rstd")

            all_rstd(dve2, act2)
            rs_done = sem("ones_column")
            v.memset(vaug[:, :, :, P:P + 1], 1.0).then_inc(rs_done, 1)
            dve.wait_ge(rs_done, 1)

            def kv_tile(t, s, rows):
                tp = pT[:, 256 * s:256 * s + 256]
                pk = (pQ, pM)[s]
                x1t = tile(x1, t) if isinstance(t, int) else tile(x1, t).rearrange("p a f -> p (a f)")
                dve.wait_ge(*PK.done(t - 2, "trans"))
                dve.wait_ge(*GK.done(t - 2, "res"))
                v.tensor_scalar(xs[:, s, :], x1t, col(rmean, t), col(rrstd, t),
                                ALU.subtract, ALU.mult).then_inc(*DK("norm"))
                dve.wait_ge(*PK.done(t, "trans"))
                dve.wait_ge(*AK.done(t, "xnT"))
                apart(dve)
                for c in range(FC):
                    v.bn_stats(cst[:, c, t, :] if isinstance(t, int) else cst[:, c, bass.ds(t, 1), :],
                               tp[:, c * P:c * P + rows]).then_inc(*DK(f"cstat{c}"))
                dve.wait_ge(*PK.done(t, "kv"))
                dve.wait_ge(*AK.done(t - 2, "kexp"))
                v.tensor_scalar(kmin[:, s, :], pk[:, 0:F], 0.0, None, ALU.min).then_inc(*DK("kmin"))
                dve.wait_ge(*AK.done(t, "kexp"))
                dve.wait_ge(*AK.done(t, "vcopy"))
                dve.wait_ge(*PKA.done(t - 2, "kvacc"))
                v.scalar_tensor_tensor(kelu[:, s, :], pk[:, 0:F], 0.0, kexp[:, s, :], ALU.max, ALU.add).then_inc(*DK("kelu"))

            with dve.Fori(0, T // 2) as i:
                for s in range(2):
                    kv_tile(2 * i + s, s, P)
            dve.wait_ge(*PKA.done(T - 3, "kvacc"))
            vt = sem("vaug_tail")
            for c in range(FC):
                v.tensor_copy(vaug[:, 0, c, P:P + 1], valid[:, T - 1:T]).then_inc(vt, 1)
            dve.wait_ge(vt, 2)
            kv_tile(T - 1, 0, TAIL)

            for c in range(FC):
                dve.wait_ge(*DK.done(T - 1, "cstat1"))
                v.bn_aggr(cmv[:, c, :], cst[:, c].rearrange("p t s -> p (t s)")).then_inc(*dve3(f"aggr{c}"))
            dve.wait_ge(*act3.done(0, "sqrt"))
            dve.wait_ge(weights, 16 * 15)
            v.tensor_scalar(cstd[:], cstd[:], STD_EPS, None, ALU.add).then_inc(*dve3("std"))
            own(dve3, "std")
            v.reciprocal(cstd[:], cstd[:]).then_inc(*dve3("inv"))
            own(dve3, "inv")
            for c in range(FC):
                v.tensor_scalar(wgs[:, c, :], wg[:, c, :], cstd[:, c:c + 1], None, ALU.mult).then_inc(*dve3(f"wgs{c}"))
            for c in range(FC):
                v.tensor_scalar(dmean[:, c, :], ident[:], cmv[:, c, 0:1], None, ALU.mult).then_inc(*dve3(f"dm{c}"))
            dve.wait_ge(*pe3.done(0, "mean"))
            v.tensor_copy(mean_bc[:], pY[:, 0:F]).then_inc(*dve3("meanbc"))
            own(dve3, "meanbc")
            dve.wait_ge(*GK.done(T - 1, "res"))
            TG = 7
            for k in range(T // TG):
                xk = xn[:, k * TG:(k + 1) * TG, :]
                v.tensor_tensor(xk, xk, mean_bc[:].unsqueeze(1).to_broadcast([P, TG, F]), ALU.subtract).then_inc(cen_made, 1)
            dve.wait_ge(cen_made, T // TG)
            for c in range(FC):
                acc = (pG, pH)[c]
                v.tensor_tensor(kvbd[:, c, 0:P], acc[:, 0:P], bdmask[:].rearrange("p a b -> p (a b)"), ALU.mult).then_inc(*dve3(f"kv{c}"))
            for c in range(FC):
                acc = (pG, pH)[c]
                v.tensor_scalar(kvbd[:, c, P:P + HPC], hmask[:], acc[:, P:P + 1], None, ALU.mult).then_inc(*dve3(f"ks{c}"))
            v.tensor_tensor(bias_bc[:], bias_bc[:], gb_bc[:], ALU.add).then_inc(*dve3("gb"))

            dve.wait_ge(chunks_loaded, 32)
            v.tensor_reduce(cmax[:], dstc[:], AX_X, ALU.max).then_inc(*dveb("cmax"))
            v.tensor_reduce(cmin[:], dstc[:], AX_X, ALU.min).then_inc(*dveb("cmin"))
            own(dveb, "cmin")
            bt = lambda z: z[:].unsqueeze(2).to_broadcast([P, T, CB])
            bc = lambda z: z[:].unsqueeze(1).to_broadcast([P, T, CB])
            v.tensor_tensor(indA[:], bc(cmin), bt(thi), ALU.is_le).then_inc(*dveb("indA"))
            v.tensor_tensor(indB[:], bc(cmax), bt(tlo), ALU.is_ge).then_inc(*dveb("indB"))
            own(dveb, "indB")
            v.tensor_tensor(indA[:], indA[:], indB[:], ALU.mult).then_inc(*dveb("ind"))
            own(dveb, "ind")
            v.tensor_tensor(indB[:], indA[:], bc(cidx), ALU.mult).then_inc(*dveb("vhi"))
            own(dveb, "vhi")
            v.tensor_reduce(vmax[:, 0:T], indB[:], AX_X, ALU.max).then_inc(*dveb("vmaxhi"))
            v.tensor_tensor(indA[:], indA[:], bc(cinv), ALU.mult).then_inc(*dveb("vlo"))
            own(dveb, "vlo")
            v.tensor_reduce(vmax[:, T:2 * T], indA[:], AX_X, ALU.max).then_inc(*dveb("vmaxlo"))
            dve.wait_ge(*peb.done(0, "t1"))
            v.tensor_reduce(vred[:], pA[0:2 * T, 0:P], AX_X, ALU.max).then_inc(*dveb("vred"))
            dve.wait_ge(*peb.done(0, "t2"))
            v.tensor_copy(brow[:], pA[0:1, 256:256 + 2 * T]).then_inc(*dveb("row"))
            own(dveb, "row")
            hi, lo = brow[:, 0:T], brow[:, T:2 * T]
            v.tensor_scalar(hi, hi, float(CH), 1.0, ALU.min, ALU.max).then_inc(*dveb("hi1"))
            v.tensor_scalar(lo, lo, -1.0, float(BIG), ALU.mult, ALU.add).then_inc(*dveb("lo1"))
            own(dveb, "lo1")
            v.tensor_scalar(bndf[:, 1, :], hi, -1.0, None, ALU.add).then_inc(*dveb("hi2"))
            own(dveb, "hi2")
            v.tensor_tensor(lo, lo, bndf[:, 1, :], ALU.min).then_inc(*dveb("lo2"))
            own(dveb, "lo2")
            v.tensor_tensor(hi, hi, lo, ALU.subtract).then_inc(*dveb("n1"))
            own(dveb, "n1")
            RECIP, SHIFT = -(-(1 << 16) // U), 16
            assert (CH + U) * RECIP < 1 << 24
            v.tensor_scalar(bndf[:, 1, :], hi, float(U - 1), None, ALU.add).then_inc(*dveb("n2"))
            own(dveb, "n2")
            v.tensor_scalar(bndf[:, 1, :], bndf[:, 1, :], float(RECIP), None, ALU.mult).then_inc(*dveb("mul"))
            v.tensor_scalar(bndf[:, 0, :], lo, float(CH - (NG - 1) * U), float(P), ALU.min, ALU.mult).then_inc(*dveb("elo"))
            own(dveb, "elo")
            v.tensor_copy(bnd[:, 0, :], bndf[:, 0, :]).then_inc(*dveb("ielo"))
            v.tensor_copy(bnd[:, 1, :], bndf[:, 1, :]).then_inc(*dveb("in"))
            own(dveb, "in")
            v.tensor_single_scalar(bnd[:, 1, :], bnd[:, 1, :], SHIFT, ALU.logical_shift_right).then_inc(*dveb("shr"))
            own(dveb, "shr")
            v.tensor_scalar(bnd[:, 1, :], bnd[:, 1, :], float(NG), None, ALU.max).then_inc(*dveb("min"))
            own(dveb, "min")
            dve.wait_ge(ccopy, 1)
            own(dve3, "gb")

            groups = dve.alloc_register("dve_groups")
            dve.reg_mov(groups, 0)

            def me_(t, name):
                dve.wait_ge(*DM.done(t, name))

            def norm(t, p, src_ap, dst_ap):
                apart(dve)
                v.bn_stats(lnst[:], src_ap).then_inc(*DM(p + "st"))
                me_(t, p + "st")
                apart(dve)
                v.bn_aggr(lnmv[:], lnst[:]).then_inc(*DM(p + "ag"))
                me_(t, p + "ag")
                v.tensor_scalar(lnve[:], lnmv[:, 1:2], EPS, None, ALU.add).then_inc(*DM(p + "ve"))
                dve.wait_ge(*AM.done(t, p + "exp"))
                v.scalar_tensor_tensor(lna[:], lny[:], lnve[:], lny[:], ALU.mult, ALU.mult).then_inc(*DM(p + "a"))
                me_(t, p + "a")
                v.tensor_scalar(lna[:], lna[:], -0.5, 1.5, ALU.mult, ALU.add).then_inc(*DM(p + "nr"))
                me_(t, p + "nr")
                v.tensor_tensor(lnr[:], lna[:], lny[:], ALU.mult).then_inc(*DM(p + "r"))
                me_(t, p + "r")
                v.tensor_scalar(dst_ap, src_ap, lnmv[:, 0:1], lnr[:], ALU.subtract, ALU.mult).then_inc(*DM(p + "ap"))

            def step_start(t):
                dve.wait_ge(onehots_made, dve.snap(groups) * (2 * U) + 1)
                v.tensor_scalar(idrow[:], idrow[:], float(P), None, ALU.add).then_inc(*DM("idrow"))
                dve.wait_ge(*PM.done(t - 1, "xT"))
                v.tensor_tensor(xs[:, 0, :], tile(xn, t).rearrange("p a f -> p (a f)"), mean_bc[:], ALU.add).then_inc(*DM("xs"))
                me_(t, "idrow")

            def step_q(t):
                dve.wait_ge(*PM.done(t, "q"))
                q3 = pQ[:, 0:F].rearrange("p (c q) -> p c q", c=FC)
                v.tensor_scalar(qmin[:], q3, 0.0, None, ALU.min).then_inc(*DM("qmin"))
                dve.wait_ge(*AM.done(t, "qexp"))
                v.scalar_tensor_tensor(qelu[:], q3, 0.0, qexp[:], ALU.max, ALU.add).then_inc(*DM("qelu"))

            def step_msg(t):
                dve.wait_ge(*PM.done(t, "num"))
                pm3 = pM[:, 0:FC * (P + HPC)].rearrange("p (c w) -> p c w", c=FC)
                v.tensor_scalar(rden[:], pm3[:, :, P:P + HPC], ATT_EPS, None, ALU.add).then_inc(*DM("eps"))
                me_(t, "eps")
                v.reciprocal(rden[:], rden[:]).then_inc(*DM("rden"))
                me_(t, "rden")
                v.tensor_tensor(msg[:].rearrange("p (c h d) -> p c h d", c=FC, h=HPC),
                                pm3[:, :, 0:P].rearrange("p c (h d) -> p c h d", h=HPC),
                                rden[:].unsqueeze(3).to_broadcast([P, FC, HPC, HD]), ALU.mult).then_inc(*DM("msg"))

            def step_mnorm(t):
                dve.wait_ge(*PM.done(t, "mm"))
                norm(t, "m", pQ[:, 0:F], mrow[:])

            def step_hnorm(t):
                dve.wait_ge(*PM.done(t, "h2"))
                norm(t, "h", pQ[:, 0:F], mrow[:])
                me_(t, "hap")
                v.tensor_tensor(mrow[:], mrow[:], g2_bc[:], ALU.mult).then_inc(*DM("g2"))
                me_(t, "g2")
                v.tensor_tensor(mrow[:], mrow[:], bias_bc[:], ALU.add).then_inc(*DM("b2"))
                me_(t, "b2")
                x1t = tile(x1, t).rearrange("p a f -> p (a f)")
                v.tensor_tensor(x1t, x1t, mrow[:], ALU.add).then_inc(*DM("res"))

            rows_of = src_row[:].rearrange("p (e k) -> p k e", k=U)

            def onehots(g):
                dve.wait_ge(edges_loaded, g * 64 + 64)
                dve.wait_ge(idx_float, g * 2)
                v.tensor_copy(dstf[:], dst_e[:]).then_inc(floats_made, 1)
                v.tensor_copy(srcf[:], src_e[:]).then_inc(floats_made, 1)
                dve.wait_ge(coef_done, g * 2)
                dve.wait_ge(floats_made, g * 2 + 2)
                for k in range(U):
                    v.tensor_scalar(reads[:, k, :], idrow[:], dstf[:, k:k + 1], w_e[:, k:k + 1],
                                    ALU.is_equal, ALU.mult).then_inc(onehots_made, 1)
                    v.tensor_scalar(same[:, k, :], rows_of[:, k, :], srcf[:, k:k + 1], None,
                                    ALU.is_equal).then_inc(onehots_made, 1)

            def indices(g):
                dve.wait_ge(counted, g * (U + 1) + 1)
                v.tensor_tensor(away[:], dummy[:], srcf[:], ALU.subtract).then_inc(counted, 1)
                dve.wait_ge(onehots_made, g * (2 * U) + 2 * U + 1)
                for k in range(U):
                    v.scalar_tensor_tensor(junk[:, k, :], same[:, k, :], 1.0, trilow[:], ALU.mult, ALU.mult,
                                           accum_out=before[:, k:k + 1]).then_inc(counted, 1)
                dve.wait_ge(counted, g * (U + 1) + U + 2)
                dve.wait_ge(idx_ready, g * U)
                v.scalar_tensor_tensor(away[:], before[:], 0.0, away[:], ALU.is_gt, ALU.mult).then_inc(idx_float, 1)
                dve.wait_ge(idx_float, g * 2 + 1)
                v.tensor_tensor(idxf[:], away[:], srcf[:], ALU.add).then_inc(idx_float, 1)

            pieces = [step_q, step_msg, step_mnorm, None, step_hnorm]
            with dve.Fori(0, T) as t:
                n = dve.value_load(bnd[0:1, 1, bass.ds(t, 1)], min_val=NG, max_val=-(-CH // U))
                step_start(t)
                g0 = dve.snap(groups)
                for i in range(NG):
                    onehots(g0 + i)
                    indices(g0 + i)
                    if pieces[i]:
                        pieces[i](t)
                with dve.If(n > NG):
                    with dve.Fori(NG, n) as i:
                        onehots(g0 + i)
                        indices(g0 + i)
                dve.reg_add(groups, groups, n)

            flat = lambda b, t: tile(b, t) if isinstance(t, int) else tile(b, t).rearrange("p a f -> p (a f)")

            def gnn(t, s):
                dve.wait_ge(*PG.done(t, "gnn"))
                v.tensor_tensor(flat(x1, t), flat(x1, t), (pM, pH)[s][:, 0:F], ALU.add).then_inc(*DG("res"))
                dve.wait_ge(*DG.done(t, "res"))
                apart(dve)
                v.bn_stats(flat(bst, t), flat(x1, t)).then_inc(*DG("stats"))

            with dve.Fori(0, T // 2) as i:
                for s in range(2):
                    gnn(2 * i + s, s)
            gnn(T - 1, 0)
            dve.wait_ge(*DG.done(T - 1, "stats"))
            all_rstd(dveo, acto)

            def outer(t, s):
                dve.wait_ge(*PR_.done(t - 2, "xT"))
                dve.wait_ge(*GR.done(t - 2, "keep"))
                v.tensor_scalar(xs[:, s, :], flat(x1, t), col(rmean, t), col(rrstd, t),
                                ALU.subtract, ALU.mult).then_inc(*DR("xt"))
                dve.wait_ge(*DR.done(t, "xt"))
                apart(dve)
                v.bn_stats(flat(bst, t), xs[:, s, :]).then_inc(*DR("stats"))

            with dve.Fori(0, T // 2) as i:
                for s in range(2):
                    outer(2 * i + s, s)
            outer(T - 1, 0)
            dve.wait_ge(*DR.done(T - 1, "stats"))
            all_rstd(dvei, acti)

            D = dver
            te = [P, T, NE]
            over_e = lambda z: z.unsqueeze(2).to_broadcast(te)
            dve.wait_ge(*AR.done(T - 1, "log"))
            v.tensor_tensor(logits[:], logits[:], br_bc[:].unsqueeze(1).to_broadcast(te), ALU.add).then_inc(*D("br"))
            own(D, "br")
            for j in range(2):
                v.tensor_reduce(best[:, j, :], logits[:], AX_X, ALU.max).then_inc(*D(f"b{j}"))
                own(D, f"b{j}")
                v.tensor_tensor(hot[:, j], logits[:], over_e(best[:, j, :]), ALU.is_equal).then_inc(*D(f"e{j}"))
                own(D, f"e{j}")
                v.tensor_tensor(work[:, 0], hot[:, j], down8[:].unsqueeze(1).to_broadcast(te), ALU.mult).then_inc(*D(f"r{j}"))
                own(D, f"r{j}")
                v.tensor_reduce(which[:], work[:, 0], AX_X, ALU.max).then_inc(*D(f"w{j}"))
                own(D, f"w{j}")
                v.tensor_tensor(hot[:, j], work[:, 0], over_e(which[:]), ALU.is_equal).then_inc(*D(f"h{j}"))
                own(D, f"h{j}")
                if j == 0:
                    v.tensor_scalar(work[:, 1], hot[:, 0], -3e38, None, ALU.mult).then_inc(*D("p0"))
                    own(D, "p0")
                    v.tensor_tensor(logits[:], logits[:], work[:, 1], ALU.add).then_inc(*D("l1"))
                    own(D, "l1")
            v.tensor_tensor(best[:, 1, :], best[:, 1, :], best[:, 0, :], ALU.subtract).then_inc(*D("dif"))
            dve.wait_ge(*actr.done(0, "exp"))
            v.tensor_scalar(best[:, 1, :], best[:, 0, :], 1.0, None, ALU.add).then_inc(*D("den"))
            own(D, "den")
            v.reciprocal(wts[:, :, 0], best[:, 1, :]).then_inc(*D("wa"))
            own(D, "wa")
            v.tensor_tensor(wts[:, :, 1], wts[:, :, 0], best[:, 0, :], ALU.mult).then_inc(*D("wb"))
            for j in range(2):
                v.tensor_tensor(hot[:, j], hot[:, j], over_e(valid[:]), ALU.mult).then_inc(*D(f"v{j}"))
            own(D, "v1")
            v.tensor_tensor(hots[:], hot[:, 0], hot[:, 1], ALU.add).then_inc(*D("sum"))
            dve.wait_ge(*per.done(0, "tot"))
            v.tensor_copy(work[:, 0].rearrange("p t e -> p (t e)"), pY[:, 0:TE]).then_inc(*D("tot"))
            own(D, "tot")
            cur, step = 0, 1
            while step < T:
                nxt = 1 - cur
                v.tensor_tensor(work[:, nxt, step:T, :], work[:, cur, step:T, :], work[:, cur, 0:T - step, :], ALU.add).then_inc(*D(f"s{step}"))
                v.tensor_copy(work[:, nxt, 0:step, :], work[:, cur, 0:step, :]).then_inc(prefix_kept, 1)
                own(D, f"s{step}")
                kept[0] += 1
                dve.wait_ge(prefix_kept, kept[0])
                cur, step = nxt, 2 * step
            run = work[:, cur]
            v.tensor_copy(lastcnt[:], run[:, T - 1, :]).then_inc(prefix_kept, 1)
            kept[0] += 1
            dve.wait_ge(prefix_kept, kept[0])
            fl = lambda z: z.rearrange("p t e -> p (t e)")
            v.tensor_tensor(fl(run), fl(run), pY[:, 0:TE], ALU.subtract).then_inc(*D("sub"))
            own(D, "sub")
            v.tensor_tensor(fl(run), fl(run), pA[:, 0:TE], ALU.add).then_inc(*D("rank"))
            own(D, "rank")
            v.tensor_tensor(run, run, ebase[:].unsqueeze(1).to_broadcast(te), ALU.add).then_inc(*D("base"))
            own(D, "base")
            for j in range(2):
                v.tensor_tensor(work[:, 1 - cur], hot[:, j], run, ALU.mult).then_inc(*D(f"p{j}x"))
                own(D, f"p{j}x")
                v.tensor_reduce(slotf[:, :, j], work[:, 1 - cur], AX_X, ALU.add).then_inc(*D(f"s{j}x"))
                own(D, f"s{j}x")
            v.tensor_tensor(carry[:], lastcnt[:], ebase[:], ALU.add).then_inc(*D("last"))

            def hand(t, s, turn):
                dve.wait_ge(dispatched[s], turn * 32)
                v.tensor_scalar(xn2[:, s, :], flat(xn, t), col(rmean, t), col(rrstd, t),
                                ALU.subtract, ALU.mult).then_inc(*DD("xn2"))
                v.tensor_copy(slot_now[:, s, :], flat(slotf, t)).then_inc(*DD("slot"))

            dve.wait_ge(*GR.done(T - 1, "keep"))
            with dve.Fori(0, T // 2) as i:
                for s in range(2):
                    hand(2 * i + s, s, i)
            hand(T - 1, 0, T // 2)

            own(dver, "last")
            dve.wait_ge(*DD.done(T - 1, "slot"))
            v.tensor_tensor(cnt[:], carry[:], ebase[:], ALU.subtract).then_inc(*dve5("cnt"))
            own(dve5, "cnt")
            v.tensor_scalar(cnt[:], cnt[:], float(BLK - 1), None, ALU.add).then_inc(*dve5("c255"))
            own(dve5, "c255")
            v.tensor_copy(cnti[:], cnt[:]).then_inc(*dve5("ci"))
            own(dve5, "ci")
            v.tensor_single_scalar(cnti[:], cnti[:], 8, ALU.logical_shift_right).then_inc(*dve5("sh"))
            own(dve5, "sh")
            v.tensor_copy(nblk[:], cnti[:]).then_inc(*dve5("nb"))
            own(dve5, "nb")
            v.tensor_tensor_scan(cum[:], one8[:], nblk[:], 0.0, ALU.mult, ALU.add).then_inc(*dve5("cum"))
            own(dve5, "cum")
            bb = bidx[:].unsqueeze(2).to_broadcast([1, MAXBLK, NE])
            v.tensor_tensor(le[:], cum[0:1].unsqueeze(1).to_broadcast([1, MAXBLK, NE]), bb, ALU.is_le).then_inc(*dve5("le"))
            own(dve5, "le")
            v.tensor_tensor(lenb[:], le[:], nblk[0:1].unsqueeze(1).to_broadcast([1, MAXBLK, NE]), ALU.mult).then_inc(*dve5("lenb"))
            own(dve5, "lenb")
            v.tensor_reduce(be[:], le[:], AX_X, ALU.add).then_inc(*dve5("be"))
            v.tensor_reduce(bprev[:], lenb[:], AX_X, ALU.add).then_inc(*dve5("bprev"))
            own(dve5, "bprev")
            v.tensor_tensor(bstart[:], bidx[:], bprev[:], ALU.subtract).then_inc(*dve5("st1"))
            own(dve5, "st1")
            v.tensor_scalar(bstart[:], bstart[:], float(BLK), None, ALU.mult).then_inc(*dve5("st2"))
            own(dve5, "st2")
            v.scalar_tensor_tensor(btab[:, 0, :], be[:], float(REG), bstart[:], ALU.mult, ALU.add).then_inc(*dve5("itab"))
            v.tensor_copy(btab[:, 1, :], be[:]).then_inc(*dve5("ibe"))
            v.tensor_copy(ztab[:, 0:NE], carry[0:1, :]).then_inc(*dve5("izt"))
            v.tensor_copy(ztab[:, NE:NE + 1], cum[0:1, NE - 1:NE]).then_inc(*dve5("inb"))
            own(dve5, "inb")
            nb = dve.value_load(ztab[0:1, NE:NE + 1], min_val=1, max_val=MAXBLK)
            with dve.Fori(0, nb) as b:
                e = dve.value_load(btab[0:1, 1, bass.ds(b, 1)], min_val=0, max_val=NE - 1)
                dve.wait_ge(*PE_.done(b - 1, f"h{EHC - 1}"))
                for c in range(FC):
                    dve.wait_ge(*PE_.done(b, f"t{c}"))
                    v.tensor_scalar(xeT[:, c, :], (pT, pR)[c][:, 0:BLK], colp[:, bass.ds(e * FC + R_G + c, 1)],
                                    colp[:, bass.ds(e * FC + R_B + c, 1)], ALU.mult, ALU.add).then_inc(*DE(f"x{c}"))
                dve.wait_ge(eb2_loaded, 16 * b + 16)
                dve.wait_ge(out_rows, 16 * b)
                for m in range(BM):
                    dve.wait_ge(*PE_.done(b, f"y{m}"))
                    v.tensor_tensor(yb[:, m, :], (pY, pG)[m][:, 0:F], eb2_bc[:], ALU.add).then_inc(*DE(f"y{m}"))

            own(dve5, "inb")
            v.tensor_tensor(delta[:], cum[:], nblk[:], ALU.subtract).then_inc(*dve6("excl"))
            own(dve6, "excl")
            v.tensor_scalar(delta[:], delta[:], float(BLK), None, ALU.mult).then_inc(*dve6("rows"))
            own(dve6, "rows")
            v.tensor_tensor(delta[:], delta[:], ebase[:], ALU.subtract).then_inc(*dve6("delta"))
            own(dve6, "delta")
            for j in range(2):
                v.tensor_tensor(hot[:, j], hot[:, j], delta[:].unsqueeze(1).to_broadcast(te), ALU.mult).then_inc(*dve6(f"hot{j}"))
            own(dve6, "hot1")
            for j in range(2):
                v.tensor_reduce(slotc[:, :, j], hot[:, j], AX_X, ALU.add).then_inc(*dve6(("shift", "slot")[j]))
            own(dve6, "slot")
            v.tensor_tensor(slotf[:], slotf[:], slotc[:], ALU.add).then_inc(prefix_kept, 1)
            dve.wait_ge(prefix_kept, kept[0] + 1)

            def combine_all(t, s, turn):
                rows = TAIL if isinstance(t, int) else P
                flat = (lambda z: z) if isinstance(t, int) else (lambda z: z.rearrange("p a f -> p (a f)"))
                x1t, wt, sl = flat(tile(x1, t)), flat(tile(wts, t)), flat(tile(slotf, t))
                v.tensor_copy(idx_c[:, s, :], sl).then_inc(*DC("idx"))
                dve.wait_ge(got[s][0], 16 * turn + 16)
                dve.wait_ge(stored[s], 16 * turn)
                v.scalar_tensor_tensor(ob[0:rows, s, :], yg[0:rows, s, 0, :], wt[0:rows, 0:1], x1t[0:rows],
                                       ALU.mult, ALU.add).then_inc(*DC("a"))
                dve.wait_ge(*DC.done(t, "a"))
                dve.wait_ge(got[s][1], 16 * turn + 16)
                v.scalar_tensor_tensor(ob[0:rows, s, :], yg[0:rows, s, 1, :], wt[0:rows, 1:2], ob[0:rows, s, :],
                                       ALU.mult, ALU.add).then_inc(*DC("b"))
                dve.wait_ge(*DC.done(t, "b"))
                apart(dve)

            with dve.Fori(0, T // 2) as i:
                for s in range(2):
                    combine_all(2 * i + s, s, i)
            combine_all(T - 1, 0, T // 2)


_INS = ['x', 'src', 'dst', 'edge_weight', 'L0_gnn_weight', 'L0_gnn_bias', 'L0_mix_Wq', 'L0_mix_Wk', 'L0_mix_Wv',
        'L0_mix_Wm', 'L0_mix_W1', 'L0_mix_W2', 'L0_mix_g1', 'L0_mix_b1', 'L0_mix_g2', 'L0_mix_b2', 'L0_ffn_Wr',
        'L0_ffn_br', 'L0_ffn_ln_g', 'L0_ffn_ln_b', 'L0_ffn_W1', 'L0_ffn_b1', 'L0_ffn_W2', 'L0_ffn_b2']


def kernel(**inputs):
    import numpy as _np
    import concourse.bacc as _bacc
    from concourse import mybir as _mybir
    from concourse.bass_utils import run_bass_kernel_spmd as _run

    nc = _bacc.Bacc("TRN2", target_bir_lowering=False, num_devices=1)
    arrays, args = {}, []
    for name in _INS:
        a = _np.ascontiguousarray(inputs[name])
        arrays[f"in_{name}_dram"] = a
        args.append(nc.dram_tensor(f"in_{name}_dram", a.shape, _mybir.dt.from_np(a.dtype), kind="ExternalInput").ap())
    out = nc.dram_tensor("out_0_dram", inputs["x"].shape, _mybir.dt.float32, kind="ExternalOutput").ap()
    gps_layer(nc, *args, out)
    r = _run(nc, [arrays], core_ids=[0])
    return r.results[0]["out_0_dram"]
```

```python
from contextlib import ExitStack

import concourse.bass as bass
from concourse import mybir

ALU = mybir.AluOpType
ACT = mybir.ActivationFunctionType
F32 = mybir.dt.float32
BF16 = mybir.dt.bfloat16
I32 = mybir.dt.int32
U32 = mybir.dt.uint32
AX_X = mybir.AxisListType.X
EPS = 1e-5
ATT_EPS = 1e-6
STD_EPS = 1e-4


class Steps:

    LEAD = 2

    def __init__(self, sem, names):
        self.sem, self.names, self.k = sem, names.split(), 0

    def first(self, engine):
        engine.sem_inc(self.sem, self.LEAD * len(self.names))

    def __call__(self, name):
        assert self.names[self.k % len(self.names)] == name, (self.names[self.k % len(self.names)], name)
        self.k += 1
        return self.sem, 1

    def done(self, turn, name):
        n = len(self.names)
        return self.sem, (turn + self.LEAD) * n + self.names.index(name) + 1


def gps_layer(nc, x, src, dst, edge_weight, gnn_W, gnn_b, Wq, Wk, Wv, Wm, W1, W2, g1, b1, g2, b2,
              Wr, br, ln_g, ln_b, eW1, eb1, eW2, eb2, out):
    N, F = x.shape
    E = src.shape[0]
    P = 128
    T = -(-N // P)
    TAIL = N - (T - 1) * P
    FC = F // P
    HID = W1.shape[1]
    HC = HID // P
    HEADS = 8
    HD = F // HEADS
    HPC = P // HD
    NE, _, EH = eW1.shape
    EHC = EH // P
    BLK = 256
    BM = BLK // P
    MAXBLK = 2 * N // BLK + NE
    REG = (-(-N // BLK) + 1) * BLK
    CH = -(-E // P)
    CB = -(-CH // P)
    U = 7
    NG = 5
    NACC = 4
    AROWS = -(-(N + P) // (2 * P)) * 2 * P
    EPAD = CH * P + U * P
    BIG = 2048
    PADDST = T * P - 1
    assert CH < BIG and FC == 2 and TAIL < P

    sums = [nc.dram_tensor(f"sums{k}", [AROWS, F], F32).ap() for k in range(NACC)]
    src_d = nc.dram_tensor("src_padded", [EPAD], I32).ap()
    dst_d = nc.dram_tensor("dst_padded", [EPAD], I32).ap()
    w_d = nc.dram_tensor("w_padded", [EPAD], F32).ap()
    erows = nc.dram_tensor("expert_rows", [NE * REG, F], F32).ap()
    eouts = nc.dram_tensor("expert_outs", [(MAXBLK + 1) * BLK, F], F32).ap()

    with ExitStack() as ctx:
        def sb(name, shape, dt=F32):
            return ctx.enter_context(nc.sbuf_tensor("sb_" + name, shape, dt))

        def ps(name, shape, dt=F32):
            return ctx.enter_context(nc.psum_tensor("ps_" + name, shape, dt))

        def sem(name):
            return ctx.enter_context(nc.semaphore(name))

        x1 = sb("x1", [P, T, F])
        ident = sb("ident", [P, P])
        ones = sb("ones", [P, P])
        tri = sb("tri", [P, P])
        bdmask = sb("bdmask", [P, HPC, HD])
        hmask = sb("hmask", [P, HPC])
        valid = sb("valid", [P, T])
        idrow = sb("idrow", [P, P])
        down8 = sb("down8", [P, NE])
        carry = sb("carry", [P, NE])
        ebase = sb("ebase", [P, NE])
        cidx = sb("cidx", [P, CB])
        cinv = sb("cinv", [P, CB])
        dummy = sb("dummy", [P, U])
        trilow = sb("trilow", [P, P])
        tlo = sb("tlo", [P, T])
        thi = sb("thi", [P, T])
        bidx = sb("bidx", [1, MAXBLK])
        PADP = 2
        assert (EPAD - E) % PADP == 0
        padi = sb("padi", [PADP, (EPAD - E) // PADP], I32)
        padz = sb("padz", [PADP, (EPAD - E) // PADP], I32)
        zrows = sb("zrows", [P, BM * F])
        wq = sb("wq", [P, FC, F])
        wkv = sb("wkv", [P, FC, 2 * F])
        wm = sb("wm", [P, FC, F])
        w1 = sb("w1", [P, 2 * FC, HID])
        w2 = sb("w2", [P, HC, F])
        wg = sb("wg", [P, FC, F])
        wgs = sb("wgs", [P, FC, F])
        wr = sb("wr", [P, FC, NE])
        PR = NE * EHC + 4 * FC + 2 * NE * FC - 2 * FC
        rows_p = sb("rows_p", [PR, P])
        colp = sb("colp", [P, PR])
        R_B1, R_G, R_B, R_G1, R_BB1 = 0, NE * EHC, NE * EHC + NE * FC, NE * EHC + 2 * NE * FC, NE * EHC + 2 * NE * FC + FC
        g2_bc = sb("g2_bc", [P, F])
        bias_bc = sb("bias_bc", [P, F])
        gb_bc = sb("gb_bc", [P, F])
        br_bc = sb("br_bc", [P, NE])
        xn = sb("xn", [P, T, F])
        bst = sb("bst", [P, T, 6])
        rmean = sb("rmean", [P, T])
        rvar = sb("rvar", [P, T])
        rtmp = sb("rtmp", [P, T])
        rrstd = sb("rrstd", [P, T])
        xs = sb("xs", [P, 2, F])
        xnT = sb("xnT", [P, 2, FC, P])
        kmin = sb("kmin", [P, 2, F])
        kexp = sb("kexp", [P, 2, F])
        kelu = sb("kelu", [P, 2, F])
        vaug = sb("vaug", [P, 2, FC, P + 1])
        cst = sb("cst", [P, FC, T, 6])
        cmv = sb("cmv", [P, FC, 2])
        cstd = sb("cstd", [P, FC])
        dmean = sb("dmean", [P, FC, P])
        mean_bc = sb("mean_bc", [P, F])
        kvbd = sb("kvbd", [P, FC, P + HPC])
        ring = sb("ring", [P, U * (F + P)])
        assert CB * P <= U * (F + P) and T * CB <= U * P
        dstc = ring[:, 0:CB * P].bitcast(I32).rearrange("p (b e) -> p b e", b=CB)
        msgs = ring[:, 0:U * F].rearrange("p (k f) -> p k f", k=U)
        coef = ring[:, U * F:U * (F + P)].rearrange("p (k q) -> p k q", k=U)
        cmax = sb("cmax", [P, CB])
        cmin = sb("cmin", [P, CB])
        vmax = sb("vmax", [P, 2 * T])
        vred = sb("vred", [2 * T, 1])
        brow = sb("brow", [1, 2 * T])
        bnd = sb("bnd", [1, 2, T], I32)
        bndf = sb("bndf", [1, 2, T])
        src_e = sb("src_e", [P, U], I32)
        dst_e = sb("dst_e", [P, U], I32)
        w_e = sb("w_e", [P, U])
        src_row = sb("src_row", [P, P * U], I32)
        srcf = sb("srcf", [P, U])
        dstf = sb("dstf", [P, U])
        reads = sb("reads", [P, U, P])
        same = sb("same", [P, U, P])
        indA, indB = (b[:].rearrange("p k e -> p (k e)")[:, 0:T * CB].rearrange("p (t b) -> p t b", t=T)
                      for b in (reads, same))
        before = sb("before", [P, U])
        junk = sb("junk", [P, U, P], BF16)
        away = sb("away", [P, U])
        idxf = sb("idxf", [P, U])
        idx_now = sb("idx_now", [P, U])
        idx = sb("idx", [P, U], I32)
        qmin = sb("qmin", [P, FC, P])
        qexp = sb("qexp", [P, FC, P])
        qelu = sb("qelu", [P, FC, P])
        rden = sb("rden", [P, FC, HPC])
        msg = sb("msg", [P, F])
        msgT = sb("msgT", [P, FC, P])
        lnst = sb("lnst", [P, 6])
        lnmv = sb("lnmv", [P, 2])
        lnve = sb("lnve", [P, 1])
        lnln = sb("lnln", [P, 1])
        lny = sb("lny", [P, 1])
        lna = sb("lna", [P, 1])
        lnr = sb("lnr", [P, 1])
        mrow = sb("mrow", [P, F])
        mT = sb("mT", [P, FC, P])
        hT = sb("hT", [P, HC, P])
        SLOTS = 4
        assert T % SLOTS == 1
        parts = xn[:].rearrange("p t f -> p (t f)")[:, 0:SLOTS * NACC * F].rearrange(
            "p (s k f) -> p s k f", s=SLOTS, k=NACC)
        aggT = sb("aggT", [P, 2, FC, P])
        xn2 = sb("xn2", [P, 2, F])
        TE = T * NE
        logits = sb("logits", [P, T, NE])
        hot = sb("hot", [P, 2, T, NE])
        hots = sb("hots", [P, T, NE])
        work = sb("work", [P, 2, T, NE])
        best = sb("best", [P, 2, T])
        which = sb("which", [P, T])
        wts = sb("wts", [P, T, 2])
        slotf = sb("slotf", [P, T, 2])
        slotc = sb("slotc", [P, T, 2])
        slot_now = sb("slot_now", [P, 2, 2], I32)
        lastcnt = sb("lastcnt", [P, NE])
        cnt = sb("cnt", [P, NE])
        cnti = sb("cnti", [P, NE], I32)
        nblk = sb("nblk", [P, NE])
        cum = sb("cum", [P, NE])
        delta = sb("delta", [P, NE])
        one8 = sb("one8", [P, NE])
        le, lenb = (b[0:1].rearrange("p s f -> p (s f)")[:, 0:MAXBLK * NE].rearrange("p (m e) -> p m e", e=NE)
                    for b in (kmin, kexp))
        be = sb("be", [1, MAXBLK])
        bprev = sb("bprev", [1, MAXBLK])
        bstart = sb("bstart", [1, MAXBLK])
        btab = sb("btab", [1, 2, MAXBLK], I32)
        ztab = sb("ztab", [1, NE + 1], I32)
        pA = ps("A", [P, 512])
        pT = ps("T", [P, 512])
        pQ = ps("Q", [P, 512])
        pM = ps("M", [P, 512])
        pH = ps("H", [P, 512])
        pY = ps("Y", [P, 512])
        pG = ps("G", [P, 512])
        pR = ps("R", [P, 512])

        pC, pX = (pA, pY), (pG, pR)
        consts_made = sem("consts_made")
        spacer = sem("spacer")
        pads_made = sem("pads_made")
        x_zeroed = sem("x_zeroed")
        x_loaded = sem("x_loaded")
        kv_weights = sem("kv_weights")
        weights = sem("weights")
        edges_padded = sem("edges_padded")
        chunks_zeroed = sem("chunks_zeroed")
        chunks_loaded = sem("chunks_loaded")
        prefix_kept = sem("prefix_kept")
        zero_made = sem("zero_made")
        sums_zeroed = sem("sums_zeroed")
        dve1 = Steps(sem("dve_norm"), "stats")
        dve2 = Steps(sem("dve_rstd"), "msum mean dif m2 dif2 dif4 var ve a nr y rstd")
        act2 = Steps(sem("act_rstd"), "ln exp")
        PT = Steps(sem("pe_trans"), "trans")
        PK = Steps(sem("pe_kv"), "kv")
        PKA = Steps(sem("pe_kvacc"), "kvacc")
        DN = Steps(sem("dve_rows"), "norm")
        DS = Steps(sem("dve_colstats"), "cstat0 cstat1")
        DK = Steps(sem("dve_kv"), "kmin kelu")
        GK = Steps(sem("pool_kv"), "keep res")
        AX = Steps(sem("act_xnT"), "xnT")
        AK = Steps(sem("act_kv"), "kexp vcopy")
        dve3 = Steps(sem("dve_cols"), "aggr0 aggr1 std inv wgs0 wgs1 dm0 dm1 meanbc "
                                      "kv0 kv1 ks0 ks1 gb")
        cen_made = sem("rows_centred")
        act3 = Steps(sem("act_cols"), "sqrt")
        pe3 = Steps(sem("pe_cols"), "params mean")
        ccopy = sem("params_copied")
        dveb = Steps(sem("dve_span"), "cmax cmin indA indB ind vhi vmaxhi vlo vmaxlo vred row "
                                      "hi1 lo1 hi2 lo2 n1 n2 mul elo ielo in shr min")
        peb = Steps(sem("pe_span"), "t1 t2")
        row_loaded = sem("row_loaded")
        ends_loaded = sem("ends_loaded")
        floats_made = sem("floats_made")
        same_made = sem("same_made")
        reads_made = sem("reads_made")
        counted = sem("counted")
        idx_float = sem("idx_float")
        idx_taken = sem("idx_taken")
        idx_ready = sem("idx_ready")
        coef_done = sem("coef_done")
        coef_copied = sem("coef_copied")
        NPAIR = (U + 1) // 2
        msg_done = sem("msg_done")
        msg_copied = sem("msg_copied")
        HALVES = (range(0, 4), range(4, U))
        PAIRS = [range(2 * j, min(2 * j + 2, U)) for j in range(NPAIR)]
        landed = sem("landed")
        copy_of = [k % NACC for k in range(U)]
        last_to = [max(b for b in range(-U, k) if copy_of[b % U] == copy_of[k]) for k in range(U)]
        upto = [max(last_to[0:k + 1] + [last_to[-1] - U]) for k in range(U)]
        waits_of = [range((upto[k - 1] if k else last_to[-1] - U) + 1, upto[k] + 1) for k in range(U)]
        assert sum(len(w) for w in waits_of) == U
        scattered = [sem(f"scattered{k}") for k in range(U)]
        LN = "st ag ve a nr r ap"
        ln = lambda p: " ".join(p + s for s in LN.split())
        PM = Steps(sem("pe_mixer"), "xT q num msgT mm mT hid h2")
        DM = Steps(sem("dve_mixer"), "idrow xs qmin qelu eps rden msg " + ln("m") + " " + ln("h") + " g2 b2 res")
        AM = Steps(sem("act_mixer"), "xT qexp msgT mln mexp mT0 mT1 relu hln hexp")
        parts_loaded = [sem(f"parts_loaded{s}") for s in range(SLOTS)]
        DA = Steps(sem("dve_gnn_add"), "add")
        PG = Steps(sem("pe_gnnT"), "aggT")
        PG2 = Steps(sem("pe_gnn"), "gnn")
        AG = Steps(sem("act_gnn"), "aggT")
        DG = Steps(sem("dve_gnn"), "res stats")
        RS = "msum mean dif m2 dif2 dif4 var ve a nr y rstd"
        dveo, acto = Steps(sem("dve_rstd_o"), RS), Steps(sem("act_rstd_o"), "ln exp")
        dvei, acti = Steps(sem("dve_rstd_i"), RS), Steps(sem("act_rstd_i"), "ln exp")
        DR = Steps(sem("dve_router"), "xt stats")
        GR = Steps(sem("pool_router"), "keep")
        PR_ = Steps(sem("pe_router"), "xT log")
        AR = Steps(sem("act_router"), "xT log")
        dver = Steps(sem("dve_top2"), "br b0 e0 r0 w0 h0 p0 l1 b1 e1 r1 w1 h1 dif den wa wb v0 v1 sum tot "
                     "s1 s2 s4 s8 s16 s32 sub rank base p0x s0x p1x s1x last")
        actr = Steps(sem("act_top2"), "exp")
        per = Steps(sem("pe_rank"), "rank tot")
        DD = Steps(sem("dve_dispatch"), "xn2 slot")
        dispatched = [sem("dispatched0"), sem("dispatched1")]
        dve5 = Steps(sem("dve_blocks"), "cnt c255 ci sh nb cum le lenb be bprev st1 st2 itab ibe izt inb")
        dve6 = Steps(sem("dve_slots"), "excl rows delta hot0 hot1 shift slot")
        all_scattered = sem("all_scattered")
        zero_rows = sem("zero_rows")
        zero_outs = sem("zero_outs")
        outs_zeroed = sem("outs_zeroed")
        ew1_loaded = sem("ew1_loaded")
        ew2_loaded = sem("ew2_loaded")
        eb2_loaded = sem("eb2_loaded")
        xb_loaded = sem("xb_loaded")
        PE_ = Steps(sem("pe_experts"), "t0 t1 " + " ".join(f"h{j}" for j in range(EHC)) + " y0 y1")
        DE = Steps(sem("dve_experts"), "x0 x1 y0 y1")
        AE = Steps(sem("act_experts"), " ".join(f"g{j}" for j in range(EHC)))
        out_rows = sem("out_rows")
        DI = Steps(sem("dve_out_idx"), "idx")
        DC = Steps(sem("dve_combine"), "a b")
        got = [[sem(f"got{s}{j}") for j in range(2)] for s in range(SLOTS)]
        stored = [sem(f"stored{s}") for s in range(SLOTS)]

        xn_flat, used = xn[:].rearrange("p t f -> p (t f)"), [0]

        def over_xn(n):
            used[0] += n
            assert used[0] <= T * F
            return xn_flat[:, used[0] - n:used[0]]

        ew1 = over_xn(FC * EH).rearrange("p (c h) -> p c h", c=FC)
        ew2 = over_xn(EHC * F).rearrange("p (j f) -> p j f", j=EHC)
        ehT = over_xn(EHC * BLK).rearrange("p (j q) -> p j q", j=EHC)
        xeT = over_xn(FC * BLK).rearrange("p (c q) -> p c q", c=FC)
        xb = over_xn(BM * F).rearrange("p (m f) -> p m f", m=BM)
        yb = over_xn(BM * F).rearrange("p (m f) -> p m f", m=BM)
        eb2_bc = over_xn(F)
        yg = over_xn(SLOTS * 2 * F).rearrange("p (s j f) -> p s j f", s=SLOTS, j=2)
        idx_c = sb("idx_c", [P, SLOTS, 2], I32)
        ob = over_xn(SLOTS * F).rearrange("p (s f) -> p s f", s=SLOTS)

        def apart(engine):
            engine.sem_inc(spacer, 1)

        def tile(buf, t):
            return buf[:, t, :] if isinstance(t, int) else buf[:, bass.ds(t, 1), :]

        def col(buf, t):
            return buf[:, t:t + 1] if isinstance(t, int) else buf[:, bass.ds(t, 1)]

        block = ctx.enter_context(nc.Block())
        XCH = 12
        nxc = (T - 1) // XCH
        assert nxc * XCH == T - 1

        @block.sync
        def _(sp):
            xr = x[0:(T - 1) * P, :].rearrange("(t p) f -> p t f", p=P)
            for k in range(nxc):
                sp.dma_start(x1[:, k * XCH:(k + 1) * XCH, :], xr[:, k * XCH:(k + 1) * XCH, :]).then_inc(x_loaded, 16)
            sp.wait_ge(x_zeroed, 1)
            sp.dma_start(x1[0:TAIL, T - 1, :], x[(T - 1) * P:N, :]).then_inc(x_loaded, 16)
            sp.dma_start(wkv[:, :, 0:F], Wk.rearrange("(c p) n -> p c n", p=P)).then_inc(kv_weights, 16)
            sp.dma_start(wkv[:, :, F:2 * F], Wv.rearrange("(c p) n -> p c n", p=P)).then_inc(kv_weights, 16)
            g = 15
            for d, s in ((src_d, src), (dst_d, dst), (w_d, edge_weight)):
                sp.dma_start(d[0:E].rearrange("(g e) -> g e", g=g), s.rearrange("(g e) -> g e", g=g)).then_inc(edges_padded, 16)
            sp.wait_ge(pads_made, 2)
            for d, b in ((src_d, padz[:]), (dst_d, padi[:]), (w_d, padz[:].bitcast(F32))):
                sp.dma_start(d[E:EPAD].rearrange("(p e) -> p e", p=PADP), b).then_inc(edges_padded, 16)
            for b, w in ((wq, Wq), (wm, Wm), (w1, W1), (w2, W2), (wg, gnn_W), (wr, Wr)):
                sp.dma_start(b[:], w.rearrange("(c p) n -> p c n", p=P)).then_inc(weights, 16)
            sp.dma_start(rows_p[R_B1:R_G, :], eb1.rearrange("e (j p) -> (e j) p", p=P)).then_inc(weights, 16)
            sp.dma_start(rows_p[R_G:R_B, :], ln_g.rearrange("e (j p) -> (e j) p", p=P)).then_inc(weights, 16)
            sp.dma_start(rows_p[R_B:R_G1, :], ln_b.rearrange("e (j p) -> (e j) p", p=P)).then_inc(weights, 16)
            sp.dma_start(rows_p[R_G1:R_BB1, :], g1.rearrange("(j p) -> j p", p=P)).then_inc(weights, 16)
            sp.dma_start(rows_p[R_BB1:PR, :], b1.rearrange("(j p) -> j p", p=P)).then_inc(weights, 16)
            for b, v in ((g2_bc, g2), (bias_bc, b2), (gb_bc, gnn_b), (br_bc, br)):
                sp.dma_start(b[:], v.partition_broadcast(P)).then_inc(weights, 16)
            sp.wait_ge(edges_padded, 6 * 16)
            sp.wait_ge(chunks_zeroed, 1)
            full = CH // P
            sp.dma_start(dstc[:, 0:full, :], dst_d[0:full * P * P].rearrange("(b p e) -> p b e", p=P, e=P)).then_inc(chunks_loaded, 16)
            sp.dma_start(dstc[0:CH - full * P, full, :],
                         dst_d[full * P * P:CH * P].rearrange("(p e) -> p e", e=P)).then_inc(chunks_loaded, 16)
            sp.wait_ge(zero_made, 1)
            for a in sums:
                n2 = AROWS // (2 * P)
                sp.dma_start(a.rearrange("(p j m) f -> p j (m f)", p=P, m=2),
                             zrows[:].unsqueeze(1).to_broadcast([P, n2, 2 * F])).then_inc(sums_zeroed, 16)
            sp.wait_ge(*dveb.done(0, "min"))
            groups = sp.alloc_register("sp_groups")
            first_edge = sp.alloc_register("sp_first_edge")
            sp.reg_mov(groups, 0)
            with sp.Fori(0, T) as t:
                e0 = sp.value_load(bnd[0:1, 0, bass.ds(t, 1)], min_val=0, max_val=CH * P)
                n = sp.value_load(bnd[0:1, 1, bass.ds(t, 1)], min_val=NG, max_val=-(-CH // U))
                sp.reg_mov(first_edge, e0)
                g0 = sp.snap(groups)
                with sp.Fori(0, n) as i:
                    eg = sp.snap(first_edge, min_val=0, max_val=EPAD - U * P)
                    at = bass.ds(eg, U * P)
                    sp.wait_ge(same_made, (g0 + i) * U + 1)
                    apart(sp)
                    sp.dma_start(src_row[:], src_d[at].partition_broadcast(P)).then_inc(row_loaded, 16)
                    sp.wait_ge(reads_made, (g0 + i) * U + 1)
                    apart(sp)
                    for b, d in ((src_e, src_d), (dst_e, dst_d), (w_e, w_d)):
                        sp.dma_start(b[:], d[at].rearrange("(p k) -> p k", k=U)).then_inc(ends_loaded, 16)
                    sp.reg_add(first_edge, first_edge, U * P)
                sp.reg_add(groups, groups, n)
            sp.wait_ge(all_scattered, 1)
            def load_parts(t, s):
                for k in range(NACC):
                    rows = bass.ds(t * P, P) if not isinstance(t, int) else slice(t * P, (t + 1) * P)
                    sp.dma_start(parts[:, s, k, :], sums[k][rows, :]).then_inc(parts_loaded[s], 16)

            for s in range(SLOTS):
                load_parts(s, s)
            with sp.Fori(1, T // SLOTS) as i:
                for s in range(SLOTS):
                    sp.wait_ge(*PG.done(SLOTS * (i - 1) + s, "aggT"))
                    load_parts(SLOTS * i + s, s)
            sp.wait_ge(*PG.done(T - 1 - SLOTS, "aggT"))
            load_parts(T - 1, 0)
            sp.wait_ge(*dve5.done(0, "inb"))
            sp.wait_ge(dispatched[0], 2 * 16 * (T // 2 + 1))
            sp.wait_ge(dispatched[1], 2 * 16 * (T // 2))
            for e in range(NE):
                z0 = sp.value_load(ztab[0:1, e:e + 1], min_val=0, max_val=NE * REG - BLK)
                sp.dma_start(erows[bass.ds(z0, BLK), :].rearrange("(p m) f -> p (m f)", m=BM), zrows[:]).then_inc(zero_rows, 16)
            sp.wait_ge(zero_rows, NE * 16)
            nb = sp.value_load(ztab[0:1, NE:NE + 1], min_val=1, max_val=MAXBLK)
            with sp.Fori(0, nb) as b:
                r0 = sp.value_load(btab[0:1, 0, bass.ds(b, 1)], min_val=0, max_val=NE * REG - BLK)
                e = sp.value_load(btab[0:1, 1, bass.ds(b, 1)], min_val=0, max_val=NE - 1)
                sp.wait_ge(*PE_.done(b - 1, "t1"))
                sp.dma_start(xb[:], erows[bass.ds(r0, BLK), :].rearrange("(m p) f -> p m f", p=P)).then_inc(xb_loaded, 16)
                sp.wait_ge(*PE_.done(b - 1, f"h{EHC - 1}"))
                sp.dma_start(ew1[:], eW1[bass.ds(e, 1)].rearrange("e (c p) h -> p (e c) h", p=P)).then_inc(ew1_loaded, 16)
                sp.wait_ge(*DE.done(b - 1, "y1"))
                sp.dma_start(ew2[:], eW2[bass.ds(e, 1)].rearrange("e (j p) f -> p (e j) f", p=P)).then_inc(ew2_loaded, 16)
                sp.dma_start(eb2_bc[:], eb2[bass.ds(e, 1), :].rearrange("e f -> (e f)").partition_broadcast(P)).then_inc(eb2_loaded, 16)
            zeroed = sp.alloc_register("sp_zeroed")
            sp.reg_mov(zeroed, 0)
            with sp.Fori(nb, MAXBLK + 1) as b:
                sp.reg_add(zeroed, zeroed, 16)
                sp.dma_start(eouts[bass.ds(b * BLK, BLK), :].rearrange("(p m) f -> p (m f)", m=BM), zrows[:]).then_inc(zero_outs, 16)
            sp.wait_ge(zero_outs, sp.snap(zeroed, min_val=16, max_val=16 * (MAXBLK + 1)))
            sp.sem_inc(outs_zeroed, 1)
            with sp.Fori(0, T // SLOTS) as i:
                for s in range(SLOTS):
                    sp.wait_ge(*DC.done(SLOTS * i + s, "b"))
                    sp.dma_start(out[bass.ds((SLOTS * i + s) * P, P), :], ob[:, s]).then_inc(stored[s], 16)
            sp.wait_ge(*DC.done(T - 1, "b"))
            sp.dma_start(out[(T - 1) * P:N, :], ob[0:TAIL, 0]).then_inc(stored[0], 16)
            for s in range(SLOTS):
                sp.wait_ge(stored[s], 16 * (T // SLOTS + (s == 0)) + 1)

        @block.gpsimd
        def _(pool):
            g = nc.gpsimd
            chain = sem("pool_chain")
            made = [0]

            def link(ins):
                made[0] += 1
                ins.then_inc(chain, 1)
                pool.wait_ge(chain, made[0])

            pool.sem_inc(landed, 2 * U)
            g.memset(x1[:, T - 1, :], 0.0).then_inc(x_zeroed, 1)
            g.memset(padz[:], 0).then_inc(pads_made, 1)
            g.memset(padi[:], PADDST).then_inc(pads_made, 1)
            g.memset(dstc[:, CB - 1, :], PADDST).then_inc(chunks_zeroed, 1)
            link(g.memset(ident[:], 0.0))
            link(g.affine_select(out=ident[:], in_=ident[:], compare_op=ALU.not_equal, fill=1.0, base=0,
                                 pattern=[[-1, P]], channel_multiplier=1))
            link(g.memset(tri[:], 0.0))
            link(g.affine_select(out=tri[:], in_=tri[:], compare_op=ALU.is_ge, fill=1.0, base=0,
                                 pattern=[[-1, P]], channel_multiplier=1))
            link(g.memset(hmask[:], 1.0))
            link(g.affine_select(out=hmask[:], in_=hmask[:], compare_op=ALU.is_ge, fill=0.0, base=0,
                                 pattern=[[-HD, HPC]], channel_multiplier=1))
            link(g.affine_select(out=hmask[:], in_=hmask[:], compare_op=ALU.is_ge, fill=0.0, base=HD - 1,
                                 pattern=[[HD, HPC]], channel_multiplier=-1))
            link(g.memset(bdmask[:], 1.0))
            link(g.affine_select(out=bdmask[:], in_=bdmask[:], compare_op=ALU.is_ge, fill=0.0, base=0,
                                 pattern=[[-HD, HPC], [0, HD]], channel_multiplier=1))
            link(g.affine_select(out=bdmask[:], in_=bdmask[:], compare_op=ALU.is_ge, fill=0.0, base=HD - 1,
                                 pattern=[[HD, HPC], [0, HD]], channel_multiplier=-1))
            link(g.memset(valid[:], 1.0))
            link(g.affine_select(out=valid[:], in_=valid[:], compare_op=ALU.is_ge, fill=0.0, base=N - 1,
                                 pattern=[[-P, T]], channel_multiplier=-1))
            g.memset(ones[:], 1.0)
            g.memset(zrows[:], 0.0).then_inc(zero_made, 1)
            link(g.memset(trilow[:], 0.0))
            link(g.affine_select(out=trilow[:], in_=trilow[:], compare_op=ALU.is_ge, fill=1.0, base=0,
                                 pattern=[[1, P]], channel_multiplier=-1))
            g.memset(one8[:], 1.0)
            io = dict(allow_small_or_imprecise_dtypes=True)
            g.iota(idrow[:], [[1, P]], base=-P, channel_multiplier=0, **io)
            g.iota(down8[:], [[-1, NE]], base=NE, channel_multiplier=0, **io)
            g.iota(ebase[:], [[REG, NE]], base=0, channel_multiplier=0, **io)
            g.iota(dummy[:], [[0, U]], base=N, channel_multiplier=1, **io)
            g.iota(cidx[:], [[P, CB]], base=1, channel_multiplier=1, **io)
            g.iota(cinv[:], [[-P, CB]], base=BIG, channel_multiplier=-1, **io)
            g.iota(tlo[:], [[P, T]], base=0, channel_multiplier=0, **io)
            g.iota(thi[:], [[P, T]], base=P - 1, channel_multiplier=0, **io)
            g.iota(bidx[:], [[1, MAXBLK]], base=0, channel_multiplier=0, **io).then_inc(consts_made, 1)

            GK.first(pool)

            def kv_tile(t, s):
                flat = (lambda z: z) if isinstance(t, int) else (lambda z: z.rearrange("p a f -> p (a f)"))
                pool.wait_ge(*DN.done(t, "norm"))
                g.tensor_copy(flat(tile(xn, t)), xs[:, s, :]).then_inc(*GK("keep"))
                g.tensor_tensor(flat(tile(x1, t)), flat(tile(x1, t)), xs[:, s, :], ALU.add).then_inc(*GK("res"))

            with pool.Fori(0, T // 2) as i:
                for s in range(2):
                    kv_tile(2 * i + s, s)
            kv_tile(T - 1, 0)

            pool.wait_ge(sums_zeroed, 16 * NACC)
            pool.wait_ge(*dveb.done(0, "min"))
            total = pool.alloc_register("pool_total")
            pool.reg_mov(total, 0)
            with pool.Fori(0, T) as t:
                pool.reg_add(total, total, pool.value_load(bnd[0:1, 1, bass.ds(t, 1)], min_val=NG, max_val=-(-CH // U)))

            def scatter(i, first=False):
                for k in range(U):
                    for b in waits_of[k]:
                        if b >= 0:
                            pool.wait_ge(scattered[b], i * 16 + 16)
                        elif not first:
                            pool.wait_ge(scattered[b + U], i * 16)
                        else:
                            continue
                        pool.sem_inc(landed, 1)
                    if k % 2 == 0:
                        pool.wait_ge(idx_ready, i * NPAIR + k // 2 + 2)
                        apart(pool)
                        pool.wait_ge(msg_copied, i * NPAIR + NPAIR + k // 2 + 1)
                        apart(pool)
                    g.indirect_dma_start(sums[copy_of[k]], bass.IndirectOffsetOnAxis(ap=idx[:, k:k + 1], axis=0),
                                         msgs[:, k, :], None, compute_op=ALU.add).then_inc(scattered[k], 16)

            scatter(0, first=True)
            with pool.Fori(1, pool.snap(total, min_val=NG * T, max_val=T * -(-CH // U))) as i:
                scatter(i)
            for k in range(U):
                pool.wait_ge(scattered[k], pool.snap(total, min_val=NG * T, max_val=T * -(-CH // U)) * 16)
                apart(pool)
            pool.sem_inc(all_scattered, 1)
            GR.first(pool)

            def keep(t, s):
                pool.wait_ge(*DR.done(t, "xt"))
                g.tensor_copy(tile(xn, t) if isinstance(t, int) else tile(xn, t).rearrange("p a f -> p (a f)"),
                              xs[:, s, :]).then_inc(*GR("keep"))

            with pool.Fori(0, T // 2) as i:
                for s in range(2):
                    keep(2 * i + s, s)
            keep(T - 1, 0)

            def dispatch(t, s, rows):
                pool.wait_ge(*DD.done(t, "slot"))
                apart(pool)
                for j in range(2):
                    g.indirect_dma_start(
                        erows, bass.IndirectOffsetOnAxis(ap=slot_now[0:rows, s, j:j + 1], axis=0),
                        xn2[0:rows, s, :], None).then_inc(dispatched[s], 16)

            with pool.Fori(0, T // 2) as i:
                for s in range(2):
                    dispatch(2 * i + s, s, P)
            dispatch(T - 1, 0, TAIL)

            pool.wait_ge(*dve5.done(0, "inb"))
            nb = pool.value_load(ztab[0:1, NE:NE + 1], min_val=1, max_val=MAXBLK)
            pool.wait_ge(outs_zeroed, 1)
            pool.wait_ge(out_rows, nb * 16 + 1)
            apart(pool)

            def fetch(t, s, rows):
                pool.wait_ge(*DI.done(t, "idx"))
                apart(pool)
                for j in range(2):
                    g.indirect_dma_start(
                        yg[0:rows, s, j, :], None, eouts,
                        bass.IndirectOffsetOnAxis(ap=idx_c[0:rows, s, j:j + 1], axis=0)).then_inc(got[s][j], 16)

            with pool.Fori(0, T // SLOTS) as i:
                for s in range(SLOTS):
                    fetch(SLOTS * i + s, s, P)
            fetch(T - 1, 0, TAIL)

        @block.tensor
        def _(pe):
            for st in (PT, PK, PKA, pe3, PM, PE_, peb, PG, PG2, PR_, per):
                st.first(pe)
            mm = nc.tensor.matmul
            pe.sem_inc(coef_done, 2)
            pe.sem_inc(msg_done, NPAIR)
            pe.wait_ge(consts_made, 1)
            pe.wait_ge(kv_weights, 32)

            def turn_rows(t, s):
                pe.wait_ge(*DN.done(t, "norm"))
                pe.wait_ge(*AX.done(t - 2, "xnT"))
                pe.wait_ge(*DS.done(t - 2, "cstat1"))
                for c in range(FC):
                    last_ = nc.tensor.transpose((pT, pA)[s][:, c * P:(c + 1) * P], xs[:, s, c * P:(c + 1) * P], ident[:])
                last_.then_inc(*PT("trans"))

            def project(t, s):
                pe.wait_ge(*AX.done(t, "xnT"))
                pe.wait_ge(*AK.done(t - 2, "vcopy"))
                pe.wait_ge(*DK.done(t - 2, "kelu"))
                for c in range(FC):
                    last_ = mm((pQ, pM)[s][:], xnT[:, s, c, :], wkv[:, c, :], start=(c == 0), stop=(c == FC - 1))
                last_.then_inc(*PK("kv"))

            def accumulate(t, s, first=False, last=False):
                pe.wait_ge(*DK.done(t, "kelu"))
                pe.wait_ge(*AK.done(t, "vcopy"))
                for c in range(FC):
                    last_ = mm((pG, pH)[c][:, 0:P + 1], kelu[:, s, c * P:(c + 1) * P], vaug[:, s, c, :],
                               start=first, stop=last)
                last_.then_inc(*PKA("kvacc"))

            turn_rows(0, 0)
            turn_rows(1, 1)
            project(0, 0)
            turn_rows(2, 0)
            project(1, 1)
            accumulate(0, 0, first=True)
            with pe.Fori(0, (T - 3) // 2) as i:
                for s in range(2):
                    turn_rows(2 * i + s + 3, 1 - s)
                    project(2 * i + s + 2, s)
                    accumulate(2 * i + s + 1, 1 - s)
            project(T - 1, 0)
            accumulate(T - 2, 1)
            accumulate(T - 1, 0, last=True)

            pe.wait_ge(weights, 16 * 15)
            nc.tensor.transpose(pR[:, 0:PR], rows_p[:], ident[0:PR, 0:PR]).then_inc(*pe3("params"))
            pe.wait_ge(*dve3.done(0, "dm1"))
            for c in range(FC):
                last_ = mm(pY[:, c * P:(c + 1) * P], ones[:], dmean[:, c, :], start=True, stop=True)
            last_.then_inc(*pe3("mean"))
            pe.wait_ge(*dveb.done(0, "vmaxlo"))
            nc.tensor.transpose(pA[0:2 * T, 0:P], vmax[:], ident[:]).then_inc(*peb("t1"))
            pe.wait_ge(*dveb.done(0, "vred"))
            nc.tensor.transpose(pA[0:1, 256:256 + 2 * T], vred[:], ident[0:2 * T, 0:2 * T]).then_inc(*peb("t2"))

            pe.wait_ge(*dveb.done(0, "min"))
            pe.wait_ge(*dve3.done(0, "gb"))
            pe.wait_ge(ccopy, 1)
            groups = pe.alloc_register("pe_groups")
            pe.reg_mov(groups, 0)
            W_ = P + HPC

            def turn(src_, step):
                for c in range(FC):
                    last_ = nc.tensor.transpose(pT[:, c * P:(c + 1) * P], src_[:, c * P:(c + 1) * P], ident[:])
                last_.then_inc(*PM(step))

            def step_xT(t):
                pe.wait_ge(*DM.done(t, "xs"))
                pe.wait_ge(*AM.done(t - 1, "mT1"))
                turn(xs[:, 0, :], "xT")

            def step_q(t):
                pe.wait_ge(*AM.done(t, "xT"))
                pe.wait_ge(*DM.done(t - 1, "hap"))
                for o in range(FC):
                    for c in range(FC):
                        last_ = mm(pQ[:, o * P:(o + 1) * P], wq[:, c, o * P:(o + 1) * P], xnT[:, 0, c, :],
                                   start=(c == 0), stop=(c == FC - 1))
                last_.then_inc(*PM("q"))

            def step_num(t):
                pe.wait_ge(*DM.done(t, "qelu"))
                for c in range(FC):
                    last_ = mm(pM[:, c * W_:(c + 1) * W_], qelu[:, c, :], kvbd[:, c, :], start=True, stop=True)
                last_.then_inc(*PM("num"))

            def step_msgT(t):
                pe.wait_ge(*DM.done(t, "msg"))
                turn(msg[:], "msgT")

            def step_mm(t):
                pe.wait_ge(*AM.done(t, "msgT"))
                for c in range(FC):
                    last_ = mm(pQ[:, 0:F], msgT[:, c, :], wm[:, c, :], start=(c == 0), stop=(c == FC - 1))
                last_.then_inc(*PM("mm"))

            def step_mT(t):
                pe.wait_ge(*DM.done(t, "map"))
                turn(mrow[:], "mT")

            def step_hid(t):
                pe.wait_ge(*AM.done(t, "mT1"))
                for o in range(HC):
                    for c in range(2 * FC):
                        r = xnT[:, 0, c, :] if c < FC else mT[:, c - FC, :]
                        last_ = mm(pH[:, o * P:(o + 1) * P], w1[:, c, o * P:(o + 1) * P], r,
                                   start=(c == 0), stop=(c == 2 * FC - 1))
                last_.then_inc(*PM("hid"))

            def step_h2(t):
                pe.wait_ge(*AM.done(t, "relu"))
                for c in range(HC):
                    last_ = mm(pQ[:, 0:F], hT[:, c, :], w2[:, c, :], start=(c == 0), stop=(c == HC - 1))
                last_.then_inc(*PM("h2"))

            def coefs(g, half):
                ks = HALVES[half]
                if half == 0:
                    pe.wait_ge(same_made, g * U + U + 1)
                pe.wait_ge(reads_made, g * U + ks[-1] + 2)
                pe.wait_ge(coef_copied, g * 2 + half + 1)
                for k in ks:
                    last_ = mm(pC[half][:, (k - ks[0]) * P:(k - ks[0] + 1) * P], reads[:, k, :], same[:, k, :],
                               start=True, stop=True)
                last_.then_inc(coef_done, 1)

            def messages(begun, t, half):
                pe.wait_ge(coef_copied, begun * 2 + half + 1)
                for j in (2 * half, 2 * half + 1):
                    pe.wait_ge(msg_copied, begun * NPAIR + j - 1)
                    for k in PAIRS[j]:
                        last_ = mm(pX[j % 2][:, (k % 2) * F:(k % 2 + 1) * F], coef[:, k, :],
                                   tile(xn, t).rearrange("p a f -> p (a f)"), start=True, stop=True)
                    last_.then_inc(msg_done, 1)

            before_coefs = [step_xT, step_num, step_msgT, step_mT, step_h2]
            before_msgs = [step_q, None, step_mm, step_hid, None]
            prev = pe.alloc_register("pe_prev_tile")
            pe.reg_mov(prev, 0)
            with pe.Fori(0, T) as t:
                n = pe.value_load(bnd[0:1, 1, bass.ds(t, 1)], min_val=NG, max_val=-(-CH // U))
                g0 = pe.snap(groups)
                for i in range(NG):
                    before_coefs[i](t)
                    coefs(g0 + i, 0)
                    if i:
                        messages(g0 + i, t, 1)
                    else:
                        with pe.If(t > 0):
                            messages(g0, pe.snap(prev, min_val=0, max_val=T - 1), 1)
                    coefs(g0 + i, 1)
                    if before_msgs[i]:
                        before_msgs[i](t)
                    messages(g0 + (i + 1), t, 0)
                with pe.If(n > NG):
                    with pe.Fori(NG, n) as i:
                        coefs(g0 + i, 0)
                        messages(g0 + i, t, 1)
                        coefs(g0 + i, 1)
                        messages(g0 + i + 1, t, 0)
                pe.reg_add(groups, groups, n)
                pe.reg_mov(prev, t)
            messages(pe.snap(groups), pe.snap(prev, min_val=0, max_val=T - 1), 1)

            pe.wait_ge(*DM.done(T - 1, "res"))
            HALF = NACC // 2

            def gnn_T(t, s):
                pe.wait_ge(*DA.done(t, "add"))
                pe.wait_ge(*AG.done(t - 2, "aggT"))
                for c in range(FC):
                    for k in range(HALF):
                        last_ = mm((pT, pQ)[s % 2][:, c * P:(c + 1) * P], parts[:, s, k, c * P:(c + 1) * P], ident[:],
                                   start=(k == 0), stop=(k == HALF - 1))
                last_.then_inc(*PG("aggT"))

            def gnn_W_(t, s):
                pe.wait_ge(*AG.done(t, "aggT"))
                pe.wait_ge(*DG.done(t - 2, "res"))
                for c in range(FC):
                    last_ = mm((pM, pH)[s % 2][:, 0:F], aggT[:, s % 2, c, :], wgs[:, c, :], start=(c == 0), stop=(c == FC - 1))
                last_.then_inc(*PG2("gnn"))

            gnn_T(0, 0)
            with pe.Fori(0, T // SLOTS) as i:
                for s in range(SLOTS):
                    if s < SLOTS - 1:
                        gnn_T(SLOTS * i + s + 1, s + 1)
                    else:
                        gnn_T(SLOTS * i + SLOTS, 0)
                    gnn_W_(SLOTS * i + s, s)
            gnn_W_(T - 1, 0)

            def route(t, s):
                pe.wait_ge(*DR.done(t, "xt"))
                pe.wait_ge(*AR.done(t - 2, "xT"))
                for c in range(FC):
                    last_ = nc.tensor.transpose((pT, pQ)[s][:, c * P:(c + 1) * P], xs[:, s, c * P:(c + 1) * P], ident[:])
                last_.then_inc(*PR_("xT"))
                pe.wait_ge(*AR.done(t, "xT"))
                pe.wait_ge(*AR.done(t - 2, "log"))
                for c in range(FC):
                    last_ = mm((pM, pH)[s][:, 0:NE], aggT[:, s, c, :], wr[:, c, :], start=(c == 0), stop=(c == FC - 1))
                last_.then_inc(*PR_("log"))

            with pe.Fori(0, T // 2) as i:
                for s in range(2):
                    route(2 * i + s, s)
            route(T - 1, 0)
            pe.wait_ge(*dver.done(0, "sum"))
            mm(pA[:, 0:TE], tri[:], hots[:].rearrange("p t e -> p (t e)"), start=True, stop=True).then_inc(*per("rank"))
            mm(pY[:, 0:TE], ones[:], hots[:].rearrange("p t e -> p (t e)"), start=True, stop=True).then_inc(*per("tot"))

            pe.wait_ge(*dve5.done(0, "inb"))
            nb = pe.value_load(ztab[0:1, NE:NE + 1], min_val=1, max_val=MAXBLK)
            with pe.Fori(0, nb) as b:
                pe.wait_ge(xb_loaded, 16 * b + 16)
                for c in range(FC):
                    pe.wait_ge(*DE.done(b - 1, f"x{c}"))
                    for m in range(BM):
                        last_ = nc.tensor.transpose((pT, pR)[c][:, m * P:(m + 1) * P], xb[:, m, c * P:(c + 1) * P], ident[:])
                    last_.then_inc(*PE_(f"t{c}"))
                pe.wait_ge(ew1_loaded, 16 * b + 16)
                pe.wait_ge(*DE.done(b, "x1"))
                for j in range(EHC):
                    if j >= 4:
                        pe.wait_ge(*AE.done(b, f"g{j - 4}"))
                    else:
                        pe.wait_ge(*AE.done(b - 1, f"g{j + 4}"))
                    for c in range(FC):
                        last_ = mm((pA, pQ, pM, pH)[j % 4][:, 0:BLK], ew1[:, c, j * P:(j + 1) * P], xeT[:, c, :],
                                   start=(c == 0), stop=(c == FC - 1))
                    last_.then_inc(*PE_(f"h{j}"))
                pe.wait_ge(ew2_loaded, 16 * b + 16)
                for m in range(BM):
                    pe.wait_ge(*DE.done(b - 1, f"y{m}"))
                    for j in range(EHC):
                        if m == 0:
                            pe.wait_ge(*AE.done(b, f"g{j}"))
                        last_ = mm((pY, pG)[m][:, 0:F], ehT[:, j, m * P:(m + 1) * P], ew2[:, j, :],
                                   start=(j == 0), stop=(j == EHC - 1))
                    last_.then_inc(*PE_(f"y{m}"))

        @block.scalar
        def _(act):
            a = nc.scalar.activation
            for st in (act2, AX, AK, act3, AM, AE, AG, AR, acto, acti, actr):
                st.first(act)
            act.sem_inc(coef_copied, 2)
            act.sem_inc(msg_copied, NPAIR)
            act.sem_inc(idx_ready, 1)
            act.sem_inc(idx_taken, 1)

            def all_rstd(DV, AC):
                act.wait_ge(*DV.done(0, "ve"))
                a(rrstd[:], rvar[:], ACT.Ln).then_inc(*AC("ln"))
                act.wait_ge(*AC.done(0, "ln"))
                a(rtmp[:], rrstd[:], ACT.Exp, scale=-0.5).then_inc(*AC("exp"))

            nc.scalar.preload_act_table_set("natural_log_exp_and_others")
            all_rstd(dve2, act2)

            def copy_rows(t, s):
                act.wait_ge(*PT.done(t, "trans"))
                act.wait_ge(*PK.done(t - 2, "kv"))
                a(xnT[:, s], (pT, pA)[s][:, 0:F].rearrange("p (c q) -> p c q", c=FC), ACT.Copy).then_inc(*AX("xnT"))

            def kv_tile(t, s):
                act.wait_ge(*DK.done(t, "kmin"))
                act.wait_ge(*DK.done(t - 2, "kelu"))
                a(kexp[:, s, :], kmin[:, s, :], ACT.Exp).then_inc(*AK("kexp"))
                act.wait_ge(*PKA.done(t - 2, "kvacc"))
                a(vaug[:, s, :, 0:P], (pQ, pM)[s][:, F:2 * F].rearrange("p (c q) -> p c q", c=FC),
                  ACT.Copy).then_inc(*AK("vcopy"))

            copy_rows(0, 0)
            with act.Fori(0, T // 2) as i:
                for s in range(2):
                    copy_rows(2 * i + s + 1, 1 - s)
                    kv_tile(2 * i + s, s)
            kv_tile(T - 1, 0)

            act.wait_ge(*dve3.done(0, "aggr1"))
            a(cstd[:], cmv[:, :, 1], ACT.Sqrt, scale=float(N) / (N - 1)).then_inc(*act3("sqrt"))
            act.wait_ge(*pe3.done(0, "params"))
            a(colp[:], pR[:, 0:PR], ACT.Copy).then_inc(ccopy, 1)

            def rstd_ln(t, p):
                act.wait_ge(*DM.done(t, p + "ve"))
                a(lnln[:], lnve[:], ACT.Ln).then_inc(*AM(p + "ln"))
                act.wait_ge(*AM.done(t, p + "ln"))
                a(lny[:], lnln[:], ACT.Exp, scale=-0.5).then_inc(*AM(p + "exp"))

            nc.scalar.preload_act_table_set("natural_log_exp_and_others")
            act.wait_ge(*dveb.done(0, "min"))
            groups = act.alloc_register("act_groups")
            act.reg_mov(groups, 0)

            def copyT(t, out_, name):
                act.wait_ge(*PM.done(t, name))
                a(out_, pT[:, 0:F].rearrange("p (c q) -> p c q", c=FC), ACT.Copy).then_inc(*AM(name))

            def step_xT(t):
                act.wait_ge(*PM.done(t - 1, "hid"))
                copyT(t, xnT[:, 0], "xT")

            def step_qexp(t):
                act.wait_ge(*DM.done(t, "qmin"))
                a(qexp[:], qmin[:], ACT.Exp).then_inc(*AM("qexp"))

            def step_mT(t):
                act.wait_ge(*PM.done(t, "mT"))
                for c in range(FC):
                    a(mT[:, c, :], pT[:, c * P:(c + 1) * P], ACT.Identity, scale=colp[:, R_G1 + c:R_G1 + c + 1],
                      bias=colp[:, R_BB1 + c:R_BB1 + c + 1]).then_inc(*AM(f"mT{c}"))

            def step_relu(t):
                act.wait_ge(*PM.done(t, "hid"))
                a(hT[:], pH[:].rearrange("p (c q) -> p c q", c=HC), ACT.Relu).then_inc(*AM("relu"))

            def coefs(g, half):
                ks = HALVES[half]
                act.wait_ge(coef_done, g * 2 + half + 3)
                act.wait_ge(msg_done, g * NPAIR + 2 * half + 2)
                a(coef[:, ks[0]:ks[-1] + 1, :], pC[half][:, 0:len(ks) * P].rearrange("p (k q) -> p k q", q=P),
                  ACT.Copy).then_inc(coef_copied, 1)

            def messages(begun, half):
                if half == 0:
                    act.wait_ge(idx_float, begun * 2 + 1)
                    act.wait_ge(idx_ready, begun * NPAIR + 1 - NPAIR)
                    a(idx_now[:], idxf[:], ACT.Copy).then_inc(idx_taken, 1)
                    act.wait_ge(idx_taken, begun + 1)
                for j in (2 * half, 2 * half + 1):
                    k0, k1 = PAIRS[j][0], PAIRS[j][-1] + 1
                    act.wait_ge(landed, begun * U + k1)
                    a(idx[:, k0:k1], idx_now[:, k0:k1], ACT.Copy).then_inc(idx_ready, 1)
                    act.wait_ge(msg_done, begun * NPAIR + j + 1)
                    a(msgs[:, k0:k1, :], pX[j % 2][:, 0:(k1 - k0) * F].rearrange("p (k f) -> p k f", f=F),
                      ACT.Copy).then_inc(msg_copied, 1)

            after_a = [step_xT, None, lambda t: copyT(t, msgT[:], "msgT"), step_mT, None]
            after_b = [step_qexp, None, lambda t: rstd_ln(t, "m"), step_relu, lambda t: rstd_ln(t, "h")]
            with act.Fori(0, T) as t:
                n = act.value_load(bnd[0:1, 1, bass.ds(t, 1)], min_val=NG, max_val=-(-CH // U))
                g0 = act.snap(groups)
                for i in range(NG):
                    if after_a[i]:
                        after_a[i](t)
                    coefs(g0 + i, 0)
                    if i:
                        messages(g0 + i, 1)
                    else:
                        with act.If(t > 0):
                            messages(g0, 1)
                    coefs(g0 + i, 1)
                    if after_b[i]:
                        after_b[i](t)
                    messages(g0 + (i + 1), 0)
                with act.If(n > NG):
                    with act.Fori(NG, n) as i:
                        coefs(g0 + i, 0)
                        messages(g0 + i, 1)
                        coefs(g0 + i, 1)
                        messages(g0 + i + 1, 0)
                act.reg_add(groups, groups, n)
            messages(act.snap(groups), 1)

            def gnn(t, s):
                act.wait_ge(*PG.done(t, "aggT"))
                act.wait_ge(*PG2.done(t - 2, "gnn"))
                a(aggT[:, s], (pT, pQ)[s][:, 0:F].rearrange("p (c q) -> p c q", c=FC), ACT.Copy).then_inc(*AG("aggT"))

            with act.Fori(0, T // 2) as i:
                for s in range(2):
                    gnn(2 * i + s, s)
            gnn(T - 1, 0)
            all_rstd(dveo, acto)

            def route(t, s):
                act.wait_ge(*PR_.done(t, "xT"))
                act.wait_ge(*PR_.done(t - 2, "log"))
                a(aggT[:, s], (pT, pQ)[s][:, 0:F].rearrange("p (c q) -> p c q", c=FC), ACT.Copy).then_inc(*AR("xT"))
                act.wait_ge(*PR_.done(t, "log"))
                lo_ = tile(logits, t)
                a(lo_ if isinstance(t, int) else lo_.rearrange("p a e -> p (a e)"), (pM, pH)[s][:, 0:NE],
                  ACT.Copy).then_inc(*AR("log"))

            with act.Fori(0, T // 2) as i:
                for s in range(2):
                    route(2 * i + s, s)
            route(T - 1, 0)
            all_rstd(dvei, acti)
            act.wait_ge(*dver.done(0, "dif"))
            a(best[:, 0, :], best[:, 1, :], ACT.Exp).then_inc(*actr("exp"))

            act.wait_ge(*dve5.done(0, "inb"))
            nb = act.value_load(ztab[0:1, NE:NE + 1], min_val=1, max_val=MAXBLK)
            with act.Fori(0, nb) as b:
                e = act.value_load(btab[0:1, 1, bass.ds(b, 1)], min_val=0, max_val=NE - 1)
                for j in range(EHC):
                    act.wait_ge(*PE_.done(b, f"h{j}"))
                    act.wait_ge(*PE_.done(b - 1, "y1"))
                    a(ehT[:, j, :], (pA, pQ, pM, pH)[j % 4][:, 0:BLK], ACT.Gelu,
                      bias=colp[:, bass.ds(e * EHC + R_B1 + j, 1)]).then_inc(*AE(f"g{j}"))
                act.wait_ge(*DE.done(b, "y1"))
                act.dma_start(eouts[bass.ds(b * BLK, BLK), :].rearrange("(m p) f -> p m f", p=P), yb[:]).then_inc(out_rows, 16)

        @block.vector
        def _(dve):
            v = nc.vector
            kept = [0]
            for st in (dve1, dve2, DN, DS, DK, dve3, DM, dve5, DE, DI, DC, dveb, dve6, DA, DG, DR, dveo, dvei, dver, DD):
                st.first(dve)
            for st in (counted, same_made, reads_made, idx_float, floats_made, out_rows, *stored):
                dve.sem_inc(st, 1)
            dve.wait_ge(consts_made, 1)
            dve.wait_ge(x_loaded, 16 * (nxc + 1))
            with dve.Fori(0, T) as t:
                v.bn_stats(tile(bst, t), tile(x1, t)).then_inc(*dve1("stats"))
            dve.wait_ge(*dve1.done(T - 1, "stats"))
            own = lambda st, name: dve.wait_ge(*st.done(0, name))

            def all_rstd(D, AC):
                me, mo, ve, vo = bst[:, :, 1], bst[:, :, 4], bst[:, :, 2], bst[:, :, 5]
                v.tensor_tensor(rmean[:], me, mo, ALU.add).then_inc(*D("msum"))
                own(D, "msum")
                v.tensor_scalar(rmean[:], rmean[:], 0.5, None, ALU.mult).then_inc(*D("mean"))
                v.tensor_tensor(rtmp[:], me, mo, ALU.subtract).then_inc(*D("dif"))
                v.tensor_tensor(rvar[:], ve, vo, ALU.add).then_inc(*D("m2"))
                own(D, "m2")
                v.tensor_tensor(rtmp[:], rtmp[:], rtmp[:], ALU.mult).then_inc(*D("dif2"))
                v.tensor_scalar(rvar[:], rvar[:], 1.0 / F, None, ALU.mult).then_inc(*D("dif4"))
                own(D, "dif4")
                v.scalar_tensor_tensor(rvar[:], rtmp[:], 0.25, rvar[:], ALU.mult, ALU.add).then_inc(*D("var"))
                own(D, "var")
                v.tensor_scalar(rvar[:], rvar[:], EPS, None, ALU.add).then_inc(*D("ve"))
                dve.wait_ge(*AC.done(0, "exp"))
                v.tensor_tensor(rrstd[:], rtmp[:], rtmp[:], ALU.mult).then_inc(*D("a"))
                own(D, "a")
                v.tensor_tensor(rvar[:], rrstd[:], rvar[:], ALU.mult).then_inc(*D("nr"))
                own(D, "nr")
                v.tensor_scalar(rvar[:], rvar[:], -0.5, 1.5, ALU.mult, ALU.add).then_inc(*D("y"))
                own(D, "y")
                v.tensor_tensor(rrstd[:], rtmp[:], rvar[:], ALU.mult).then_inc(*D("rstd"))
                own(D, "rstd")

            all_rstd(dve2, act2)
            rs_done = sem("ones_column")
            v.memset(vaug[:, :, :, P:P + 1], 1.0).then_inc(rs_done, 1)
            dve.wait_ge(rs_done, 1)

            def norm_rows(t, s):
                dve.wait_ge(*PT.done(t - 2, "trans"))
                dve.wait_ge(*GK.done(t - 2, "res"))
                x1t = tile(x1, t) if isinstance(t, int) else tile(x1, t).rearrange("p a f -> p (a f)")
                v.tensor_scalar(xs[:, s, :], x1t, col(rmean, t), col(rrstd, t),
                                ALU.subtract, ALU.mult).then_inc(*DN("norm"))

            def col_stats(t, s, rows=P):
                dve.wait_ge(*PT.done(t, "trans"))
                dve.wait_ge(*AX.done(t, "xnT"))
                apart(dve)
                for c in range(FC):
                    v.bn_stats(cst[:, c, t, :] if isinstance(t, int) else cst[:, c, bass.ds(t, 1), :],
                               (pT, pA)[s][:, c * P:c * P + rows]).then_inc(*DS(f"cstat{c}"))

            def k_min(t, s):
                dve.wait_ge(*PK.done(t, "kv"))
                dve.wait_ge(*AK.done(t - 2, "kexp"))
                v.tensor_scalar(kmin[:, s, :], (pQ, pM)[s][:, 0:F], 0.0, None, ALU.min).then_inc(*DK("kmin"))

            def k_elu(t, s):
                dve.wait_ge(*AK.done(t, "kexp"))
                dve.wait_ge(*AK.done(t, "vcopy"))
                dve.wait_ge(*PKA.done(t - 2, "kvacc"))
                v.scalar_tensor_tensor(kelu[:, s, :], (pQ, pM)[s][:, 0:F], 0.0, kexp[:, s, :],
                                       ALU.max, ALU.add).then_inc(*DK("kelu"))

            def kv_tile(t, s):
                k_min(t, s)
                col_stats(t + 1, 1 - s)
                norm_rows(t + 2, s)
                k_elu(t, s)

            norm_rows(0, 0)
            norm_rows(1, 1)
            col_stats(0, 0)
            with dve.Fori(0, (T - 3) // 2) as i:
                for s in range(2):
                    kv_tile(2 * i + s, s)
            kv_tile(T - 3, 0)
            k_min(T - 2, 1)
            col_stats(T - 1, 0, TAIL)
            k_elu(T - 2, 1)
            dve.wait_ge(*PKA.done(T - 3, "kvacc"))
            vt = sem("vaug_tail")
            for c in range(FC):
                v.tensor_copy(vaug[:, 0, c, P:P + 1], valid[:, T - 1:T]).then_inc(vt, 1)
            dve.wait_ge(vt, 2)
            k_min(T - 1, 0)
            k_elu(T - 1, 0)

            for c in range(FC):
                dve.wait_ge(*DS.done(T - 1, "cstat1"))
                v.bn_aggr(cmv[:, c, :], cst[:, c].rearrange("p t s -> p (t s)")).then_inc(*dve3(f"aggr{c}"))
            dve.wait_ge(*act3.done(0, "sqrt"))
            dve.wait_ge(weights, 16 * 15)
            v.tensor_scalar(cstd[:], cstd[:], STD_EPS, None, ALU.add).then_inc(*dve3("std"))
            own(dve3, "std")
            v.reciprocal(cstd[:], cstd[:]).then_inc(*dve3("inv"))
            own(dve3, "inv")
            for c in range(FC):
                v.tensor_scalar(wgs[:, c, :], wg[:, c, :], cstd[:, c:c + 1], None, ALU.mult).then_inc(*dve3(f"wgs{c}"))
            for c in range(FC):
                v.tensor_scalar(dmean[:, c, :], ident[:], cmv[:, c, 0:1], None, ALU.mult).then_inc(*dve3(f"dm{c}"))
            dve.wait_ge(*pe3.done(0, "mean"))
            v.tensor_copy(mean_bc[:], pY[:, 0:F]).then_inc(*dve3("meanbc"))
            own(dve3, "meanbc")
            dve.wait_ge(*GK.done(T - 1, "res"))
            TG = 7
            for k in range(T // TG):
                xk = xn[:, k * TG:(k + 1) * TG, :]
                v.tensor_tensor(xk, xk, mean_bc[:].unsqueeze(1).to_broadcast([P, TG, F]), ALU.subtract).then_inc(cen_made, 1)
            dve.wait_ge(cen_made, T // TG)
            for c in range(FC):
                acc = (pG, pH)[c]
                v.tensor_tensor(kvbd[:, c, 0:P], acc[:, 0:P], bdmask[:].rearrange("p a b -> p (a b)"), ALU.mult).then_inc(*dve3(f"kv{c}"))
            for c in range(FC):
                acc = (pG, pH)[c]
                v.tensor_scalar(kvbd[:, c, P:P + HPC], hmask[:], acc[:, P:P + 1], None, ALU.mult).then_inc(*dve3(f"ks{c}"))
            v.tensor_tensor(bias_bc[:], bias_bc[:], gb_bc[:], ALU.add).then_inc(*dve3("gb"))

            dve.wait_ge(chunks_loaded, 32)
            v.tensor_reduce(cmax[:], dstc[:], AX_X, ALU.max).then_inc(*dveb("cmax"))
            v.tensor_reduce(cmin[:], dstc[:], AX_X, ALU.min).then_inc(*dveb("cmin"))
            own(dveb, "cmin")
            bt = lambda z: z[:].unsqueeze(2).to_broadcast([P, T, CB])
            bc = lambda z: z[:].unsqueeze(1).to_broadcast([P, T, CB])
            v.tensor_tensor(indA[:], bc(cmin), bt(thi), ALU.is_le).then_inc(*dveb("indA"))
            v.tensor_tensor(indB[:], bc(cmax), bt(tlo), ALU.is_ge).then_inc(*dveb("indB"))
            own(dveb, "indB")
            v.tensor_tensor(indA[:], indA[:], indB[:], ALU.mult).then_inc(*dveb("ind"))
            own(dveb, "ind")
            v.tensor_tensor(indB[:], indA[:], bc(cidx), ALU.mult).then_inc(*dveb("vhi"))
            own(dveb, "vhi")
            v.tensor_reduce(vmax[:, 0:T], indB[:], AX_X, ALU.max).then_inc(*dveb("vmaxhi"))
            v.tensor_tensor(indA[:], indA[:], bc(cinv), ALU.mult).then_inc(*dveb("vlo"))
            own(dveb, "vlo")
            v.tensor_reduce(vmax[:, T:2 * T], indA[:], AX_X, ALU.max).then_inc(*dveb("vmaxlo"))
            dve.wait_ge(*peb.done(0, "t1"))
            v.tensor_reduce(vred[:], pA[0:2 * T, 0:P], AX_X, ALU.max).then_inc(*dveb("vred"))
            dve.wait_ge(*peb.done(0, "t2"))
            v.tensor_copy(brow[:], pA[0:1, 256:256 + 2 * T]).then_inc(*dveb("row"))
            own(dveb, "row")
            hi, lo = brow[:, 0:T], brow[:, T:2 * T]
            v.tensor_scalar(hi, hi, float(CH), 1.0, ALU.min, ALU.max).then_inc(*dveb("hi1"))
            v.tensor_scalar(lo, lo, -1.0, float(BIG), ALU.mult, ALU.add).then_inc(*dveb("lo1"))
            own(dveb, "lo1")
            v.tensor_scalar(bndf[:, 1, :], hi, -1.0, None, ALU.add).then_inc(*dveb("hi2"))
            own(dveb, "hi2")
            v.tensor_tensor(lo, lo, bndf[:, 1, :], ALU.min).then_inc(*dveb("lo2"))
            own(dveb, "lo2")
            v.tensor_tensor(hi, hi, lo, ALU.subtract).then_inc(*dveb("n1"))
            own(dveb, "n1")
            RECIP, SHIFT = -(-(1 << 16) // U), 16
            assert (CH + U) * RECIP < 1 << 24
            v.tensor_scalar(bndf[:, 1, :], hi, float(U - 1), None, ALU.add).then_inc(*dveb("n2"))
            own(dveb, "n2")
            v.tensor_scalar(bndf[:, 1, :], bndf[:, 1, :], float(RECIP), None, ALU.mult).then_inc(*dveb("mul"))
            v.tensor_scalar(bndf[:, 0, :], lo, float(CH - (NG - 1) * U), float(P), ALU.min, ALU.mult).then_inc(*dveb("elo"))
            own(dveb, "elo")
            v.tensor_copy(bnd[:, 0, :], bndf[:, 0, :]).then_inc(*dveb("ielo"))
            v.tensor_copy(bnd[:, 1, :], bndf[:, 1, :]).then_inc(*dveb("in"))
            own(dveb, "in")
            v.tensor_single_scalar(bnd[:, 1, :], bnd[:, 1, :], SHIFT, ALU.logical_shift_right).then_inc(*dveb("shr"))
            own(dveb, "shr")
            v.tensor_scalar(bnd[:, 1, :], bnd[:, 1, :], float(NG), None, ALU.max).then_inc(*dveb("min"))
            own(dveb, "min")
            dve.wait_ge(ccopy, 1)
            own(dve3, "gb")

            groups = dve.alloc_register("dve_groups")
            dve.reg_mov(groups, 0)

            def me_(t, name):
                dve.wait_ge(*DM.done(t, name))

            def norm(t, p, src_ap, dst_ap):
                apart(dve)
                v.bn_stats(lnst[:], src_ap).then_inc(*DM(p + "st"))
                me_(t, p + "st")
                apart(dve)
                v.bn_aggr(lnmv[:], lnst[:]).then_inc(*DM(p + "ag"))
                me_(t, p + "ag")
                v.tensor_scalar(lnve[:], lnmv[:, 1:2], EPS, None, ALU.add).then_inc(*DM(p + "ve"))
                dve.wait_ge(*AM.done(t, p + "exp"))
                v.scalar_tensor_tensor(lna[:], lny[:], lnve[:], lny[:], ALU.mult, ALU.mult).then_inc(*DM(p + "a"))
                me_(t, p + "a")
                v.tensor_scalar(lna[:], lna[:], -0.5, 1.5, ALU.mult, ALU.add).then_inc(*DM(p + "nr"))
                me_(t, p + "nr")
                v.tensor_tensor(lnr[:], lna[:], lny[:], ALU.mult).then_inc(*DM(p + "r"))
                me_(t, p + "r")
                v.tensor_scalar(dst_ap, src_ap, lnmv[:, 0:1], lnr[:], ALU.subtract, ALU.mult).then_inc(*DM(p + "ap"))

            def step_start(t):
                dve.wait_ge(reads_made, dve.snap(groups) * U + 1)
                v.tensor_scalar(idrow[:], idrow[:], float(P), None, ALU.add).then_inc(*DM("idrow"))
                dve.wait_ge(*PM.done(t - 1, "xT"))
                v.tensor_tensor(xs[:, 0, :], tile(xn, t).rearrange("p a f -> p (a f)"), mean_bc[:], ALU.add).then_inc(*DM("xs"))
                me_(t, "idrow")

            def step_q(t):
                dve.wait_ge(*PM.done(t, "q"))
                q3 = pQ[:, 0:F].rearrange("p (c q) -> p c q", c=FC)
                v.tensor_scalar(qmin[:], q3, 0.0, None, ALU.min).then_inc(*DM("qmin"))
                dve.wait_ge(*AM.done(t, "qexp"))
                v.scalar_tensor_tensor(qelu[:], q3, 0.0, qexp[:], ALU.max, ALU.add).then_inc(*DM("qelu"))

            def step_msg(t):
                dve.wait_ge(*PM.done(t, "num"))
                pm3 = pM[:, 0:FC * (P + HPC)].rearrange("p (c w) -> p c w", c=FC)
                v.tensor_scalar(rden[:], pm3[:, :, P:P + HPC], ATT_EPS, None, ALU.add).then_inc(*DM("eps"))
                me_(t, "eps")
                v.reciprocal(rden[:], rden[:]).then_inc(*DM("rden"))
                me_(t, "rden")
                v.tensor_tensor(msg[:].rearrange("p (c h d) -> p c h d", c=FC, h=HPC),
                                pm3[:, :, 0:P].rearrange("p c (h d) -> p c h d", h=HPC),
                                rden[:].unsqueeze(3).to_broadcast([P, FC, HPC, HD]), ALU.mult).then_inc(*DM("msg"))

            def step_mnorm(t):
                dve.wait_ge(*PM.done(t, "mm"))
                norm(t, "m", pQ[:, 0:F], mrow[:])

            def step_hnorm(t):
                dve.wait_ge(*PM.done(t, "h2"))
                norm(t, "h", pQ[:, 0:F], mrow[:])
                me_(t, "hap")
                v.tensor_tensor(mrow[:], mrow[:], g2_bc[:], ALU.mult).then_inc(*DM("g2"))
                me_(t, "g2")
                v.tensor_tensor(mrow[:], mrow[:], bias_bc[:], ALU.add).then_inc(*DM("b2"))
                me_(t, "b2")
                x1t = tile(x1, t).rearrange("p a f -> p (a f)")
                v.tensor_tensor(x1t, x1t, mrow[:], ALU.add).then_inc(*DM("res"))

            rows_of = src_row[:].rearrange("p (e k) -> p k e", k=U)

            def onehots(g):
                dve.wait_ge(ends_loaded, g * 48 + 48)
                dve.wait_ge(idx_float, g * 2 + 1)
                v.tensor_copy(srcf[:], src_e[:]).then_inc(floats_made, 1)
                v.tensor_copy(dstf[:], dst_e[:]).then_inc(floats_made, 1)
                dve.wait_ge(row_loaded, g * 16 + 16)
                dve.wait_ge(floats_made, g * 2 + 3)
                for half in range(2):
                    dve.wait_ge(coef_done, g * 2 + half + 1)
                    for k in HALVES[half]:
                        v.tensor_scalar(same[:, k, :], rows_of[:, k, :], srcf[:, k:k + 1], None,
                                        ALU.is_equal).then_inc(same_made, 1)
                for k in range(U):
                    v.tensor_scalar(reads[:, k, :], idrow[:], dstf[:, k:k + 1], w_e[:, k:k + 1],
                                    ALU.is_equal, ALU.mult).then_inc(reads_made, 1)

            def indices(g):
                dve.wait_ge(counted, g * (U + 1) + 1)
                v.tensor_tensor(away[:], dummy[:], srcf[:], ALU.subtract).then_inc(counted, 1)
                dve.wait_ge(same_made, g * U + U + 1)
                for k in range(U):
                    v.scalar_tensor_tensor(junk[:, k, :], same[:, k, :], 1.0, trilow[:], ALU.mult, ALU.mult,
                                           accum_out=before[:, k:k + 1]).then_inc(counted, 1)
                dve.wait_ge(counted, g * (U + 1) + U + 2)
                dve.wait_ge(idx_taken, g + 1)
                v.scalar_tensor_tensor(away[:], before[:], 0.0, away[:], ALU.is_gt, ALU.mult).then_inc(idx_float, 1)
                dve.wait_ge(idx_float, g * 2 + 2)
                v.tensor_tensor(idxf[:], away[:], srcf[:], ALU.add).then_inc(idx_float, 1)

            pieces = [step_q, step_msg, step_mnorm, None, step_hnorm]
            with dve.Fori(0, T) as t:
                n = dve.value_load(bnd[0:1, 1, bass.ds(t, 1)], min_val=NG, max_val=-(-CH // U))
                step_start(t)
                g0 = dve.snap(groups)
                for i in range(NG):
                    onehots(g0 + i)
                    indices(g0 + i)
                    if pieces[i]:
                        pieces[i](t)
                with dve.If(n > NG):
                    with dve.Fori(NG, n) as i:
                        onehots(g0 + i)
                        indices(g0 + i)
                dve.reg_add(groups, groups, n)

            flat = lambda b, t: tile(b, t) if isinstance(t, int) else tile(b, t).rearrange("p a f -> p (a f)")

            def add_parts(t, s, turn):
                dve.wait_ge(parts_loaded[s], 16 * NACC * (turn + 1))
                v.tensor_tensor(parts[:, s, 0:NACC // 2, :], parts[:, s, 0:NACC // 2, :], parts[:, s, NACC // 2:NACC, :],
                                ALU.add).then_inc(*DA("add"))

            def gnn(t):
                dve.wait_ge(*PG2.done(t, "gnn"))
                v.tensor_tensor(flat(x1, t), flat(x1, t), (pM, pH)[gnn_turn[0] % 2][:, 0:F], ALU.add).then_inc(*DG("res"))
                gnn_turn[0] += 1
                dve.wait_ge(*DG.done(t, "res"))
                apart(dve)
                v.bn_stats(flat(bst, t), flat(x1, t)).then_inc(*DG("stats"))

            gnn_turn = [0]
            add_parts(0, 0, 0)
            add_parts(1, 1, 0)
            with dve.Fori(0, T // SLOTS - 1) as i:
                for s in range(SLOTS):
                    add_parts(SLOTS * i + s + 2, (s + 2) % SLOTS, i + (s + 2) // SLOTS)
                    gnn(SLOTS * i + s)
            i = T // SLOTS - 1
            for s in range(SLOTS + 1):
                if s + 2 <= SLOTS:
                    add_parts(SLOTS * i + s + 2, (s + 2) % SLOTS, i + (s + 2) // SLOTS)
                gnn(SLOTS * i + s)
            dve.wait_ge(*DG.done(T - 1, "stats"))
            all_rstd(dveo, acto)

            def outer(t, s):
                dve.wait_ge(*PR_.done(t - 2, "xT"))
                dve.wait_ge(*GR.done(t - 2, "keep"))
                v.tensor_scalar(xs[:, s, :], flat(x1, t), col(rmean, t), col(rrstd, t),
                                ALU.subtract, ALU.mult).then_inc(*DR("xt"))
                dve.wait_ge(*DR.done(t, "xt"))
                apart(dve)
                v.bn_stats(flat(bst, t), xs[:, s, :]).then_inc(*DR("stats"))

            with dve.Fori(0, T // 2) as i:
                for s in range(2):
                    outer(2 * i + s, s)
            outer(T - 1, 0)
            dve.wait_ge(*DR.done(T - 1, "stats"))
            all_rstd(dvei, acti)

            D = dver
            te = [P, T, NE]
            over_e = lambda z: z.unsqueeze(2).to_broadcast(te)
            dve.wait_ge(*AR.done(T - 1, "log"))
            v.tensor_tensor(logits[:], logits[:], br_bc[:].unsqueeze(1).to_broadcast(te), ALU.add).then_inc(*D("br"))
            own(D, "br")
            for j in range(2):
                v.tensor_reduce(best[:, j, :], logits[:], AX_X, ALU.max).then_inc(*D(f"b{j}"))
                own(D, f"b{j}")
                v.tensor_tensor(hot[:, j], logits[:], over_e(best[:, j, :]), ALU.is_equal).then_inc(*D(f"e{j}"))
                own(D, f"e{j}")
                v.tensor_tensor(work[:, 0], hot[:, j], down8[:].unsqueeze(1).to_broadcast(te), ALU.mult).then_inc(*D(f"r{j}"))
                own(D, f"r{j}")
                v.tensor_reduce(which[:], work[:, 0], AX_X, ALU.max).then_inc(*D(f"w{j}"))
                own(D, f"w{j}")
                v.tensor_tensor(hot[:, j], work[:, 0], over_e(which[:]), ALU.is_equal).then_inc(*D(f"h{j}"))
                own(D, f"h{j}")
                if j == 0:
                    v.tensor_scalar(work[:, 1], hot[:, 0], -3e38, None, ALU.mult).then_inc(*D("p0"))
                    own(D, "p0")
                    v.tensor_tensor(logits[:], logits[:], work[:, 1], ALU.add).then_inc(*D("l1"))
                    own(D, "l1")
            v.tensor_tensor(best[:, 1, :], best[:, 1, :], best[:, 0, :], ALU.subtract).then_inc(*D("dif"))
            dve.wait_ge(*actr.done(0, "exp"))
            v.tensor_scalar(best[:, 1, :], best[:, 0, :], 1.0, None, ALU.add).then_inc(*D("den"))
            own(D, "den")
            v.reciprocal(wts[:, :, 0], best[:, 1, :]).then_inc(*D("wa"))
            own(D, "wa")
            v.tensor_tensor(wts[:, :, 1], wts[:, :, 0], best[:, 0, :], ALU.mult).then_inc(*D("wb"))
            for j in range(2):
                v.tensor_tensor(hot[:, j], hot[:, j], over_e(valid[:]), ALU.mult).then_inc(*D(f"v{j}"))
            own(D, "v1")
            v.tensor_tensor(hots[:], hot[:, 0], hot[:, 1], ALU.add).then_inc(*D("sum"))
            dve.wait_ge(*per.done(0, "tot"))
            v.tensor_copy(work[:, 0].rearrange("p t e -> p (t e)"), pY[:, 0:TE]).then_inc(*D("tot"))
            own(D, "tot")
            cur, step = 0, 1
            while step < T:
                nxt = 1 - cur
                v.tensor_tensor(work[:, nxt, step:T, :], work[:, cur, step:T, :], work[:, cur, 0:T - step, :], ALU.add).then_inc(*D(f"s{step}"))
                v.tensor_copy(work[:, nxt, 0:step, :], work[:, cur, 0:step, :]).then_inc(prefix_kept, 1)
                own(D, f"s{step}")
                kept[0] += 1
                dve.wait_ge(prefix_kept, kept[0])
                cur, step = nxt, 2 * step
            run = work[:, cur]
            v.tensor_copy(lastcnt[:], run[:, T - 1, :]).then_inc(prefix_kept, 1)
            kept[0] += 1
            dve.wait_ge(prefix_kept, kept[0])
            fl = lambda z: z.rearrange("p t e -> p (t e)")
            v.tensor_tensor(fl(run), fl(run), pY[:, 0:TE], ALU.subtract).then_inc(*D("sub"))
            own(D, "sub")
            v.tensor_tensor(fl(run), fl(run), pA[:, 0:TE], ALU.add).then_inc(*D("rank"))
            own(D, "rank")
            v.tensor_tensor(run, run, ebase[:].unsqueeze(1).to_broadcast(te), ALU.add).then_inc(*D("base"))
            own(D, "base")
            for j in range(2):
                v.tensor_tensor(work[:, 1 - cur], hot[:, j], run, ALU.mult).then_inc(*D(f"p{j}x"))
                own(D, f"p{j}x")
                v.tensor_reduce(slotf[:, :, j], work[:, 1 - cur], AX_X, ALU.add).then_inc(*D(f"s{j}x"))
                own(D, f"s{j}x")
            v.tensor_tensor(carry[:], lastcnt[:], ebase[:], ALU.add).then_inc(*D("last"))

            def hand(t, s, turn):
                if turn is not None:
                    dve.wait_ge(dispatched[s], turn * 32)
                v.tensor_scalar(xn2[:, s, :], flat(xn, t), col(rmean, t), col(rrstd, t),
                                ALU.subtract, ALU.mult).then_inc(*DD("xn2"))
                v.tensor_copy(slot_now[:, s, :], flat(slotf, t)).then_inc(*DD("slot"))

            dve.wait_ge(*GR.done(T - 1, "keep"))
            hand(0, 0, None)
            hand(1, 1, None)
            with dve.Fori(1, T // 2) as i:
                for s in range(2):
                    hand(2 * i + s, s, i)
            hand(T - 1, 0, T // 2)

            own(dver, "last")
            dve.wait_ge(*DD.done(T - 1, "slot"))
            v.tensor_tensor(cnt[:], carry[:], ebase[:], ALU.subtract).then_inc(*dve5("cnt"))
            own(dve5, "cnt")
            v.tensor_scalar(cnt[:], cnt[:], float(BLK - 1), None, ALU.add).then_inc(*dve5("c255"))
            own(dve5, "c255")
            v.tensor_copy(cnti[:], cnt[:]).then_inc(*dve5("ci"))
            own(dve5, "ci")
            v.tensor_single_scalar(cnti[:], cnti[:], 8, ALU.logical_shift_right).then_inc(*dve5("sh"))
            own(dve5, "sh")
            v.tensor_copy(nblk[:], cnti[:]).then_inc(*dve5("nb"))
            own(dve5, "nb")
            v.tensor_tensor_scan(cum[:], one8[:], nblk[:], 0.0, ALU.mult, ALU.add).then_inc(*dve5("cum"))
            own(dve5, "cum")
            bb = bidx[:].unsqueeze(2).to_broadcast([1, MAXBLK, NE])
            v.tensor_tensor(le[:], cum[0:1].unsqueeze(1).to_broadcast([1, MAXBLK, NE]), bb, ALU.is_le).then_inc(*dve5("le"))
            own(dve5, "le")
            v.tensor_tensor(lenb[:], le[:], nblk[0:1].unsqueeze(1).to_broadcast([1, MAXBLK, NE]), ALU.mult).then_inc(*dve5("lenb"))
            own(dve5, "lenb")
            v.tensor_reduce(be[:], le[:], AX_X, ALU.add).then_inc(*dve5("be"))
            v.tensor_reduce(bprev[:], lenb[:], AX_X, ALU.add).then_inc(*dve5("bprev"))
            own(dve5, "bprev")
            v.tensor_tensor(bstart[:], bidx[:], bprev[:], ALU.subtract).then_inc(*dve5("st1"))
            own(dve5, "st1")
            v.tensor_scalar(bstart[:], bstart[:], float(BLK), None, ALU.mult).then_inc(*dve5("st2"))
            own(dve5, "st2")
            v.scalar_tensor_tensor(btab[:, 0, :], be[:], float(REG), bstart[:], ALU.mult, ALU.add).then_inc(*dve5("itab"))
            v.tensor_copy(btab[:, 1, :], be[:]).then_inc(*dve5("ibe"))
            v.tensor_copy(ztab[:, 0:NE], carry[0:1, :]).then_inc(*dve5("izt"))
            v.tensor_copy(ztab[:, NE:NE + 1], cum[0:1, NE - 1:NE]).then_inc(*dve5("inb"))
            own(dve5, "inb")
            nb = dve.value_load(ztab[0:1, NE:NE + 1], min_val=1, max_val=MAXBLK)
            with dve.Fori(0, nb) as b:
                e = dve.value_load(btab[0:1, 1, bass.ds(b, 1)], min_val=0, max_val=NE - 1)
                dve.wait_ge(*PE_.done(b - 1, f"h{EHC - 1}"))
                for c in range(FC):
                    dve.wait_ge(*PE_.done(b, f"t{c}"))
                    v.tensor_scalar(xeT[:, c, :], (pT, pR)[c][:, 0:BLK], colp[:, bass.ds(e * FC + R_G + c, 1)],
                                    colp[:, bass.ds(e * FC + R_B + c, 1)], ALU.mult, ALU.add).then_inc(*DE(f"x{c}"))
                dve.wait_ge(eb2_loaded, 16 * b + 16)
                dve.wait_ge(out_rows, 16 * b + 1)
                for m in range(BM):
                    dve.wait_ge(*PE_.done(b, f"y{m}"))
                    v.tensor_tensor(yb[:, m, :], (pY, pG)[m][:, 0:F], eb2_bc[:], ALU.add).then_inc(*DE(f"y{m}"))

            own(dve5, "inb")
            v.tensor_tensor(delta[:], cum[:], nblk[:], ALU.subtract).then_inc(*dve6("excl"))
            own(dve6, "excl")
            v.tensor_scalar(delta[:], delta[:], float(BLK), None, ALU.mult).then_inc(*dve6("rows"))
            own(dve6, "rows")
            v.tensor_tensor(delta[:], delta[:], ebase[:], ALU.subtract).then_inc(*dve6("delta"))
            own(dve6, "delta")
            for j in range(2):
                v.tensor_tensor(hot[:, j], hot[:, j], delta[:].unsqueeze(1).to_broadcast(te), ALU.mult).then_inc(*dve6(f"hot{j}"))
            own(dve6, "hot1")
            for j in range(2):
                v.tensor_reduce(slotc[:, :, j], hot[:, j], AX_X, ALU.add).then_inc(*dve6(("shift", "slot")[j]))
            own(dve6, "slot")
            v.tensor_tensor(slotf[:], slotf[:], slotc[:], ALU.add).then_inc(prefix_kept, 1)
            dve.wait_ge(prefix_kept, kept[0] + 1)

            def out_idx(t, s):
                v.tensor_copy(idx_c[:, s, :], flat(slotf, t)).then_inc(*DI("idx"))

            def combine(t, s, turn):
                rows = TAIL if isinstance(t, int) and t == T - 1 else P
                x1t, wt = flat(x1, t), flat(wts, t)
                dve.wait_ge(got[s][0], 16 * turn + 16)
                dve.wait_ge(stored[s], 16 * turn + 1)
                v.scalar_tensor_tensor(ob[0:rows, s, :], yg[0:rows, s, 0, :], wt[0:rows, 0:1], x1t[0:rows],
                                       ALU.mult, ALU.add).then_inc(*DC("a"))
                dve.wait_ge(*DC.done(t, "a"))
                dve.wait_ge(got[s][1], 16 * turn + 16)
                v.scalar_tensor_tensor(ob[0:rows, s, :], yg[0:rows, s, 1, :], wt[0:rows, 1:2], ob[0:rows, s, :],
                                       ALU.mult, ALU.add).then_inc(*DC("b"))
                dve.wait_ge(*DC.done(t, "b"))
                apart(dve)

            for s in range(SLOTS):
                out_idx(s, s)
            with dve.Fori(0, T // SLOTS - 1) as i:
                for s in range(SLOTS):
                    combine(SLOTS * i + s, s, i)
                    out_idx(SLOTS * (i + 1) + s, s)
            for t in range(T - 1 - SLOTS, T):
                combine(t, t % SLOTS, t // SLOTS)
                if t == T - 1 - SLOTS:
                    out_idx(T - 1, 0)


_INS = ['x', 'src', 'dst', 'edge_weight', 'L0_gnn_weight', 'L0_gnn_bias', 'L0_mix_Wq', 'L0_mix_Wk', 'L0_mix_Wv',
        'L0_mix_Wm', 'L0_mix_W1', 'L0_mix_W2', 'L0_mix_g1', 'L0_mix_b1', 'L0_mix_g2', 'L0_mix_b2', 'L0_ffn_Wr',
        'L0_ffn_br', 'L0_ffn_ln_g', 'L0_ffn_ln_b', 'L0_ffn_W1', 'L0_ffn_b1', 'L0_ffn_W2', 'L0_ffn_b2']


def kernel(**inputs):
    import numpy as _np
    import concourse.bacc as _bacc
    from concourse import mybir as _mybir
    from concourse.bass_utils import run_bass_kernel_spmd as _run

    nc = _bacc.Bacc("TRN2", target_bir_lowering=False, num_devices=1)
    arrays, args = {}, []
    for name in _INS:
        a = _np.ascontiguousarray(inputs[name])
        arrays[f"in_{name}_dram"] = a
        args.append(nc.dram_tensor(f"in_{name}_dram", a.shape, _mybir.dt.from_np(a.dtype), kind="ExternalInput").ap())
    out = nc.dram_tensor("out_0_dram", inputs["x"].shape, _mybir.dt.float32, kind="ExternalOutput").ap()
    gps_layer(nc, *args, out)
    r = _run(nc, [arrays], core_ids=[0])
    return r.results[0]["out_0_dram"]
```

```python
from contextlib import ExitStack

import concourse.bass as bass
from concourse import mybir

ALU = mybir.AluOpType
ACT = mybir.ActivationFunctionType
F32 = mybir.dt.float32
BF16 = mybir.dt.bfloat16
I32 = mybir.dt.int32
AX_X = mybir.AxisListType.X
EPS = 1e-5
ATT_EPS = 1e-6
STD_EPS = 1e-4


class Steps:

    LEAD = 2

    def __init__(self, sem, names):
        self.sem, self.names, self.k = sem, names.split(), 0

    def first(self, engine):
        engine.sem_inc(self.sem, self.LEAD * len(self.names))

    def __call__(self, name):
        assert self.names[self.k % len(self.names)] == name, (self.names[self.k % len(self.names)], name)
        self.k += 1
        return self.sem, 1

    def done(self, turn, name):
        n = len(self.names)
        return self.sem, (turn + self.LEAD) * n + self.names.index(name) + 1


def gps_layer(nc, x, src, dst, edge_weight, gnn_W, gnn_b, Wq, Wk, Wv, Wm, W1, W2, g1, b1, g2, b2,
              Wr, br, ln_g, ln_b, eW1, eb1, eW2, eb2, out):
    N, F = x.shape
    E = src.shape[0]
    P = 128
    T = -(-N // P)
    TAIL = N - (T - 1) * P
    FC = F // P
    HID = W1.shape[1]
    HC = HID // P
    HEADS = 8
    HD = F // HEADS
    HPC = P // HD
    NE, _, EH = eW1.shape
    EHC = EH // P
    BLK = 256
    BM = BLK // P
    MAXBLK = 2 * N // BLK + NE
    REG = (-(-N // BLK) + 1) * BLK
    CH = -(-E // P)
    CB = -(-CH // P)
    U = 7
    NG = 5
    NACC = U
    AHEAD = 4
    AROWS = -(-(N + P) // (2 * P)) * 2 * P
    EPAD = CH * P + U * P
    BIG = 2048
    PADDST = T * P - 1
    assert CH < BIG and FC == 2 and TAIL < P

    sums = [nc.dram_tensor(f"sums{k}", [AROWS, F], F32).ap() for k in range(NACC)]
    src_d = nc.dram_tensor("src_padded", [EPAD], I32).ap()
    dst_d = nc.dram_tensor("dst_padded", [EPAD], I32).ap()
    w_d = nc.dram_tensor("w_padded", [EPAD], F32).ap()
    erows = nc.dram_tensor("expert_rows", [NE * REG, F], F32).ap()
    eouts = nc.dram_tensor("expert_outs", [(MAXBLK + 1) * BLK, F], F32).ap()

    with ExitStack() as ctx:
        def sb(name, shape, dt=F32):
            return ctx.enter_context(nc.sbuf_tensor("sb_" + name, shape, dt))

        def ps(name, shape, dt=F32):
            return ctx.enter_context(nc.psum_tensor("ps_" + name, shape, dt))

        def sem(name):
            return ctx.enter_context(nc.semaphore(name))

        x1 = sb("x1", [P, T, F])
        ident = sb("ident", [P, P])
        ones = sb("ones", [P, P])
        tri = sb("tri", [P, P])
        bdmask = sb("bdmask", [P, HPC, HD])
        hmask = sb("hmask", [P, HPC])
        valid = sb("valid", [P, T])
        idrow = sb("idrow", [P, P])
        down8 = sb("down8", [P, NE])
        carry = sb("carry", [P, NE])
        ebase = sb("ebase", [P, NE])
        cidx = sb("cidx", [P, CB])
        cinv = sb("cinv", [P, CB])
        dummy = sb("dummy", [P, U])
        trilow = sb("trilow", [P, P])
        tlo = sb("tlo", [P, T])
        thi = sb("thi", [P, T])
        bidx = sb("bidx", [1, MAXBLK + 1])
        PADP = 2
        assert (EPAD - E) % PADP == 0
        padi = sb("padi", [PADP, (EPAD - E) // PADP], I32)
        padz = sb("padz", [PADP, (EPAD - E) // PADP], I32)
        zrows = sb("zrows", [P, BM * F])
        wq = sb("wq", [P, FC, F])
        wkv = sb("wkv", [P, FC, 2 * F])
        wm = sb("wm", [P, FC, F])
        w1 = sb("w1", [P, 2 * FC, HID])
        w2 = sb("w2", [P, HC, F])
        wg = sb("wg", [P, FC, F])
        wgs = sb("wgs", [P, FC, F])
        wr = sb("wr", [P, FC, NE])
        PR = NE * EHC + 4 * FC + 2 * NE * FC - 2 * FC
        rows_p = sb("rows_p", [PR, P])
        colp = sb("colp", [P, PR])
        R_B1, R_G, R_B, R_G1, R_BB1 = 0, NE * EHC, NE * EHC + NE * FC, NE * EHC + 2 * NE * FC, NE * EHC + 2 * NE * FC + FC
        g2_bc = sb("g2_bc", [P, F])
        bias_bc = sb("bias_bc", [P, F])
        gb_bc = sb("gb_bc", [P, F])
        br_bc = sb("br_bc", [P, NE])
        xn = sb("xn", [P, T, F])
        bst = sb("bst", [P, T, 6])
        rmean = sb("rmean", [P, T])
        rvar = sb("rvar", [P, T])
        rtmp = sb("rtmp", [P, T])
        rrstd = sb("rrstd", [P, T])
        xs = sb("xs", [P, 2, F])
        xnT = sb("xnT", [P, 2, FC, P])
        kmin = sb("kmin", [P, 2, F])
        kexp = sb("kexp", [P, 2, F])
        kelu = sb("kelu", [P, 2, F])
        vaug = sb("vaug", [P, 2, FC, P + 1])
        cst = sb("cst", [P, FC, T, 6])
        cmv = sb("cmv", [P, FC, 2])
        cstd = sb("cstd", [P, FC])
        dmean = sb("dmean", [P, FC, P])
        mean_bc = sb("mean_bc", [P, F])
        kvbd = sb("kvbd", [P, FC, P + HPC])
        ring = sb("ring", [P, U * (F + P)])
        assert CB * P <= U * (F + P) and T * CB <= U * P
        dstc = ring[:, 0:CB * P].bitcast(I32).rearrange("p (b e) -> p b e", b=CB)
        msgs = ring[:, 0:U * F].rearrange("p (k f) -> p k f", k=U)
        coef = ring[:, U * F:U * (F + P)].rearrange("p (k q) -> p k q", k=U)
        cmax = sb("cmax", [P, CB])
        cmin = sb("cmin", [P, CB])
        vmax = sb("vmax", [P, 2 * T])
        vred = sb("vred", [2 * T, 1])
        brow = sb("brow", [1, 2 * T])
        bnd = sb("bnd", [1, 2, T], I32)
        bndf = sb("bndf", [1, 2, T])
        total_i = sb("total_i", [1, 1], I32)
        src_e = sb("src_e", [P, U], I32)
        dst_e = sb("dst_e", [P, U], I32)
        w_e = sb("w_e", [P, U])
        src_row = sb("src_row", [P, P * U], I32)
        srcf = sb("srcf", [P, U])
        dstf = sb("dstf", [P, U])
        reads = sb("reads", [P, U, P])
        same = sb("same", [P, U, P])
        indA, indB = (b[:].rearrange("p k e -> p (k e)")[:, 0:T * CB].rearrange("p (t b) -> p t b", t=T)
                      for b in (reads, same))
        before = sb("before", [P, U])
        junk = sb("junk", [P, U, P], BF16)
        away = sb("away", [P, U])
        idxf = sb("idxf", [P, U])
        idx_now = sb("idx_now", [P, U])
        idx = sb("idx", [P, U], I32)
        qmin = sb("qmin", [P, FC, P])
        qexp = sb("qexp", [P, FC, P])
        qelu = sb("qelu", [P, FC, P])
        rden = sb("rden", [P, FC, HPC])
        msg = sb("msg", [P, F])
        msgT = sb("msgT", [P, FC, P])
        lnst, lnmv, lnve, lnln, lny, lna, lnr = (
            {p: sb(f"ln{name}_{p}", [P, w]) for p in "mh"}
            for name, w in (("st", 6), ("mv", 2), ("ve", 1), ("ln", 1), ("y", 1), ("a", 1), ("r", 1)))
        mrow = sb("mrow", [P, F])
        hrow = sb("hrow", [P, F])
        mT = sb("mT", [P, FC, P])
        hT = sb("hT", [P, HC, P])
        SLOTS = 6
        assert T % SLOTS == 1 and SLOTS % 2 == 0
        parts = xn[:].rearrange("p t f -> p (t f)")[:, 0:SLOTS * NACC * F].rearrange(
            "p (s k f) -> p s k f", s=SLOTS, k=NACC)
        KEPT = NACC // 2
        assert NACC % 2 == 1
        aggT = sb("aggT", [P, 2, FC, P])
        xn2 = sb("xn2", [P, 2, F])
        TE = T * NE
        logits = sb("logits", [P, T, NE])
        hot = sb("hot", [P, 2, T, NE])
        hots = sb("hots", [P, T, NE])
        work = sb("work", [P, 2, T, NE])
        best = sb("best", [P, 2, T])
        which = sb("which", [P, T])
        wts = sb("wts", [P, T, 2])
        slotf = sb("slotf", [P, T, 2])
        slotc = sb("slotc", [P, T, 2])
        slot_now = sb("slot_now", [P, 2, 2], I32)
        lastcnt = sb("lastcnt", [P, NE])
        cnt = sb("cnt", [P, NE])
        cnti = sb("cnti", [P, NE], I32)
        nblk = sb("nblk", [P, NE])
        cum = sb("cum", [P, NE])
        delta = sb("delta", [P, NE])
        one8 = sb("one8", [P, NE])
        le, lenb = (b[0:1].rearrange("p s f -> p (s f)")[:, 0:(MAXBLK + 1) * NE].rearrange("p (m e) -> p m e", e=NE)
                    for b in (kmin, kexp))
        be = sb("be", [1, MAXBLK + 1])
        bprev = sb("bprev", [1, MAXBLK + 1])
        bstart = sb("bstart", [1, MAXBLK + 1])
        btab = sb("btab", [1, 2, MAXBLK + 1], I32)
        ztab = sb("ztab", [1, NE + 1], I32)
        pA = ps("A", [P, 512])
        pT = ps("T", [P, 512])
        pQ = ps("Q", [P, 512])
        pM = ps("M", [P, 512])
        pH = ps("H", [P, 512])
        pY = ps("Y", [P, 512])
        pG = ps("G", [P, 512])
        pR = ps("R", [P, 512])

        pC, pX = (pA, pY), (pG, pR)
        consts_made = sem("consts_made")
        spacer = sem("spacer")
        pads_made = sem("pads_made")
        x_zeroed = sem("x_zeroed")
        XCH = 12
        nxc = (T - 1) // XCH
        assert nxc * XCH == T - 1
        x_loaded = [sem(f"x_loaded{k}") for k in range(nxc + 1)]
        kv_weights = sem("kv_weights")
        weights = sem("weights")
        edges_padded = sem("edges_padded")
        chunks_zeroed = sem("chunks_zeroed")
        chunks_loaded = sem("chunks_loaded")
        prefix_kept = sem("prefix_kept")
        zero_made = sem("zero_made")
        sums_zeroed = sem("sums_zeroed")
        dve1 = Steps(sem("dve_norm"), "stats")
        dve2 = Steps(sem("dve_rstd"), "msum mean dif m2 dif2 dif4 var ve a nr y rstd")
        act2 = Steps(sem("act_rstd"), "ln exp")
        PT = Steps(sem("pe_trans"), "trans")
        PK = Steps(sem("pe_kv"), "kv")
        PKA = Steps(sem("pe_kvacc"), "kvacc")
        DN = Steps(sem("dve_rows"), "norm")
        DS = Steps(sem("dve_colstats"), "cstat0 cstat1")
        DK = Steps(sem("dve_kv"), "kmin kelu")
        GK = Steps(sem("pool_kv"), "keep res")
        AX = Steps(sem("act_xnT"), "xnT")
        AK = Steps(sem("act_kv"), "kexp vcopy")
        dve3 = Steps(sem("dve_cols"), "aggr0 aggr1 std inv wgs0 wgs1 dm0 dm1 meanbc "
                                      "kv0 kv1 ks0 ks1 gb")
        cen_made = sem("rows_centred")
        act3 = Steps(sem("act_cols"), "sqrt")
        pe3 = Steps(sem("pe_cols"), "params mean")
        ccopy = sem("params_copied")
        dveb = Steps(sem("dve_span"), "cmax cmin indA indB ind vhi vmaxhi vlo vmaxlo vred row "
                                      "hi1 lo1 hi2 lo2 n1 n2 mul elo ielo in shr min totf tot toti")
        peb = Steps(sem("pe_span"), "t1 t2")
        row_loaded = sem("row_loaded")
        ends_loaded = sem("ends_loaded")
        floats_made = sem("floats_made")
        same_made = sem("same_made")
        reads_made = sem("reads_made")
        counted = sem("counted")
        idx_float = sem("idx_float")
        idx_taken = sem("idx_taken")
        idx_ready = sem("idx_ready")
        coef_done = sem("coef_done")
        coef_copied = sem("coef_copied")
        NPAIR = (U + 1) // 2
        msg_done = sem("msg_done")
        msg_copied = sem("msg_copied")
        HALVES = (range(0, 4), range(4, U))
        PAIRS = [range(2 * j, min(2 * j + 2, U)) for j in range(NPAIR)]
        landed = sem("landed")
        assert AHEAD + 1 < U
        scattered = [sem(f"scattered{k}") for k in range(U)]
        LN = "st ag ve a nr r ap"
        ln = lambda p: " ".join(p + s for s in LN.split())
        PM = Steps(sem("pe_mixer"), "xT q num msgT mm mT hid0 hid1")
        PH = Steps(sem("pe_mlp"), "h2")
        DXS = Steps(sem("dve_mixer_rows"), "xs")
        DM = Steps(sem("dve_mixer"), "idrow qmin qelu eps rden msg " + ln("m"))
        DH = Steps(sem("dve_mlp"), ln("h") + " g2 b2 res")
        AM = Steps(sem("act_mixer"), "xT qexp msgT mln mexp mT0 mT1")
        AH = Steps(sem("act_mlp"), "relu hln hexp")
        parts_loaded = [sem(f"parts_loaded{j}") for j in range(SLOTS // 2)]
        GG = Steps(sem("pool_gnn_add"), "add")
        DA = Steps(sem("dve_gnn_add"), "add")
        PG = Steps(sem("pe_gnnT"), "aggT")
        PG2 = Steps(sem("pe_gnn"), "gnn")
        AG = Steps(sem("act_gnn"), "aggT")
        DG = Steps(sem("dve_gnn"), "res stats")
        RS = "msum mean dif m2 dif2 dif4 var ve a nr y rstd"
        dveo, acto = Steps(sem("dve_rstd_o"), RS), Steps(sem("act_rstd_o"), "ln exp")
        dvei, acti = Steps(sem("dve_rstd_i"), RS), Steps(sem("act_rstd_i"), "ln exp")
        DR = Steps(sem("dve_router"), "xt stats")
        GR = Steps(sem("pool_router"), "keep")
        PRT = Steps(sem("pe_routerT"), "xT")
        PR_ = Steps(sem("pe_router"), "log")
        ART = Steps(sem("act_routerT"), "xT")
        AR = Steps(sem("act_router"), "log")
        dver = Steps(sem("dve_top2"), "br b0 e0 r0 w0 h0 p0 l1 b1 e1 r1 w1 h1 dif den wa wb v0 v1 sum tot "
                     "s1 s2 s4 s8 s16 s32 sub rank base p0x s0x p1x s1x last")
        actr = Steps(sem("act_top2"), "exp")
        per = Steps(sem("pe_rank"), "rank tot")
        DD = Steps(sem("dve_dispatch"), "xn2 slot")
        dispatched = [sem("dispatched0"), sem("dispatched1")]
        dve5 = Steps(sem("dve_blocks"), "cnt c255 ci sh nb cum le lenb be bprev st1 st2 bemax itab ibe izt inb")
        dve6 = Steps(sem("dve_slots"), "excl rows delta hot0 hot1 shift slot")
        all_scattered = sem("all_scattered")
        zero_rows = sem("zero_rows")
        zero_outs = sem("zero_outs")
        outs_zeroed = sem("outs_zeroed")
        ew1_loaded = sem("ew1_loaded")
        ew2_loaded = sem("ew2_loaded")
        eb2_loaded = sem("eb2_loaded")
        xb_loaded = sem("xb_loaded")
        PT_ = Steps(sem("pe_rowsT"), "t0 t1")
        PE_ = Steps(sem("pe_experts"), " ".join(f"h{j}" for j in range(EHC)) + " y0 y1")
        DX = Steps(sem("dve_rowsT"), "x0 x1")
        DE = Steps(sem("dve_experts"), "y0 y1")
        AE = Steps(sem("act_experts"), " ".join(f"g{j}" for j in range(EHC)))
        out_rows = sem("out_rows")
        DI = Steps(sem("dve_out_idx"), "idx")
        DC = Steps(sem("dve_combine"), "a b")
        got = [[sem(f"got{s}{j}") for j in range(2)] for s in range(SLOTS)]
        stored = [sem(f"stored{s}") for s in range(SLOTS)]

        xn_flat, used = xn[:].rearrange("p t f -> p (t f)"), [0]

        def over_xn(n):
            used[0] += n
            assert used[0] <= T * F
            return xn_flat[:, used[0] - n:used[0]]

        ew1 = over_xn(FC * EH).rearrange("p (c h) -> p c h", c=FC)
        ew2 = over_xn(EHC * F).rearrange("p (j f) -> p j f", j=EHC)
        ehT = over_xn(EHC * BLK).rearrange("p (j q) -> p j q", j=EHC)
        xeT = over_xn(FC * BLK).rearrange("p (c q) -> p c q", c=FC)
        xb = over_xn(BM * F).rearrange("p (m f) -> p m f", m=BM)
        yb = over_xn(BM * F).rearrange("p (m f) -> p m f", m=BM)
        eb2_bc = over_xn(F)
        yg = over_xn(SLOTS * 2 * F).rearrange("p (s j f) -> p s j f", s=SLOTS, j=2)
        idx_c = sb("idx_c", [P, SLOTS, 2], I32)
        ob = over_xn(SLOTS * F).rearrange("p (s f) -> p s f", s=SLOTS)

        def apart(engine):
            engine.sem_inc(spacer, 1)

        def tile(buf, t):
            return buf[:, t, :] if isinstance(t, int) else buf[:, bass.ds(t, 1), :]

        def col(buf, t):
            return buf[:, t:t + 1] if isinstance(t, int) else buf[:, bass.ds(t, 1)]

        block = ctx.enter_context(nc.Block())

        @block.sync
        def _(sp):
            xr = x[0:(T - 1) * P, :].rearrange("(t p) f -> p t f", p=P)
            for k in range(nxc):
                sp.dma_start(x1[:, k * XCH:(k + 1) * XCH, :], xr[:, k * XCH:(k + 1) * XCH, :]).then_inc(x_loaded[k], 16)
            sp.wait_ge(x_zeroed, 1)
            sp.dma_start(x1[0:TAIL, T - 1, :], x[(T - 1) * P:N, :]).then_inc(x_loaded[nxc], 16)
            sp.dma_start(wkv[:, :, 0:F], Wk.rearrange("(c p) n -> p c n", p=P)).then_inc(kv_weights, 16)
            sp.dma_start(wkv[:, :, F:2 * F], Wv.rearrange("(c p) n -> p c n", p=P)).then_inc(kv_weights, 16)
            g = 15
            for d, s in ((src_d, src), (dst_d, dst), (w_d, edge_weight)):
                sp.dma_start(d[0:E].rearrange("(g e) -> g e", g=g), s.rearrange("(g e) -> g e", g=g)).then_inc(edges_padded, 16)
            sp.wait_ge(pads_made, 2)
            for d, b in ((src_d, padz[:]), (dst_d, padi[:]), (w_d, padz[:].bitcast(F32))):
                sp.dma_start(d[E:EPAD].rearrange("(p e) -> p e", p=PADP), b).then_inc(edges_padded, 16)
            for b, w in ((wq, Wq), (wm, Wm), (w1, W1), (w2, W2), (wg, gnn_W), (wr, Wr)):
                sp.dma_start(b[:], w.rearrange("(c p) n -> p c n", p=P)).then_inc(weights, 16)
            sp.dma_start(rows_p[R_B1:R_G, :], eb1.rearrange("e (j p) -> (e j) p", p=P)).then_inc(weights, 16)
            sp.dma_start(rows_p[R_G:R_B, :], ln_g.rearrange("e (j p) -> (e j) p", p=P)).then_inc(weights, 16)
            sp.dma_start(rows_p[R_B:R_G1, :], ln_b.rearrange("e (j p) -> (e j) p", p=P)).then_inc(weights, 16)
            sp.dma_start(rows_p[R_G1:R_BB1, :], g1.rearrange("(j p) -> j p", p=P)).then_inc(weights, 16)
            sp.dma_start(rows_p[R_BB1:PR, :], b1.rearrange("(j p) -> j p", p=P)).then_inc(weights, 16)
            for b, v in ((g2_bc, g2), (bias_bc, b2), (gb_bc, gnn_b), (br_bc, br)):
                sp.dma_start(b[:], v.partition_broadcast(P)).then_inc(weights, 16)
            sp.wait_ge(edges_padded, 6 * 16)
            sp.wait_ge(chunks_zeroed, 1)
            full = CH // P
            sp.dma_start(dstc[:, 0:full, :], dst_d[0:full * P * P].rearrange("(b p e) -> p b e", p=P, e=P)).then_inc(chunks_loaded, 16)
            sp.dma_start(dstc[0:CH - full * P, full, :],
                         dst_d[full * P * P:CH * P].rearrange("(p e) -> p e", e=P)).then_inc(chunks_loaded, 16)
            sp.wait_ge(zero_made, 1)
            for a in sums:
                n2 = AROWS // (2 * P)
                sp.dma_start(a.rearrange("(p j m) f -> p j (m f)", p=P, m=2),
                             zrows[:].unsqueeze(1).to_broadcast([P, n2, 2 * F])).then_inc(sums_zeroed, 16)
            sp.wait_ge(*dveb.done(0, "toti"))
            groups = sp.alloc_register("sp_groups")
            first_edge = sp.alloc_register("sp_first_edge")
            sp.reg_mov(groups, 0)
            with sp.Fori(0, T) as t:
                e0 = sp.value_load(bnd[0:1, 0, bass.ds(t, 1)], min_val=0, max_val=CH * P)
                n = sp.value_load(bnd[0:1, 1, bass.ds(t, 1)], min_val=NG, max_val=-(-CH // U))
                sp.reg_mov(first_edge, e0)
                g0 = sp.snap(groups)
                with sp.Fori(0, n) as i:
                    eg = sp.snap(first_edge, min_val=0, max_val=EPAD - U * P)
                    at = bass.ds(eg, U * P)
                    sp.wait_ge(same_made, (g0 + i) * U + 1)
                    apart(sp)
                    sp.dma_start(src_row[:], src_d[at].partition_broadcast(P)).then_inc(row_loaded, 16)
                    sp.wait_ge(reads_made, (g0 + i) * U + 1)
                    apart(sp)
                    for b, d in ((src_e, src_d), (dst_e, dst_d), (w_e, w_d)):
                        sp.dma_start(b[:], d[at].rearrange("(p k) -> p k", k=U)).then_inc(ends_loaded, 16)
                    sp.reg_add(first_edge, first_edge, U * P)
                sp.reg_add(groups, groups, n)
            sp.wait_ge(all_scattered, 1)
            def load_parts(t, s, tiles=2):
                rows = bass.ds(t * P, tiles * P) if not isinstance(t, int) else slice(t * P, (t + tiles) * P)
                for k in range(NACC):
                    sp.dma_start(parts[:, s:s + tiles, k, :],
                                 sums[k][rows, :].rearrange("(s p) f -> p s f", p=P)).then_inc(parts_loaded[s // 2], 16)

            for s in range(0, SLOTS, 2):
                load_parts(s, s)
            with sp.Fori(1, T // SLOTS) as i:
                for s in range(0, SLOTS, 2):
                    sp.wait_ge(*PG.done(SLOTS * (i - 1) + s + 1, "aggT"))
                    load_parts(SLOTS * i + s, s)
            sp.wait_ge(*PG.done(T - 1 - SLOTS, "aggT"))
            load_parts(T - 1, 0, tiles=1)
            sp.wait_ge(*dve5.done(0, "inb"))
            sp.wait_ge(dispatched[0], 2 * 16 * (T // 2 + 1))
            sp.wait_ge(dispatched[1], 2 * 16 * (T // 2))
            for e in range(NE):
                z0 = sp.value_load(ztab[0:1, e:e + 1], min_val=0, max_val=NE * REG - BLK)
                sp.dma_start(erows[bass.ds(z0, BLK), :].rearrange("(p m) f -> p (m f)", m=BM), zrows[:]).then_inc(zero_rows, 16)
            sp.wait_ge(zero_rows, NE * 16)
            nb = sp.value_load(ztab[0:1, NE:NE + 1], min_val=1, max_val=MAXBLK)

            def load_rows(b):
                r0 = sp.value_load(btab[0:1, 0, bass.ds(b, 1)], min_val=0, max_val=NE * REG - BLK)
                sp.wait_ge(*PT_.done(b - 1, "t1"))
                sp.dma_start(xb[:], erows[bass.ds(r0, BLK), :].rearrange("(m p) f -> p m f", p=P)).then_inc(xb_loaded, 16)

            load_rows(0)
            with sp.Fori(0, nb) as b:
                e = sp.value_load(btab[0:1, 1, bass.ds(b, 1)], min_val=0, max_val=NE - 1)
                sp.wait_ge(*PE_.done(b - 1, f"h{EHC - 1}"))
                sp.dma_start(ew1[:], eW1[bass.ds(e, 1)].rearrange("e (c p) h -> p (e c) h", p=P)).then_inc(ew1_loaded, 16)
                load_rows(b + 1)
                sp.wait_ge(*DE.done(b - 1, "y1"))
                sp.dma_start(ew2[:], eW2[bass.ds(e, 1)].rearrange("e (j p) f -> p (e j) f", p=P)).then_inc(ew2_loaded, 16)
                sp.dma_start(eb2_bc[:], eb2[bass.ds(e, 1), :].rearrange("e f -> (e f)").partition_broadcast(P)).then_inc(eb2_loaded, 16)
            zeroed = sp.alloc_register("sp_zeroed")
            sp.reg_mov(zeroed, 0)
            with sp.Fori(nb, MAXBLK + 1) as b:
                sp.reg_add(zeroed, zeroed, 16)
                sp.dma_start(eouts[bass.ds(b * BLK, BLK), :].rearrange("(p m) f -> p (m f)", m=BM), zrows[:]).then_inc(zero_outs, 16)
            sp.wait_ge(zero_outs, sp.snap(zeroed, min_val=16, max_val=16 * (MAXBLK + 1)))
            sp.sem_inc(outs_zeroed, 1)
            with sp.Fori(0, T // SLOTS) as i:
                for s in range(SLOTS):
                    sp.wait_ge(*DC.done(SLOTS * i + s, "b"))
                    sp.dma_start(out[bass.ds((SLOTS * i + s) * P, P), :], ob[:, s]).then_inc(stored[s], 16)
            sp.wait_ge(*DC.done(T - 1, "b"))
            sp.dma_start(out[(T - 1) * P:N, :], ob[0:TAIL, 0]).then_inc(stored[0], 16)
            for s in range(SLOTS):
                sp.wait_ge(stored[s], 16 * (T // SLOTS + (s == 0)) + 1)

        @block.gpsimd
        def _(pool):
            g = nc.gpsimd
            chain = sem("pool_chain")
            made = [0]

            def link(ins):
                made[0] += 1
                ins.then_inc(chain, 1)
                pool.wait_ge(chain, made[0])

            pool.sem_inc(landed, 2 * U)
            g.memset(x1[:, T - 1, :], 0.0).then_inc(x_zeroed, 1)
            g.memset(padz[:], 0).then_inc(pads_made, 1)
            g.memset(padi[:], PADDST).then_inc(pads_made, 1)
            g.memset(dstc[:, CB - 1, :], PADDST).then_inc(chunks_zeroed, 1)
            link(g.memset(ident[:], 0.0))
            link(g.affine_select(out=ident[:], in_=ident[:], compare_op=ALU.not_equal, fill=1.0, base=0,
                                 pattern=[[-1, P]], channel_multiplier=1))
            link(g.memset(tri[:], 0.0))
            link(g.affine_select(out=tri[:], in_=tri[:], compare_op=ALU.is_ge, fill=1.0, base=0,
                                 pattern=[[-1, P]], channel_multiplier=1))
            link(g.memset(hmask[:], 1.0))
            link(g.affine_select(out=hmask[:], in_=hmask[:], compare_op=ALU.is_ge, fill=0.0, base=0,
                                 pattern=[[-HD, HPC]], channel_multiplier=1))
            link(g.affine_select(out=hmask[:], in_=hmask[:], compare_op=ALU.is_ge, fill=0.0, base=HD - 1,
                                 pattern=[[HD, HPC]], channel_multiplier=-1))
            link(g.memset(bdmask[:], 1.0))
            link(g.affine_select(out=bdmask[:], in_=bdmask[:], compare_op=ALU.is_ge, fill=0.0, base=0,
                                 pattern=[[-HD, HPC], [0, HD]], channel_multiplier=1))
            link(g.affine_select(out=bdmask[:], in_=bdmask[:], compare_op=ALU.is_ge, fill=0.0, base=HD - 1,
                                 pattern=[[HD, HPC], [0, HD]], channel_multiplier=-1))
            link(g.memset(valid[:], 1.0))
            link(g.affine_select(out=valid[:], in_=valid[:], compare_op=ALU.is_ge, fill=0.0, base=N - 1,
                                 pattern=[[-P, T]], channel_multiplier=-1))
            g.memset(ones[:], 1.0)
            g.memset(zrows[:], 0.0).then_inc(zero_made, 1)
            link(g.memset(trilow[:], 0.0))
            link(g.affine_select(out=trilow[:], in_=trilow[:], compare_op=ALU.is_ge, fill=1.0, base=0,
                                 pattern=[[1, P]], channel_multiplier=-1))
            g.memset(one8[:], 1.0)
            io = dict(allow_small_or_imprecise_dtypes=True)
            g.iota(idrow[:], [[1, P]], base=-P, channel_multiplier=0, **io)
            g.iota(down8[:], [[-1, NE]], base=NE, channel_multiplier=0, **io)
            g.iota(ebase[:], [[REG, NE]], base=0, channel_multiplier=0, **io)
            g.iota(dummy[:], [[0, U]], base=N, channel_multiplier=1, **io)
            g.iota(cidx[:], [[P, CB]], base=1, channel_multiplier=1, **io)
            g.iota(cinv[:], [[-P, CB]], base=BIG, channel_multiplier=-1, **io)
            g.iota(tlo[:], [[P, T]], base=0, channel_multiplier=0, **io)
            g.iota(thi[:], [[P, T]], base=P - 1, channel_multiplier=0, **io)
            g.iota(bidx[:], [[1, MAXBLK + 1]], base=0, channel_multiplier=0, **io).then_inc(consts_made, 1)

            GK.first(pool)

            def kv_tile(t, s):
                flat = (lambda z: z) if isinstance(t, int) else (lambda z: z.rearrange("p a f -> p (a f)"))
                pool.wait_ge(*DN.done(t, "norm"))
                g.tensor_copy(flat(tile(xn, t)), xs[:, s, :]).then_inc(*GK("keep"))
                g.tensor_tensor(flat(tile(x1, t)), flat(tile(x1, t)), xs[:, s, :], ALU.add).then_inc(*GK("res"))

            with pool.Fori(0, T // 2) as i:
                for s in range(2):
                    kv_tile(2 * i + s, s)
            kv_tile(T - 1, 0)

            pool.wait_ge(sums_zeroed, 16 * NACC)
            pool.wait_ge(*dveb.done(0, "toti"))
            total = pool.value_load(total_i[0:1, 0:1], min_val=NG * T, max_val=T * -(-CH // U))

            def scatter(i, first=False):
                for k in range(U):
                    if k >= AHEAD:
                        pool.wait_ge(scattered[k - AHEAD], i * 16 + 16)
                        pool.sem_inc(landed, 1)
                    elif not first:
                        pool.wait_ge(scattered[k - AHEAD + U], i * 16)
                        pool.sem_inc(landed, 1)
                    if k % 2 == 0:
                        pool.wait_ge(idx_ready, i * NPAIR + k // 2 + 2)
                        apart(pool)
                        pool.wait_ge(msg_copied, i * NPAIR + NPAIR + k // 2 + 1)
                        apart(pool)
                    g.indirect_dma_start(sums[k], bass.IndirectOffsetOnAxis(ap=idx[:, k:k + 1], axis=0),
                                         msgs[:, k, :], None, compute_op=ALU.add).then_inc(scattered[k], 16)

            scatter(0, first=True)
            with pool.Fori(1, total) as i:
                scatter(i)
            for k in range(U):
                pool.wait_ge(scattered[k], total * 16)
                apart(pool)
            pool.sem_inc(all_scattered, 1)
            GG.first(pool)

            def add_last(s, turn):
                pool.wait_ge(parts_loaded[s // 2], 16 * NACC * (turn + 1))
                g.tensor_tensor(parts[:, s, NACC - 2, :], parts[:, s, NACC - 2, :], parts[:, s, NACC - 1, :],
                                ALU.add).then_inc(*GG("add"))

            with pool.Fori(0, T // SLOTS) as i:
                for s in range(SLOTS):
                    add_last(s, i)
            add_last(0, T // SLOTS)
            GR.first(pool)

            def keep(t, s):
                pool.wait_ge(*DR.done(t, "xt"))
                g.tensor_copy(tile(xn, t) if isinstance(t, int) else tile(xn, t).rearrange("p a f -> p (a f)"),
                              xs[:, s, :]).then_inc(*GR("keep"))

            with pool.Fori(0, T // 2) as i:
                for s in range(2):
                    keep(2 * i + s, s)
            keep(T - 1, 0)

            def dispatch(t, s, rows):
                pool.wait_ge(*DD.done(t, "slot"))
                apart(pool)
                for j in range(2):
                    g.indirect_dma_start(
                        erows, bass.IndirectOffsetOnAxis(ap=slot_now[0:rows, s, j:j + 1], axis=0),
                        xn2[0:rows, s, :], None).then_inc(dispatched[s], 16)

            with pool.Fori(0, T // 2) as i:
                for s in range(2):
                    dispatch(2 * i + s, s, P)
            dispatch(T - 1, 0, TAIL)

            pool.wait_ge(*dve5.done(0, "inb"))
            nb = pool.value_load(ztab[0:1, NE:NE + 1], min_val=1, max_val=MAXBLK)
            pool.wait_ge(outs_zeroed, 1)
            pool.wait_ge(out_rows, nb * 16 + 1)
            apart(pool)

            def fetch(t, s, rows):
                pool.wait_ge(*DI.done(t, "idx"))
                apart(pool)
                for j in range(2):
                    g.indirect_dma_start(
                        yg[0:rows, s, j, :], None, eouts,
                        bass.IndirectOffsetOnAxis(ap=idx_c[0:rows, s, j:j + 1], axis=0)).then_inc(got[s][j], 16)

            with pool.Fori(0, T // SLOTS) as i:
                for s in range(SLOTS):
                    fetch(SLOTS * i + s, s, P)
            fetch(T - 1, 0, TAIL)

        @block.tensor
        def _(pe):
            for st in (PT, PK, PKA, pe3, PM, PH, PT_, PE_, peb, PG, PG2, PRT, PR_, per):
                st.first(pe)
            mm = nc.tensor.matmul
            pe.sem_inc(coef_done, 2)
            pe.sem_inc(msg_done, NPAIR)
            pe.wait_ge(consts_made, 1)
            pe.wait_ge(kv_weights, 32)

            def turn_rows(t, s):
                pe.wait_ge(*DN.done(t, "norm"))
                pe.wait_ge(*AX.done(t - 2, "xnT"))
                pe.wait_ge(*DS.done(t - 2, "cstat1"))
                for c in range(FC):
                    last_ = nc.tensor.transpose((pT, pA)[s][:, c * P:(c + 1) * P], xs[:, s, c * P:(c + 1) * P], ident[:])
                last_.then_inc(*PT("trans"))

            def project(t, s):
                pe.wait_ge(*AX.done(t, "xnT"))
                pe.wait_ge(*AK.done(t - 2, "vcopy"))
                pe.wait_ge(*DK.done(t - 2, "kelu"))
                for c in range(FC):
                    last_ = mm((pQ, pM)[s][:], xnT[:, s, c, :], wkv[:, c, :], start=(c == 0), stop=(c == FC - 1))
                last_.then_inc(*PK("kv"))

            def accumulate(t, s, first=False, last=False):
                pe.wait_ge(*DK.done(t, "kelu"))
                pe.wait_ge(*AK.done(t, "vcopy"))
                for c in range(FC):
                    last_ = mm((pG, pH)[c][:, 0:P + 1], kelu[:, s, c * P:(c + 1) * P], vaug[:, s, c, :],
                               start=first, stop=last)
                last_.then_inc(*PKA("kvacc"))

            turn_rows(0, 0)
            turn_rows(1, 1)
            project(0, 0)
            turn_rows(2, 0)
            project(1, 1)
            accumulate(0, 0, first=True)
            with pe.Fori(0, (T - 3) // 2) as i:
                for s in range(2):
                    turn_rows(2 * i + s + 3, 1 - s)
                    project(2 * i + s + 2, s)
                    accumulate(2 * i + s + 1, 1 - s)
            project(T - 1, 0)
            accumulate(T - 2, 1)
            accumulate(T - 1, 0, last=True)

            pe.wait_ge(weights, 16 * 15)
            nc.tensor.transpose(pR[:, 0:PR], rows_p[:], ident[0:PR, 0:PR]).then_inc(*pe3("params"))
            pe.wait_ge(*dve3.done(0, "dm1"))
            for c in range(FC):
                last_ = mm(pY[:, c * P:(c + 1) * P], ones[:], dmean[:, c, :], start=True, stop=True)
            last_.then_inc(*pe3("mean"))
            pe.wait_ge(*dveb.done(0, "vmaxlo"))
            nc.tensor.transpose(pA[0:2 * T, 0:P], vmax[:], ident[:]).then_inc(*peb("t1"))
            pe.wait_ge(*dveb.done(0, "vred"))
            nc.tensor.transpose(pA[0:1, 256:256 + 2 * T], vred[:], ident[0:2 * T, 0:2 * T]).then_inc(*peb("t2"))

            pe.wait_ge(*dveb.done(0, "toti"))
            pe.wait_ge(*dve3.done(0, "gb"))
            pe.wait_ge(ccopy, 1)
            groups = pe.alloc_register("pe_groups")
            pe.reg_mov(groups, 0)
            W_ = P + HPC

            def turn(src_, step):
                for c in range(FC):
                    last_ = nc.tensor.transpose(pT[:, c * P:(c + 1) * P], src_[:, c * P:(c + 1) * P], ident[:])
                last_.then_inc(*PM(step))

            def step_xT(t):
                pe.wait_ge(*DXS.done(t, "xs"))
                pe.wait_ge(*AM.done(t - 1, "mT1"))
                turn(xs[:, 0, :], "xT")

            def step_q(t):
                pe.wait_ge(*AM.done(t, "xT"))
                pe.wait_ge(*DM.done(t - 1, "map"))
                for o in range(FC):
                    for c in range(FC):
                        last_ = mm(pQ[:, o * P:(o + 1) * P], wq[:, c, o * P:(o + 1) * P], xnT[:, 0, c, :],
                                   start=(c == 0), stop=(c == FC - 1))
                last_.then_inc(*PM("q"))

            def step_num(t):
                pe.wait_ge(*DM.done(t, "qelu"))
                for c in range(FC):
                    last_ = mm(pM[:, c * W_:(c + 1) * W_], qelu[:, c, :], kvbd[:, c, :], start=True, stop=True)
                last_.then_inc(*PM("num"))

            def step_msgT(t):
                pe.wait_ge(*DM.done(t, "msg"))
                turn(msg[:], "msgT")

            def step_mm(t):
                pe.wait_ge(*AM.done(t, "msgT"))
                for c in range(FC):
                    last_ = mm(pQ[:, 0:F], msgT[:, c, :], wm[:, c, :], start=(c == 0), stop=(c == FC - 1))
                last_.then_inc(*PM("mm"))

            def step_mT(t):
                pe.wait_ge(*DM.done(t, "map"))
                turn(mrow[:], "mT")

            def step_hid(t, half):
                pe.wait_ge(*AM.done(t, "mT1"))
                pe.wait_ge(*DH.done(t - 1, "hap"))
                for o in range(half * HC // 2, (half + 1) * HC // 2):
                    for c in range(2 * FC):
                        r = xnT[:, 0, c, :] if c < FC else mT[:, c - FC, :]
                        last_ = mm(pH[:, o * P:(o + 1) * P], w1[:, c, o * P:(o + 1) * P], r,
                                   start=(c == 0), stop=(c == 2 * FC - 1))
                last_.then_inc(*PM(f"hid{half}"))

            def step_h2(t):
                pe.wait_ge(*AH.done(t, "relu"))
                for c in range(HC):
                    last_ = mm(pH[:, 0:F], hT[:, c, :], w2[:, c, :], start=(c == 0), stop=(c == HC - 1))
                last_.then_inc(*PH("h2"))

            def coefs(g, half):
                ks = HALVES[half]
                if half == 0:
                    pe.wait_ge(same_made, g * U + U + 1)
                pe.wait_ge(reads_made, g * U + ks[-1] + 2)
                pe.wait_ge(coef_copied, g * 2 + half + 1)
                for k in ks:
                    last_ = mm(pC[half][:, (k - ks[0]) * P:(k - ks[0] + 1) * P], reads[:, k, :], same[:, k, :],
                               start=True, stop=True)
                last_.then_inc(coef_done, 1)

            def messages(begun, t, half):
                pe.wait_ge(coef_copied, begun * 2 + half + 1)
                for j in (2 * half, 2 * half + 1):
                    pe.wait_ge(msg_copied, begun * NPAIR + j - 1)
                    for k in PAIRS[j]:
                        last_ = mm(pX[j % 2][:, (k % 2) * F:(k % 2 + 1) * F], coef[:, k, :],
                                   tile(xn, t).rearrange("p a f -> p (a f)"), start=True, stop=True)
                    last_.then_inc(msg_done, 1)

            before_coefs = {0: step_xT, 2: step_msgT, 4: lambda t: step_hid(t, 0)}
            after_first = {0: step_q, 1: step_num, 2: step_mm}
            before_msgs = {3: step_mT, 4: lambda t: step_hid(t, 1)}
            prev = pe.alloc_register("pe_prev_tile")
            pe.reg_mov(prev, 0)
            with pe.Fori(0, T) as t:
                g0 = pe.snap(groups)
                for i in range(NG):
                    if i in before_coefs:
                        before_coefs[i](t)
                    coefs(g0 + i, 0)
                    if i in after_first:
                        after_first[i](t)
                    if i == 0:
                        with pe.If(t > 0):
                            step_h2(pe.snap(prev, min_val=0, max_val=T - 1))
                    if i:
                        messages(g0 + i, t, 1)
                    else:
                        with pe.If(t > 0):
                            messages(g0, pe.snap(prev, min_val=0, max_val=T - 1), 1)
                    coefs(g0 + i, 1)
                    if i in before_msgs:
                        before_msgs[i](t)
                    messages(g0 + (i + 1), t, 0)
                n = pe.value_load(bnd[0:1, 1, bass.ds(t, 1)], min_val=NG, max_val=-(-CH // U))
                with pe.If(n > NG):
                    with pe.Fori(NG, n) as i:
                        coefs(g0 + i, 0)
                        messages(g0 + i, t, 1)
                        coefs(g0 + i, 1)
                        messages(g0 + i + 1, t, 0)
                pe.reg_add(groups, groups, n)
                pe.reg_mov(prev, t)
            step_h2(T - 1)
            messages(pe.snap(groups), pe.snap(prev, min_val=0, max_val=T - 1), 1)

            pe.wait_ge(*DH.done(T - 1, "res"))

            def gnn_T(t, s):
                pe.wait_ge(*DA.done(t, "add"))
                pe.wait_ge(*AG.done(t - 2, "aggT"))
                for c in range(FC):
                    for k in range(KEPT):
                        last_ = mm((pT, pQ)[s % 2][:, c * P:(c + 1) * P], parts[:, s, k, c * P:(c + 1) * P], ident[:],
                                   start=(k == 0), stop=(k == KEPT - 1))
                last_.then_inc(*PG("aggT"))

            def gnn_W_(t, s):
                pe.wait_ge(*AG.done(t, "aggT"))
                pe.wait_ge(*DG.done(t - 2, "res"))
                for c in range(FC):
                    last_ = mm((pM, pH)[s % 2][:, 0:F], aggT[:, s % 2, c, :], wgs[:, c, :], start=(c == 0), stop=(c == FC - 1))
                last_.then_inc(*PG2("gnn"))

            gnn_T(0, 0)
            with pe.Fori(0, T // SLOTS) as i:
                for s in range(SLOTS):
                    if s < SLOTS - 1:
                        gnn_T(SLOTS * i + s + 1, s + 1)
                    else:
                        gnn_T(SLOTS * i + SLOTS, 0)
                    gnn_W_(SLOTS * i + s, s)
            gnn_W_(T - 1, 0)

            def route_T(t, s):
                pe.wait_ge(*DR.done(t, "xt"))
                pe.wait_ge(*ART.done(t - 2, "xT"))
                for c in range(FC):
                    last_ = nc.tensor.transpose((pT, pQ)[s][:, c * P:(c + 1) * P], xs[:, s, c * P:(c + 1) * P], ident[:])
                last_.then_inc(*PRT("xT"))

            def route(t, s):
                pe.wait_ge(*ART.done(t, "xT"))
                pe.wait_ge(*AR.done(t - 2, "log"))
                for c in range(FC):
                    last_ = mm((pM, pH)[s][:, 0:NE], aggT[:, s, c, :], wr[:, c, :], start=(c == 0), stop=(c == FC - 1))
                last_.then_inc(*PR_("log"))

            route_T(0, 0)
            with pe.Fori(0, T // 2) as i:
                for s in range(2):
                    route_T(2 * i + s + 1, 1 - s)
                    route(2 * i + s, s)
            route(T - 1, 0)
            pe.wait_ge(*dver.done(0, "sum"))
            mm(pA[:, 0:TE], tri[:], hots[:].rearrange("p t e -> p (t e)"), start=True, stop=True).then_inc(*per("rank"))
            mm(pY[:, 0:TE], ones[:], hots[:].rearrange("p t e -> p (t e)"), start=True, stop=True).then_inc(*per("tot"))

            pe.wait_ge(*dve5.done(0, "inb"))
            nb = pe.value_load(ztab[0:1, NE:NE + 1], min_val=1, max_val=MAXBLK)

            def turn_block(b):
                pe.wait_ge(xb_loaded, 16 * b + 16)
                for c in range(FC):
                    pe.wait_ge(*DX.done(b - 1, f"x{c}"))
                    for m in range(BM):
                        last_ = nc.tensor.transpose((pT, pR)[c][:, m * P:(m + 1) * P], xb[:, m, c * P:(c + 1) * P], ident[:])
                    last_.then_inc(*PT_(f"t{c}"))

            turn_block(0)
            with pe.Fori(0, nb) as b:
                pe.wait_ge(ew1_loaded, 16 * b + 16)
                pe.wait_ge(*DX.done(b, "x1"))
                for j in range(EHC):
                    if j >= 4:
                        pe.wait_ge(*AE.done(b, f"g{j - 4}"))
                    else:
                        pe.wait_ge(*AE.done(b - 1, f"g{j + 4}"))
                    for c in range(FC):
                        last_ = mm((pA, pQ, pM, pH)[j % 4][:, 0:BLK], ew1[:, c, j * P:(j + 1) * P], xeT[:, c, :],
                                   start=(c == 0), stop=(c == FC - 1))
                    last_.then_inc(*PE_(f"h{j}"))
                turn_block(b + 1)
                pe.wait_ge(ew2_loaded, 16 * b + 16)
                for m in range(BM):
                    pe.wait_ge(*DE.done(b - 1, f"y{m}"))
                    for j in range(EHC):
                        if m == 0:
                            pe.wait_ge(*AE.done(b, f"g{j}"))
                        last_ = mm((pY, pG)[m][:, 0:F], ehT[:, j, m * P:(m + 1) * P], ew2[:, j, :],
                                   start=(j == 0), stop=(j == EHC - 1))
                    last_.then_inc(*PE_(f"y{m}"))

        @block.scalar
        def _(act):
            a = nc.scalar.activation
            for st in (act2, AX, AK, act3, AM, AH, AE, AG, ART, AR, acto, acti, actr):
                st.first(act)
            act.sem_inc(coef_copied, 2)
            act.sem_inc(msg_copied, NPAIR)
            act.sem_inc(idx_ready, 1)
            act.sem_inc(idx_taken, 1)

            def all_rstd(DV, AC):
                act.wait_ge(*DV.done(0, "ve"))
                a(rrstd[:], rvar[:], ACT.Ln).then_inc(*AC("ln"))
                act.wait_ge(*AC.done(0, "ln"))
                a(rtmp[:], rrstd[:], ACT.Exp, scale=-0.5).then_inc(*AC("exp"))

            nc.scalar.preload_act_table_set("natural_log_exp_and_others")
            all_rstd(dve2, act2)

            def copy_rows(t, s):
                act.wait_ge(*PT.done(t, "trans"))
                act.wait_ge(*PK.done(t - 2, "kv"))
                a(xnT[:, s], (pT, pA)[s][:, 0:F].rearrange("p (c q) -> p c q", c=FC), ACT.Copy).then_inc(*AX("xnT"))

            def kv_tile(t, s):
                act.wait_ge(*DK.done(t, "kmin"))
                act.wait_ge(*DK.done(t - 2, "kelu"))
                a(kexp[:, s, :], kmin[:, s, :], ACT.Exp).then_inc(*AK("kexp"))
                act.wait_ge(*PKA.done(t - 2, "kvacc"))
                a(vaug[:, s, :, 0:P], (pQ, pM)[s][:, F:2 * F].rearrange("p (c q) -> p c q", c=FC),
                  ACT.Copy).then_inc(*AK("vcopy"))

            copy_rows(0, 0)
            with act.Fori(0, T // 2) as i:
                for s in range(2):
                    copy_rows(2 * i + s + 1, 1 - s)
                    kv_tile(2 * i + s, s)
            kv_tile(T - 1, 0)

            act.wait_ge(*dve3.done(0, "aggr1"))
            a(cstd[:], cmv[:, :, 1], ACT.Sqrt, scale=float(N) / (N - 1)).then_inc(*act3("sqrt"))
            act.wait_ge(*pe3.done(0, "params"))
            a(colp[:], pR[:, 0:PR], ACT.Copy).then_inc(ccopy, 1)

            def rstd_ln(t, p, D, A):
                act.wait_ge(*D.done(t, p + "ve"))
                a(lnln[p][:], lnve[p][:], ACT.Ln).then_inc(*A(p + "ln"))
                act.wait_ge(*A.done(t, p + "ln"))
                a(lny[p][:], lnln[p][:], ACT.Exp, scale=-0.5).then_inc(*A(p + "exp"))

            nc.scalar.preload_act_table_set("natural_log_exp_and_others")
            act.wait_ge(*dveb.done(0, "toti"))
            groups = act.alloc_register("act_groups")
            act.reg_mov(groups, 0)

            def copyT(t, out_, name):
                act.wait_ge(*PM.done(t, name))
                a(out_, pT[:, 0:F].rearrange("p (c q) -> p c q", c=FC), ACT.Copy).then_inc(*AM(name))

            def step_xT(t):
                act.wait_ge(*PM.done(t - 1, "hid1"))
                copyT(t, xnT[:, 0], "xT")

            def step_qexp(t):
                act.wait_ge(*DM.done(t, "qmin"))
                a(qexp[:], qmin[:], ACT.Exp).then_inc(*AM("qexp"))

            def step_mT(t):
                act.wait_ge(*PM.done(t, "mT"))
                for c in range(FC):
                    a(mT[:, c, :], pT[:, c * P:(c + 1) * P], ACT.Identity, scale=colp[:, R_G1 + c:R_G1 + c + 1],
                      bias=colp[:, R_BB1 + c:R_BB1 + c + 1]).then_inc(*AM(f"mT{c}"))

            def step_relu(t):
                act.wait_ge(*PM.done(t, "hid1"))
                act.wait_ge(*PH.done(t - 1, "h2"))
                a(hT[:], pH[:].rearrange("p (c q) -> p c q", c=HC), ACT.Relu).then_inc(*AH("relu"))

            def coefs(g, half):
                ks = HALVES[half]
                act.wait_ge(coef_done, g * 2 + half + 3)
                act.wait_ge(msg_done, g * NPAIR + 2 * half + 2)
                a(coef[:, ks[0]:ks[-1] + 1, :], pC[half][:, 0:len(ks) * P].rearrange("p (k q) -> p k q", q=P),
                  ACT.Copy).then_inc(coef_copied, 1)

            def messages(begun, half):
                if half == 0:
                    act.wait_ge(idx_float, begun * 2 + 1)
                    act.wait_ge(idx_ready, begun * NPAIR + 1 - NPAIR)
                    a(idx_now[:], idxf[:], ACT.Copy).then_inc(idx_taken, 1)
                    act.wait_ge(idx_taken, begun + 1)
                for j in (2 * half, 2 * half + 1):
                    k0, k1 = PAIRS[j][0], PAIRS[j][-1] + 1
                    act.wait_ge(landed, begun * U + k1)
                    a(idx[:, k0:k1], idx_now[:, k0:k1], ACT.Copy).then_inc(idx_ready, 1)
                    act.wait_ge(msg_done, begun * NPAIR + j + 1)
                    a(msgs[:, k0:k1, :], pX[j % 2][:, 0:(k1 - k0) * F].rearrange("p (k f) -> p k f", f=F),
                      ACT.Copy).then_inc(msg_copied, 1)

            before_coefs = {0: step_xT, 1: step_qexp, 2: lambda t: copyT(t, msgT[:], "msgT"),
                            3: lambda t: rstd_ln(t, "m", DM, AM)}
            before_msgs = {3: step_mT}
            prev = act.alloc_register("act_prev_tile")
            act.reg_mov(prev, 0)
            with act.Fori(0, T) as t:
                g0 = act.snap(groups)
                for i in range(NG):
                    if i == 0:
                        with act.If(t > 0):
                            step_relu(act.snap(prev, min_val=0, max_val=T - 1))
                    if i in before_coefs:
                        before_coefs[i](t)
                    coefs(g0 + i, 0)
                    if i == 1:
                        with act.If(t > 0):
                            rstd_ln(act.snap(prev, min_val=0, max_val=T - 1), "h", DH, AH)
                    if i:
                        messages(g0 + i, 1)
                    else:
                        with act.If(t > 0):
                            messages(g0, 1)
                    coefs(g0 + i, 1)
                    if i in before_msgs:
                        before_msgs[i](t)
                    messages(g0 + (i + 1), 0)
                n = act.value_load(bnd[0:1, 1, bass.ds(t, 1)], min_val=NG, max_val=-(-CH // U))
                with act.If(n > NG):
                    with act.Fori(NG, n) as i:
                        coefs(g0 + i, 0)
                        messages(g0 + i, 1)
                        coefs(g0 + i, 1)
                        messages(g0 + i + 1, 0)
                act.reg_add(groups, groups, n)
                act.reg_mov(prev, t)
            step_relu(T - 1)
            messages(act.snap(groups), 1)
            rstd_ln(T - 1, "h", DH, AH)

            def gnn(t, s):
                act.wait_ge(*PG.done(t, "aggT"))
                act.wait_ge(*PG2.done(t - 2, "gnn"))
                a(aggT[:, s], (pT, pQ)[s][:, 0:F].rearrange("p (c q) -> p c q", c=FC), ACT.Copy).then_inc(*AG("aggT"))

            with act.Fori(0, T // 2) as i:
                for s in range(2):
                    gnn(2 * i + s, s)
            gnn(T - 1, 0)
            all_rstd(dveo, acto)

            def route_T(t, s):
                act.wait_ge(*PRT.done(t, "xT"))
                act.wait_ge(*PR_.done(t - 2, "log"))
                a(aggT[:, s], (pT, pQ)[s][:, 0:F].rearrange("p (c q) -> p c q", c=FC), ACT.Copy).then_inc(*ART("xT"))

            def route(t, s):
                act.wait_ge(*PR_.done(t, "log"))
                lo_ = tile(logits, t)
                a(lo_ if isinstance(t, int) else lo_.rearrange("p a e -> p (a e)"), (pM, pH)[s][:, 0:NE],
                  ACT.Copy).then_inc(*AR("log"))

            route_T(0, 0)
            with act.Fori(0, T // 2) as i:
                for s in range(2):
                    route_T(2 * i + s + 1, 1 - s)
                    route(2 * i + s, s)
            route(T - 1, 0)
            all_rstd(dvei, acti)
            act.wait_ge(*dver.done(0, "dif"))
            a(best[:, 0, :], best[:, 1, :], ACT.Exp).then_inc(*actr("exp"))

            act.wait_ge(*dve5.done(0, "inb"))
            nc.scalar.preload_act_table(ACT.Gelu)
            nb = act.value_load(ztab[0:1, NE:NE + 1], min_val=1, max_val=MAXBLK)
            with act.Fori(0, nb) as b:
                e = act.value_load(btab[0:1, 1, bass.ds(b, 1)], min_val=0, max_val=NE - 1)
                for j in range(EHC):
                    act.wait_ge(*PE_.done(b, f"h{j}"))
                    act.wait_ge(*PE_.done(b - 1, "y1"))
                    a(ehT[:, j, :], (pA, pQ, pM, pH)[j % 4][:, 0:BLK], ACT.Gelu,
                      bias=colp[:, bass.ds(e * EHC + R_B1 + j, 1)]).then_inc(*AE(f"g{j}"))
                act.wait_ge(*DE.done(b, "y1"))
                act.dma_start(eouts[bass.ds(b * BLK, BLK), :].rearrange("(m p) f -> p m f", p=P), yb[:]).then_inc(out_rows, 16)

        @block.vector
        def _(dve):
            v = nc.vector
            kept = [0]
            for st in (dve1, dve2, DN, DS, DK, dve3, DM, DXS, DH, dve5, DX, DE, DI, DC, dveb, dve6, DA, DG, DR, dveo, dvei, dver, DD):
                st.first(dve)
            for st in (counted, same_made, reads_made, idx_float, floats_made, out_rows, *stored):
                dve.sem_inc(st, 1)
            dve.wait_ge(consts_made, 1)
            for k in range(nxc):
                dve.wait_ge(x_loaded[k], 16)
                with dve.Fori(k * XCH // 4, (k + 1) * XCH // 4) as i:
                    for j in range(4):
                        v.bn_stats(tile(bst, 4 * i + j), tile(x1, 4 * i + j)).then_inc(*dve1("stats"))
            dve.wait_ge(x_loaded[nxc], 16)
            v.bn_stats(bst[:, T - 1, :], x1[:, T - 1, :]).then_inc(*dve1("stats"))
            dve.wait_ge(*dve1.done(T - 1, "stats"))
            own = lambda st, name: dve.wait_ge(*st.done(0, name))

            def all_rstd(D, AC):
                me, mo, ve, vo = bst[:, :, 1], bst[:, :, 4], bst[:, :, 2], bst[:, :, 5]
                v.tensor_tensor(rmean[:], me, mo, ALU.add).then_inc(*D("msum"))
                own(D, "msum")
                v.tensor_scalar(rmean[:], rmean[:], 0.5, None, ALU.mult).then_inc(*D("mean"))
                v.tensor_tensor(rtmp[:], me, mo, ALU.subtract).then_inc(*D("dif"))
                v.tensor_tensor(rvar[:], ve, vo, ALU.add).then_inc(*D("m2"))
                own(D, "m2")
                v.tensor_tensor(rtmp[:], rtmp[:], rtmp[:], ALU.mult).then_inc(*D("dif2"))
                v.tensor_scalar(rvar[:], rvar[:], 1.0 / F, None, ALU.mult).then_inc(*D("dif4"))
                own(D, "dif4")
                v.scalar_tensor_tensor(rvar[:], rtmp[:], 0.25, rvar[:], ALU.mult, ALU.add).then_inc(*D("var"))
                own(D, "var")
                v.tensor_scalar(rvar[:], rvar[:], EPS, None, ALU.add).then_inc(*D("ve"))
                dve.wait_ge(*AC.done(0, "exp"))
                v.tensor_tensor(rrstd[:], rtmp[:], rtmp[:], ALU.mult).then_inc(*D("a"))
                own(D, "a")
                v.tensor_tensor(rvar[:], rrstd[:], rvar[:], ALU.mult).then_inc(*D("nr"))
                own(D, "nr")
                v.tensor_scalar(rvar[:], rvar[:], -0.5, 1.5, ALU.mult, ALU.add).then_inc(*D("y"))
                own(D, "y")
                v.tensor_tensor(rrstd[:], rtmp[:], rvar[:], ALU.mult).then_inc(*D("rstd"))
                own(D, "rstd")

            all_rstd(dve2, act2)
            rs_done = sem("ones_column")
            v.memset(vaug[:, :, :, P:P + 1], 1.0).then_inc(rs_done, 1)
            dve.wait_ge(rs_done, 1)

            def norm_rows(t, s):
                dve.wait_ge(*PT.done(t - 2, "trans"))
                dve.wait_ge(*GK.done(t - 2, "res"))
                x1t = tile(x1, t) if isinstance(t, int) else tile(x1, t).rearrange("p a f -> p (a f)")
                v.tensor_scalar(xs[:, s, :], x1t, col(rmean, t), col(rrstd, t),
                                ALU.subtract, ALU.mult).then_inc(*DN("norm"))

            def col_stats(t, s, rows=P):
                dve.wait_ge(*PT.done(t, "trans"))
                dve.wait_ge(*AX.done(t, "xnT"))
                apart(dve)
                for c in range(FC):
                    v.bn_stats(cst[:, c, t, :] if isinstance(t, int) else cst[:, c, bass.ds(t, 1), :],
                               (pT, pA)[s][:, c * P:c * P + rows]).then_inc(*DS(f"cstat{c}"))

            def k_min(t, s):
                dve.wait_ge(*PK.done(t, "kv"))
                dve.wait_ge(*AK.done(t - 2, "kexp"))
                v.tensor_scalar(kmin[:, s, :], (pQ, pM)[s][:, 0:F], 0.0, None, ALU.min).then_inc(*DK("kmin"))

            def k_elu(t, s):
                dve.wait_ge(*AK.done(t, "kexp"))
                dve.wait_ge(*AK.done(t, "vcopy"))
                dve.wait_ge(*PKA.done(t - 2, "kvacc"))
                v.scalar_tensor_tensor(kelu[:, s, :], (pQ, pM)[s][:, 0:F], 0.0, kexp[:, s, :],
                                       ALU.max, ALU.add).then_inc(*DK("kelu"))

            def kv_tile(t, s):
                k_min(t, s)
                col_stats(t + 1, 1 - s)
                norm_rows(t + 2, s)
                k_elu(t, s)

            norm_rows(0, 0)
            norm_rows(1, 1)
            col_stats(0, 0)
            with dve.Fori(0, (T - 3) // 2) as i:
                for s in range(2):
                    kv_tile(2 * i + s, s)
            kv_tile(T - 3, 0)
            k_min(T - 2, 1)
            col_stats(T - 1, 0, TAIL)
            k_elu(T - 2, 1)
            dve.wait_ge(*PKA.done(T - 3, "kvacc"))
            vt = sem("vaug_tail")
            for c in range(FC):
                v.tensor_copy(vaug[:, 0, c, P:P + 1], valid[:, T - 1:T]).then_inc(vt, 1)
            dve.wait_ge(vt, 2)
            k_min(T - 1, 0)
            k_elu(T - 1, 0)

            for c in range(FC):
                dve.wait_ge(*DS.done(T - 1, "cstat1"))
                v.bn_aggr(cmv[:, c, :], cst[:, c].rearrange("p t s -> p (t s)")).then_inc(*dve3(f"aggr{c}"))
            dve.wait_ge(*act3.done(0, "sqrt"))
            dve.wait_ge(weights, 16 * 15)
            v.tensor_scalar(cstd[:], cstd[:], STD_EPS, None, ALU.add).then_inc(*dve3("std"))
            own(dve3, "std")
            v.reciprocal(cstd[:], cstd[:]).then_inc(*dve3("inv"))
            own(dve3, "inv")
            for c in range(FC):
                v.tensor_scalar(wgs[:, c, :], wg[:, c, :], cstd[:, c:c + 1], None, ALU.mult).then_inc(*dve3(f"wgs{c}"))
            for c in range(FC):
                v.tensor_scalar(dmean[:, c, :], ident[:], cmv[:, c, 0:1], None, ALU.mult).then_inc(*dve3(f"dm{c}"))
            dve.wait_ge(*pe3.done(0, "mean"))
            v.tensor_copy(mean_bc[:], pY[:, 0:F]).then_inc(*dve3("meanbc"))
            own(dve3, "meanbc")
            dve.wait_ge(*GK.done(T - 1, "res"))
            TG = 7
            for k in range(T // TG):
                xk = xn[:, k * TG:(k + 1) * TG, :]
                v.tensor_tensor(xk, xk, mean_bc[:].unsqueeze(1).to_broadcast([P, TG, F]), ALU.subtract).then_inc(cen_made, 1)
            dve.wait_ge(cen_made, T // TG)
            for c in range(FC):
                acc = (pG, pH)[c]
                v.tensor_tensor(kvbd[:, c, 0:P], acc[:, 0:P], bdmask[:].rearrange("p a b -> p (a b)"), ALU.mult).then_inc(*dve3(f"kv{c}"))
            for c in range(FC):
                acc = (pG, pH)[c]
                v.tensor_scalar(kvbd[:, c, P:P + HPC], hmask[:], acc[:, P:P + 1], None, ALU.mult).then_inc(*dve3(f"ks{c}"))
            v.tensor_tensor(bias_bc[:], bias_bc[:], gb_bc[:], ALU.add).then_inc(*dve3("gb"))

            dve.wait_ge(chunks_loaded, 32)
            v.tensor_reduce(cmax[:], dstc[:], AX_X, ALU.max).then_inc(*dveb("cmax"))
            v.tensor_reduce(cmin[:], dstc[:], AX_X, ALU.min).then_inc(*dveb("cmin"))
            own(dveb, "cmin")
            bt = lambda z: z[:].unsqueeze(2).to_broadcast([P, T, CB])
            bc = lambda z: z[:].unsqueeze(1).to_broadcast([P, T, CB])
            v.tensor_tensor(indA[:], bc(cmin), bt(thi), ALU.is_le).then_inc(*dveb("indA"))
            v.tensor_tensor(indB[:], bc(cmax), bt(tlo), ALU.is_ge).then_inc(*dveb("indB"))
            own(dveb, "indB")
            v.tensor_tensor(indA[:], indA[:], indB[:], ALU.mult).then_inc(*dveb("ind"))
            own(dveb, "ind")
            v.tensor_tensor(indB[:], indA[:], bc(cidx), ALU.mult).then_inc(*dveb("vhi"))
            own(dveb, "vhi")
            v.tensor_reduce(vmax[:, 0:T], indB[:], AX_X, ALU.max).then_inc(*dveb("vmaxhi"))
            v.tensor_tensor(indA[:], indA[:], bc(cinv), ALU.mult).then_inc(*dveb("vlo"))
            own(dveb, "vlo")
            v.tensor_reduce(vmax[:, T:2 * T], indA[:], AX_X, ALU.max).then_inc(*dveb("vmaxlo"))
            dve.wait_ge(*peb.done(0, "t1"))
            v.tensor_reduce(vred[:], pA[0:2 * T, 0:P], AX_X, ALU.max).then_inc(*dveb("vred"))
            dve.wait_ge(*peb.done(0, "t2"))
            v.tensor_copy(brow[:], pA[0:1, 256:256 + 2 * T]).then_inc(*dveb("row"))
            own(dveb, "row")
            hi, lo = brow[:, 0:T], brow[:, T:2 * T]
            v.tensor_scalar(hi, hi, float(CH), 1.0, ALU.min, ALU.max).then_inc(*dveb("hi1"))
            v.tensor_scalar(lo, lo, -1.0, float(BIG), ALU.mult, ALU.add).then_inc(*dveb("lo1"))
            own(dveb, "lo1")
            v.tensor_scalar(bndf[:, 1, :], hi, -1.0, None, ALU.add).then_inc(*dveb("hi2"))
            own(dveb, "hi2")
            v.tensor_tensor(lo, lo, bndf[:, 1, :], ALU.min).then_inc(*dveb("lo2"))
            own(dveb, "lo2")
            v.tensor_tensor(hi, hi, lo, ALU.subtract).then_inc(*dveb("n1"))
            own(dveb, "n1")
            RECIP, SHIFT = -(-(1 << 16) // U), 16
            assert (CH + U) * RECIP < 1 << 24
            v.tensor_scalar(bndf[:, 1, :], hi, float(U - 1), None, ALU.add).then_inc(*dveb("n2"))
            own(dveb, "n2")
            v.tensor_scalar(bndf[:, 1, :], bndf[:, 1, :], float(RECIP), None, ALU.mult).then_inc(*dveb("mul"))
            v.tensor_scalar(bndf[:, 0, :], lo, float(CH - (NG - 1) * U), float(P), ALU.min, ALU.mult).then_inc(*dveb("elo"))
            own(dveb, "elo")
            v.tensor_copy(bnd[:, 0, :], bndf[:, 0, :]).then_inc(*dveb("ielo"))
            v.tensor_copy(bnd[:, 1, :], bndf[:, 1, :]).then_inc(*dveb("in"))
            own(dveb, "in")
            v.tensor_single_scalar(bnd[:, 1, :], bnd[:, 1, :], SHIFT, ALU.logical_shift_right).then_inc(*dveb("shr"))
            own(dveb, "shr")
            v.tensor_scalar(bnd[:, 1, :], bnd[:, 1, :], float(NG), None, ALU.max).then_inc(*dveb("min"))
            own(dveb, "min")
            v.tensor_copy(bndf[:, 1, :], bnd[:, 1, :]).then_inc(*dveb("totf"))
            own(dveb, "totf")
            v.tensor_reduce(brow[:, 0:1], bndf[:, 1, :], AX_X, ALU.add).then_inc(*dveb("tot"))
            own(dveb, "tot")
            v.tensor_copy(total_i[:], brow[:, 0:1]).then_inc(*dveb("toti"))
            dve.wait_ge(ccopy, 1)
            own(dve3, "gb")

            flat = lambda b, t: tile(b, t) if isinstance(t, int) else tile(b, t).rearrange("p a f -> p (a f)")
            groups = dve.alloc_register("dve_groups")
            dve.reg_mov(groups, 0)

            def me_(t, name):
                dve.wait_ge(*DM.done(t, name))

            def norm_stats(t, p, D, src_ap):
                apart(dve)
                v.bn_stats(lnst[p][:], src_ap).then_inc(*D(p + "st"))
                dve.wait_ge(*D.done(t, p + "st"))
                apart(dve)
                v.bn_aggr(lnmv[p][:], lnst[p][:]).then_inc(*D(p + "ag"))
                dve.wait_ge(*D.done(t, p + "ag"))
                v.tensor_scalar(lnve[p][:], lnmv[p][:, 1:2], EPS, None, ALU.add).then_inc(*D(p + "ve"))

            def norm_apply(t, p, D, A, src_ap, dst_ap):
                own_ = lambda name: dve.wait_ge(*D.done(t, p + name))
                dve.wait_ge(*A.done(t, p + "exp"))
                v.scalar_tensor_tensor(lna[p][:], lny[p][:], lnve[p][:], lny[p][:], ALU.mult, ALU.mult).then_inc(*D(p + "a"))
                own_("a")
                v.tensor_scalar(lna[p][:], lna[p][:], -0.5, 1.5, ALU.mult, ALU.add).then_inc(*D(p + "nr"))
                own_("nr")
                v.tensor_tensor(lnr[p][:], lna[p][:], lny[p][:], ALU.mult).then_inc(*D(p + "r"))
                own_("r")
                v.tensor_scalar(dst_ap, src_ap, lnmv[p][:, 0:1], lnr[p][:], ALU.subtract, ALU.mult).then_inc(*D(p + "ap"))

            def step_start(t):
                dve.wait_ge(reads_made, dve.snap(groups) * U + 1)
                v.tensor_scalar(idrow[:], idrow[:], float(P), None, ALU.add).then_inc(*DM("idrow"))
                me_(t, "idrow")

            def step_xs(t):
                dve.wait_ge(*PM.done(t - 1, "xT"))
                v.tensor_tensor(xs[:, 0, :], flat(xn, t), mean_bc[:], ALU.add).then_inc(*DXS("xs"))

            q3 = pQ[:, 0:F].rearrange("p (c q) -> p c q", c=FC)

            def step_qmin(t):
                dve.wait_ge(*PM.done(t, "q"))
                v.tensor_scalar(qmin[:], q3, 0.0, None, ALU.min).then_inc(*DM("qmin"))

            def step_qelu(t):
                dve.wait_ge(*AM.done(t, "qexp"))
                v.scalar_tensor_tensor(qelu[:], q3, 0.0, qexp[:], ALU.max, ALU.add).then_inc(*DM("qelu"))

            def step_msg(t):
                dve.wait_ge(*PM.done(t, "num"))
                pm3 = pM[:, 0:FC * (P + HPC)].rearrange("p (c w) -> p c w", c=FC)
                v.tensor_scalar(rden[:], pm3[:, :, P:P + HPC], ATT_EPS, None, ALU.add).then_inc(*DM("eps"))
                me_(t, "eps")
                v.reciprocal(rden[:], rden[:]).then_inc(*DM("rden"))
                me_(t, "rden")
                v.tensor_tensor(msg[:].rearrange("p (c h d) -> p c h d", c=FC, h=HPC),
                                pm3[:, :, 0:P].rearrange("p c (h d) -> p c h d", h=HPC),
                                rden[:].unsqueeze(3).to_broadcast([P, FC, HPC, HD]), ALU.mult).then_inc(*DM("msg"))

            def step_mstats(t):
                dve.wait_ge(*PM.done(t, "mm"))
                norm_stats(t, "m", DM, pQ[:, 0:F])

            def step_mnorm(t):
                norm_apply(t, "m", DM, AM, pQ[:, 0:F], mrow[:])

            def step_hstats(t):
                dve.wait_ge(*PH.done(t, "h2"))
                norm_stats(t, "h", DH, pH[:, 0:F])

            def step_hnorm(t):
                norm_apply(t, "h", DH, AH, pH[:, 0:F], hrow[:])
                dve.wait_ge(*DH.done(t, "hap"))
                v.tensor_tensor(hrow[:], hrow[:], g2_bc[:], ALU.mult).then_inc(*DH("g2"))
                dve.wait_ge(*DH.done(t, "g2"))
                v.tensor_tensor(hrow[:], hrow[:], bias_bc[:], ALU.add).then_inc(*DH("b2"))
                dve.wait_ge(*DH.done(t, "b2"))
                v.tensor_tensor(flat(x1, t), flat(x1, t), hrow[:], ALU.add).then_inc(*DH("res"))

            rows_of = src_row[:].rearrange("p (e k) -> p k e", k=U)

            def onehots(g):
                dve.wait_ge(ends_loaded, g * 48 + 48)
                dve.wait_ge(idx_float, g * 2 + 1)
                v.tensor_copy(srcf[:], src_e[:]).then_inc(floats_made, 1)
                v.tensor_copy(dstf[:], dst_e[:]).then_inc(floats_made, 1)
                dve.wait_ge(row_loaded, g * 16 + 16)
                dve.wait_ge(floats_made, g * 2 + 3)
                for half in range(2):
                    dve.wait_ge(coef_done, g * 2 + half + 1)
                    for k in HALVES[half]:
                        v.tensor_scalar(same[:, k, :], rows_of[:, k, :], srcf[:, k:k + 1], None,
                                        ALU.is_equal).then_inc(same_made, 1)
                for k in range(U):
                    v.tensor_scalar(reads[:, k, :], idrow[:], dstf[:, k:k + 1], w_e[:, k:k + 1],
                                    ALU.is_equal, ALU.mult).then_inc(reads_made, 1)

            def indices(g):
                dve.wait_ge(counted, g * (U + 1) + 1)
                v.tensor_tensor(away[:], dummy[:], srcf[:], ALU.subtract).then_inc(counted, 1)
                dve.wait_ge(same_made, g * U + U + 1)
                for k in range(U):
                    v.scalar_tensor_tensor(junk[:, k, :], same[:, k, :], 1.0, trilow[:], ALU.mult, ALU.mult,
                                           accum_out=before[:, k:k + 1]).then_inc(counted, 1)
                dve.wait_ge(counted, g * (U + 1) + U + 2)
                dve.wait_ge(idx_taken, g + 1)
                v.scalar_tensor_tensor(away[:], before[:], 0.0, away[:], ALU.is_gt, ALU.mult).then_inc(idx_float, 1)
                dve.wait_ge(idx_float, g * 2 + 2)
                v.tensor_tensor(idxf[:], away[:], srcf[:], ALU.add).then_inc(idx_float, 1)

            after_onehots = {1: step_qelu, 3: step_mnorm}
            after_indices = {0: step_qmin, 1: step_msg, 2: step_mstats}
            step_xs(0)
            following = dve.alloc_register("dve_following_tile")
            prev = dve.alloc_register("dve_prev_tile")
            dve.reg_mov(prev, 0)
            with dve.Fori(0, T) as t:
                step_start(t)
                g0 = dve.snap(groups)
                for i in range(NG):
                    onehots(g0 + i)
                    if i == 2:
                        with dve.If(t > 0):
                            step_hnorm(dve.snap(prev, min_val=0, max_val=T - 1))
                    if i in after_onehots:
                        after_onehots[i](t)
                    indices(g0 + i)
                    if i == 0:
                        with dve.If(t > 0):
                            step_hstats(dve.snap(prev, min_val=0, max_val=T - 1))
                    if i in after_indices:
                        after_indices[i](t)
                    if i == 3:
                        with dve.If(t < T - 1):
                            dve.reg_mov(following, t)
                            dve.reg_add(following, following, 1)
                            step_xs(dve.snap(following, min_val=1, max_val=T - 1))
                n = dve.value_load(bnd[0:1, 1, bass.ds(t, 1)], min_val=NG, max_val=-(-CH // U))
                with dve.If(n > NG):
                    with dve.Fori(NG, n) as i:
                        onehots(g0 + i)
                        indices(g0 + i)
                dve.reg_add(groups, groups, n)
                dve.reg_mov(prev, t)
            step_hstats(T - 1)
            step_hnorm(T - 1)

            def add_parts(t, s, turn):
                dve.wait_ge(parts_loaded[s // 2], 16 * NACC * (turn + 1))
                dve.wait_ge(*GG.done(t, "add"))
                v.tensor_tensor(parts[:, s, 0:KEPT, :], parts[:, s, 0:KEPT, :], parts[:, s, KEPT:2 * KEPT, :], ALU.add).then_inc(*DA("add"))

            def gnn(t):
                dve.wait_ge(*PG2.done(t, "gnn"))
                v.tensor_tensor(flat(x1, t), flat(x1, t), (pM, pH)[gnn_turn[0] % 2][:, 0:F], ALU.add).then_inc(*DG("res"))
                gnn_turn[0] += 1
                dve.wait_ge(*DG.done(t, "res"))
                apart(dve)
                v.bn_stats(flat(bst, t), flat(x1, t)).then_inc(*DG("stats"))

            gnn_turn = [0]
            add_parts(0, 0, 0)
            add_parts(1, 1, 0)
            with dve.Fori(0, T // SLOTS - 1) as i:
                for s in range(SLOTS):
                    add_parts(SLOTS * i + s + 2, (s + 2) % SLOTS, i + (s + 2) // SLOTS)
                    gnn(SLOTS * i + s)
            i = T // SLOTS - 1
            for s in range(SLOTS + 1):
                if s + 2 <= SLOTS:
                    add_parts(SLOTS * i + s + 2, (s + 2) % SLOTS, i + (s + 2) // SLOTS)
                gnn(SLOTS * i + s)
            dve.wait_ge(*DG.done(T - 1, "stats"))
            all_rstd(dveo, acto)

            def outer(t, s):
                dve.wait_ge(*PRT.done(t - 2, "xT"))
                dve.wait_ge(*GR.done(t - 2, "keep"))
                v.tensor_scalar(xs[:, s, :], flat(x1, t), col(rmean, t), col(rrstd, t),
                                ALU.subtract, ALU.mult).then_inc(*DR("xt"))
                dve.wait_ge(*DR.done(t, "xt"))
                apart(dve)
                v.bn_stats(flat(bst, t), xs[:, s, :]).then_inc(*DR("stats"))

            with dve.Fori(0, T // 2) as i:
                for s in range(2):
                    outer(2 * i + s, s)
            outer(T - 1, 0)
            dve.wait_ge(*DR.done(T - 1, "stats"))
            all_rstd(dvei, acti)

            D = dver
            te = [P, T, NE]
            over_e = lambda z: z.unsqueeze(2).to_broadcast(te)
            dve.wait_ge(*AR.done(T - 1, "log"))
            v.tensor_tensor(logits[:], logits[:], br_bc[:].unsqueeze(1).to_broadcast(te), ALU.add).then_inc(*D("br"))
            own(D, "br")
            for j in range(2):
                v.tensor_reduce(best[:, j, :], logits[:], AX_X, ALU.max).then_inc(*D(f"b{j}"))
                own(D, f"b{j}")
                v.tensor_tensor(hot[:, j], logits[:], over_e(best[:, j, :]), ALU.is_equal).then_inc(*D(f"e{j}"))
                own(D, f"e{j}")
                v.tensor_tensor(work[:, 0], hot[:, j], down8[:].unsqueeze(1).to_broadcast(te), ALU.mult).then_inc(*D(f"r{j}"))
                own(D, f"r{j}")
                v.tensor_reduce(which[:], work[:, 0], AX_X, ALU.max).then_inc(*D(f"w{j}"))
                own(D, f"w{j}")
                v.tensor_tensor(hot[:, j], work[:, 0], over_e(which[:]), ALU.is_equal).then_inc(*D(f"h{j}"))
                own(D, f"h{j}")
                if j == 0:
                    v.tensor_scalar(work[:, 1], hot[:, 0], -3e38, None, ALU.mult).then_inc(*D("p0"))
                    own(D, "p0")
                    v.tensor_tensor(logits[:], logits[:], work[:, 1], ALU.add).then_inc(*D("l1"))
                    own(D, "l1")
            v.tensor_tensor(best[:, 1, :], best[:, 1, :], best[:, 0, :], ALU.subtract).then_inc(*D("dif"))
            dve.wait_ge(*actr.done(0, "exp"))
            v.tensor_scalar(best[:, 1, :], best[:, 0, :], 1.0, None, ALU.add).then_inc(*D("den"))
            own(D, "den")
            v.reciprocal(wts[:, :, 0], best[:, 1, :]).then_inc(*D("wa"))
            own(D, "wa")
            v.tensor_tensor(wts[:, :, 1], wts[:, :, 0], best[:, 0, :], ALU.mult).then_inc(*D("wb"))
            for j in range(2):
                v.tensor_tensor(hot[:, j], hot[:, j], over_e(valid[:]), ALU.mult).then_inc(*D(f"v{j}"))
            own(D, "v1")
            v.tensor_tensor(hots[:], hot[:, 0], hot[:, 1], ALU.add).then_inc(*D("sum"))
            dve.wait_ge(*per.done(0, "tot"))
            v.tensor_copy(work[:, 0].rearrange("p t e -> p (t e)"), pY[:, 0:TE]).then_inc(*D("tot"))
            own(D, "tot")
            cur, step = 0, 1
            while step < T:
                nxt = 1 - cur
                v.tensor_tensor(work[:, nxt, step:T, :], work[:, cur, step:T, :], work[:, cur, 0:T - step, :], ALU.add).then_inc(*D(f"s{step}"))
                v.tensor_copy(work[:, nxt, 0:step, :], work[:, cur, 0:step, :]).then_inc(prefix_kept, 1)
                own(D, f"s{step}")
                kept[0] += 1
                dve.wait_ge(prefix_kept, kept[0])
                cur, step = nxt, 2 * step
            run = work[:, cur]
            v.tensor_copy(lastcnt[:], run[:, T - 1, :]).then_inc(prefix_kept, 1)
            kept[0] += 1
            dve.wait_ge(prefix_kept, kept[0])
            fl = lambda z: z.rearrange("p t e -> p (t e)")
            v.tensor_tensor(fl(run), fl(run), pY[:, 0:TE], ALU.subtract).then_inc(*D("sub"))
            own(D, "sub")
            v.tensor_tensor(fl(run), fl(run), pA[:, 0:TE], ALU.add).then_inc(*D("rank"))
            own(D, "rank")
            v.tensor_tensor(run, run, ebase[:].unsqueeze(1).to_broadcast(te), ALU.add).then_inc(*D("base"))
            own(D, "base")
            for j in range(2):
                v.tensor_tensor(work[:, 1 - cur], hot[:, j], run, ALU.mult).then_inc(*D(f"p{j}x"))
                own(D, f"p{j}x")
                v.tensor_reduce(slotf[:, :, j], work[:, 1 - cur], AX_X, ALU.add).then_inc(*D(f"s{j}x"))
                own(D, f"s{j}x")
            v.tensor_tensor(carry[:], lastcnt[:], ebase[:], ALU.add).then_inc(*D("last"))

            def hand(t, s, turn):
                if turn is not None:
                    dve.wait_ge(dispatched[s], turn * 32)
                v.tensor_scalar(xn2[:, s, :], flat(xn, t), col(rmean, t), col(rrstd, t),
                                ALU.subtract, ALU.mult).then_inc(*DD("xn2"))
                v.tensor_copy(slot_now[:, s, :], flat(slotf, t)).then_inc(*DD("slot"))

            dve.wait_ge(*GR.done(T - 1, "keep"))
            hand(0, 0, None)
            hand(1, 1, None)
            with dve.Fori(1, T // 2) as i:
                for s in range(2):
                    hand(2 * i + s, s, i)
            hand(T - 1, 0, T // 2)

            own(dver, "last")
            dve.wait_ge(*DD.done(T - 1, "slot"))
            v.tensor_tensor(cnt[:], carry[:], ebase[:], ALU.subtract).then_inc(*dve5("cnt"))
            own(dve5, "cnt")
            v.tensor_scalar(cnt[:], cnt[:], float(BLK - 1), None, ALU.add).then_inc(*dve5("c255"))
            own(dve5, "c255")
            v.tensor_copy(cnti[:], cnt[:]).then_inc(*dve5("ci"))
            own(dve5, "ci")
            v.tensor_single_scalar(cnti[:], cnti[:], 8, ALU.logical_shift_right).then_inc(*dve5("sh"))
            own(dve5, "sh")
            v.tensor_copy(nblk[:], cnti[:]).then_inc(*dve5("nb"))
            own(dve5, "nb")
            v.tensor_tensor_scan(cum[:], one8[:], nblk[:], 0.0, ALU.mult, ALU.add).then_inc(*dve5("cum"))
            own(dve5, "cum")
            bb = bidx[:].unsqueeze(2).to_broadcast([1, MAXBLK + 1, NE])
            v.tensor_tensor(le[:], cum[0:1].unsqueeze(1).to_broadcast([1, MAXBLK + 1, NE]), bb, ALU.is_le).then_inc(*dve5("le"))
            own(dve5, "le")
            v.tensor_tensor(lenb[:], le[:], nblk[0:1].unsqueeze(1).to_broadcast([1, MAXBLK + 1, NE]), ALU.mult).then_inc(*dve5("lenb"))
            own(dve5, "lenb")
            v.tensor_reduce(be[:], le[:], AX_X, ALU.add).then_inc(*dve5("be"))
            v.tensor_reduce(bprev[:], lenb[:], AX_X, ALU.add).then_inc(*dve5("bprev"))
            own(dve5, "bprev")
            v.tensor_tensor(bstart[:], bidx[:], bprev[:], ALU.subtract).then_inc(*dve5("st1"))
            own(dve5, "st1")
            v.tensor_scalar(bstart[:], bstart[:], float(BLK), None, ALU.mult).then_inc(*dve5("st2"))
            own(dve5, "st2")
            v.tensor_scalar(be[:], be[:], float(NE - 1), None, ALU.min).then_inc(*dve5("bemax"))
            own(dve5, "bemax")
            v.scalar_tensor_tensor(btab[:, 0, :], be[:], float(REG), bstart[:], ALU.mult, ALU.add).then_inc(*dve5("itab"))
            v.tensor_copy(btab[:, 1, :], be[:]).then_inc(*dve5("ibe"))
            v.tensor_copy(ztab[:, 0:NE], carry[0:1, :]).then_inc(*dve5("izt"))
            v.tensor_copy(ztab[:, NE:NE + 1], cum[0:1, NE - 1:NE]).then_inc(*dve5("inb"))
            own(dve5, "inb")
            nb = dve.value_load(ztab[0:1, NE:NE + 1], min_val=1, max_val=MAXBLK)

            def scale_rows(b):
                e = dve.value_load(btab[0:1, 1, bass.ds(b, 1)], min_val=0, max_val=NE - 1)
                dve.wait_ge(*PE_.done(b - 1, f"h{EHC - 1}"))
                for c in range(FC):
                    dve.wait_ge(*PT_.done(b, f"t{c}"))
                    v.tensor_scalar(xeT[:, c, :], (pT, pR)[c][:, 0:BLK], colp[:, bass.ds(e * FC + R_G + c, 1)],
                                    colp[:, bass.ds(e * FC + R_B + c, 1)], ALU.mult, ALU.add).then_inc(*DX(f"x{c}"))

            scale_rows(0)
            with dve.Fori(0, nb) as b:
                scale_rows(b + 1)
                dve.wait_ge(eb2_loaded, 16 * b + 16)
                dve.wait_ge(out_rows, 16 * b + 1)
                for m in range(BM):
                    dve.wait_ge(*PE_.done(b, f"y{m}"))
                    v.tensor_tensor(yb[:, m, :], (pY, pG)[m][:, 0:F], eb2_bc[:], ALU.add).then_inc(*DE(f"y{m}"))

            own(dve5, "inb")
            v.tensor_tensor(delta[:], cum[:], nblk[:], ALU.subtract).then_inc(*dve6("excl"))
            own(dve6, "excl")
            v.tensor_scalar(delta[:], delta[:], float(BLK), None, ALU.mult).then_inc(*dve6("rows"))
            own(dve6, "rows")
            v.tensor_tensor(delta[:], delta[:], ebase[:], ALU.subtract).then_inc(*dve6("delta"))
            own(dve6, "delta")
            for j in range(2):
                v.tensor_tensor(hot[:, j], hot[:, j], delta[:].unsqueeze(1).to_broadcast(te), ALU.mult).then_inc(*dve6(f"hot{j}"))
            own(dve6, "hot1")
            for j in range(2):
                v.tensor_reduce(slotc[:, :, j], hot[:, j], AX_X, ALU.add).then_inc(*dve6(("shift", "slot")[j]))
            own(dve6, "slot")
            v.tensor_tensor(slotf[:], slotf[:], slotc[:], ALU.add).then_inc(prefix_kept, 1)
            dve.wait_ge(prefix_kept, kept[0] + 1)

            def out_idx(t, s):
                v.tensor_copy(idx_c[:, s, :], flat(slotf, t)).then_inc(*DI("idx"))

            def combine(t, s, turn):
                rows = TAIL if isinstance(t, int) and t == T - 1 else P
                x1t, wt = flat(x1, t), flat(wts, t)
                dve.wait_ge(got[s][0], 16 * turn + 16)
                dve.wait_ge(stored[s], 16 * turn + 1)
                v.scalar_tensor_tensor(ob[0:rows, s, :], yg[0:rows, s, 0, :], wt[0:rows, 0:1], x1t[0:rows],
                                       ALU.mult, ALU.add).then_inc(*DC("a"))
                dve.wait_ge(*DC.done(t, "a"))
                dve.wait_ge(got[s][1], 16 * turn + 16)
                v.scalar_tensor_tensor(ob[0:rows, s, :], yg[0:rows, s, 1, :], wt[0:rows, 1:2], ob[0:rows, s, :],
                                       ALU.mult, ALU.add).then_inc(*DC("b"))
                dve.wait_ge(*DC.done(t, "b"))
                apart(dve)

            for s in range(SLOTS):
                out_idx(s, s)
            with dve.Fori(0, T // SLOTS - 1) as i:
                for s in range(SLOTS):
                    combine(SLOTS * i + s, s, i)
                    out_idx(SLOTS * (i + 1) + s, s)
            for t in range(T - 1 - SLOTS, T):
                combine(t, t % SLOTS, t // SLOTS)
                if t == T - 1 - SLOTS:
                    out_idx(T - 1, 0)


_INS = ['x', 'src', 'dst', 'edge_weight', 'L0_gnn_weight', 'L0_gnn_bias', 'L0_mix_Wq', 'L0_mix_Wk', 'L0_mix_Wv',
        'L0_mix_Wm', 'L0_mix_W1', 'L0_mix_W2', 'L0_mix_g1', 'L0_mix_b1', 'L0_mix_g2', 'L0_mix_b2', 'L0_ffn_Wr',
        'L0_ffn_br', 'L0_ffn_ln_g', 'L0_ffn_ln_b', 'L0_ffn_W1', 'L0_ffn_b1', 'L0_ffn_W2', 'L0_ffn_b2']


def kernel(**inputs):
    import numpy as _np
    import concourse.bacc as _bacc
    from concourse import mybir as _mybir
    from concourse.bass_utils import run_bass_kernel_spmd as _run

    nc = _bacc.Bacc("TRN2", target_bir_lowering=False, num_devices=1)
    arrays, args = {}, []
    for name in _INS:
        a = _np.ascontiguousarray(inputs[name])
        arrays[f"in_{name}_dram"] = a
        args.append(nc.dram_tensor(f"in_{name}_dram", a.shape, _mybir.dt.from_np(a.dtype), kind="ExternalInput").ap())
    out = nc.dram_tensor("out_0_dram", inputs["x"].shape, _mybir.dt.float32, kind="ExternalOutput").ap()
    gps_layer(nc, *args, out)
    r = _run(nc, [arrays], core_ids=[0])
    return r.results[0]["out_0_dram"]
```
